# Optimizing a Trainium2 kernel written in Bass

```python
import numpy as np
import jax
import jax.numpy as jnp

def _softmax(x, axis=-1):
    return jax.nn.softmax(x, axis=axis)

def _gelu(x):
    return jax.nn.gelu(x, approximate=True)

def _silu(x):
    return jax.nn.silu(x)

def _sigmoid(x):
    return jax.nn.sigmoid(x)

def _layernorm(x, axis=-1, eps=1e-05):
    m = jnp.mean(x, axis=axis, keepdims=True)
    v = jnp.var(x, axis=axis, keepdims=True)
    return (x - m) / jnp.sqrt(v + eps)

def _scatter_add(tgt, idx, src, axis=0):
    return tgt.at[idx].add(src)

def _segment_sum(src, seg, n):
    return jax.ops.segment_sum(src, seg, n)
kernel_name = 'mk_flamingo_gated_d4_seqx_r8_e7e8da'

def setup_inputs(seed: int=0):
    np.random.seed(seed)
    _w = jnp.asarray

    def _rec_inputs():
        import jax
        import jax.numpy as jnp
        _rk = jax.random.key(seed)
        x = 0.01048 + 0.1018 * jax.random.normal(jax.random.fold_in(_rk, 1), (4, 256, 256), jnp.float32)
        _lenS = 256 - jax.random.randint(jax.random.fold_in(_rk, 7), (4,), 0, max(1, 256 // 4) + 1, jnp.int32)
        _lenS2 = 256 - jax.random.randint(jax.random.fold_in(_rk, 8), (4,), 0, max(1, 256 // 4) + 1, jnp.int32)
        _ctx_512P = jax.random.normal(jax.random.fold_in(_rk, 11), (4, 16, 64), jnp.float32)
        _ctx_512c = jax.random.dirichlet(jax.random.fold_in(_rk, 511), 0.3 * jnp.ones((16,), jnp.float32), (4, 256))
        _ctx_512t = jnp.einsum('bsk,bkd->bsd', _ctx_512c, _ctx_512P)
        _ctx_512t = _ctx_512t * jax.lax.rsqrt(jnp.mean(jnp.square(_ctx_512t)) + 1e-12) * 0.953939
        ctx_512 = -0.000292821 + 1.00034 * (_ctx_512t + 0.3 * jax.random.normal(jax.random.fold_in(_rk, 611), (4, 256, 64), jnp.float32))
        _validS = jnp.arange(256)[None, :] < _lenS[:, None]
        _validS2 = jnp.arange(256)[None, :] < _lenS2[:, None]
        _causal = jnp.tril(jnp.ones((256, 256), dtype=bool))
        mask_SxS2_bk1 = jnp.broadcast_to(_validS2[0:1, :], (256, 256))
        mask_BxS2_bf0 = jnp.logical_not(jnp.ones((4, 256), dtype=bool))
        _g = jax.random.normal(jax.random.fold_in(_rk, 9001), (2, 4), jnp.float32)
        _g = jnp.sign(_g) * jnp.maximum(jnp.abs(_g), 1.0) + (_g == 0) * 1.0
        g_xattn = _g[0]
        g_ffn = _g[1]
        return (x, ctx_512, mask_SxS2_bk1, mask_BxS2_bf0, g_xattn, g_ffn)
    x, ctx_512, mask_SxS2_bk1, mask_BxS2_bf0, g_xattn, g_ffn = _rec_inputs()

    def _L0_xattn_setup():
        import jax, jax.numpy as jnp
        import numpy as np
        LRELU_ALPHA = 0.2
        MASK_VAL = -10000000000.0
        B, N, F_IN = (4, 256, 64)
        H, F_OUT = (8, 32)
        F_HID = H * F_OUT

        def gat_layer(x, adj, W, a_self, a_neigh, b):
            feat = jnp.einsum('nf,hfo->hno', x, W)
            attn_self = jnp.einsum('hno,ho->hn', feat, a_self)
            attn_neigh = jnp.einsum('hno,ho->hn', feat, a_neigh)
            e = attn_self[:, :, None] + attn_neigh[:, None, :]
            e = jax.nn.leaky_relu(e, LRELU_ALPHA)
            e = e + MASK_VAL * (1.0 - adj)[None, :, :]
            alpha = jax.nn.softmax(e, axis=-1)
            out = jnp.einsum('hnm,hmo->hno', alpha, feat) + b[:, None, :]
            out = jnp.transpose(out, (1, 0, 2)).reshape(out.shape[1], -1)
            return jax.nn.elu(out)
        key = jax.random.key(seed)
        ks = jax.random.split(key, 10)
        feats = jax.random.normal(ks[0], (B, N, F_IN), dtype=jnp.float32)
        a = (jax.random.uniform(ks[1], (B, N, N)) < 0.01).astype(jnp.float32)
        adj = jnp.maximum(a, jnp.eye(N, dtype=jnp.float32)[None])
        s0 = 1.0 / np.sqrt(F_IN)
        s1 = 1.0 / np.sqrt(F_HID)
        return {'feats': feats, 'adj': adj, 'W0': jax.random.normal(ks[2], (H, F_IN, F_OUT), dtype=jnp.float32) * s0, 'a_self0': jax.random.normal(ks[3], (H, F_OUT), dtype=jnp.float32) * 0.1, 'a_neigh0': jax.random.normal(ks[4], (H, F_OUT), dtype=jnp.float32) * 0.1, 'b0': jnp.zeros((H, F_OUT), dtype=jnp.float32), 'W1': jax.random.normal(ks[5], (H, F_HID, F_OUT), dtype=jnp.float32) * s1, 'a_self1': jax.random.normal(ks[6], (H, F_OUT), dtype=jnp.float32) * 0.1, 'a_neigh1': jax.random.normal(ks[7], (H, F_OUT), dtype=jnp.float32) * 0.1, 'b1': jnp.zeros((H, F_OUT), dtype=jnp.float32)}
    _L0_xattn_all = _L0_xattn_setup()
    _L0_xattn_in = {k: v for k, v in _L0_xattn_all.items() if k in ('W0', 'a_self0', 'a_neigh0', 'b0', 'W1', 'a_self1', 'a_neigh1', 'b1')}
    del _L0_xattn_all

    def _L0_ffn_setup():
        import jax, jax.numpy as jnp
        import numpy as np
        HID = 256
        N_HEADS = 16
        N_KV = 16
        HEAD_DIM = HID // N_HEADS
        N_EXP = 8
        TOP_K = 2
        MOE_I = 176
        SH_I = 704
        EPS = 1e-06
        ROPE_THETA = 1000000.0

        def _rms(x, w):
            v = jnp.mean(jnp.square(x), axis=-1, keepdims=True)
            return x * jax.lax.rsqrt(v + EPS) * w

        def _rope(q, k):
            S, D = (q.shape[1], q.shape[-1])
            inv = 1.0 / ROPE_THETA ** (jnp.arange(0, D, 2, dtype=jnp.float32) / D)
            freqs = jnp.arange(S, dtype=jnp.float32)[:, None] * inv[None, :]
            emb = jnp.concatenate([freqs, freqs], axis=-1)
            cos = jnp.cos(emb)[None, :, None, :]
            sin = jnp.sin(emb)[None, :, None, :]

            def rot(t):
                t1, t2 = (t[..., :D // 2], t[..., D // 2:])
                return jnp.concatenate([-t2, t1], axis=-1)
            return (q * cos + rot(q) * sin, k * cos + rot(k) * sin)
        key = jax.random.key(seed)
        ks = jax.random.split(key, 20)
        s = 0.02
        d = {'x': jax.random.normal(ks[0], (2, 128, HID), jnp.float32), 'w_ln1': jnp.ones((HID,), jnp.float32), 'wq': jax.random.normal(ks[1], (HID, N_HEADS * HEAD_DIM), jnp.float32) * s, 'bq': jnp.zeros((N_HEADS * HEAD_DIM,), jnp.float32), 'wk': jax.random.normal(ks[2], (HID, N_KV * HEAD_DIM), jnp.float32) * s, 'bk': jnp.zeros((N_KV * HEAD_DIM,), jnp.float32), 'wv': jax.random.normal(ks[3], (HID, N_KV * HEAD_DIM), jnp.float32) * s, 'bv': jnp.zeros((N_KV * HEAD_DIM,), jnp.float32), 'wo': jax.random.normal(ks[4], (N_HEADS * HEAD_DIM, HID), jnp.float32) * s, 'w_ln2': jnp.ones((HID,), jnp.float32), 'w_router': jax.random.normal(ks[5], (HID, N_EXP), jnp.float32) * s, 'w_gate_e': jax.random.normal(ks[6], (N_EXP, HID, MOE_I), jnp.float32) * s, 'w_up_e': jax.random.normal(ks[7], (N_EXP, HID, MOE_I), jnp.float32) * s, 'w_down_e': jax.random.normal(ks[8], (N_EXP, MOE_I, HID), jnp.float32) * s, 'w_sh_gate': jax.random.normal(ks[9], (HID, SH_I), jnp.float32) * s, 'w_sh_up': jax.random.normal(ks[10], (HID, SH_I), jnp.float32) * s, 'w_sh_down': jax.random.normal(ks[11], (SH_I, HID), jnp.float32) * s, 'w_sh_eg': jax.random.normal(ks[12], (HID, 1), jnp.float32) * s}
        return d
    _L0_ffn_all = _L0_ffn_setup()
    _L0_ffn_in = {k: v for k, v in _L0_ffn_all.items() if k in ('w_ln1', 'wq', 'bq', 'wk', 'bk', 'wv', 'bv', 'wo', 'w_ln2', 'w_router', 'w_gate_e', 'w_up_e', 'w_down_e', 'w_sh_gate', 'w_sh_up', 'w_sh_down', 'w_sh_eg')}
    del _L0_ffn_all

    def _L1_xattn_setup():
        import jax, jax.numpy as jnp
        import numpy as np
        B, S, L = (2, 128, 128)
        DIM_Q, H, K, D_C, D_CQ, R = (256, 16, 128, 64, 192, 64)

        def _rope_tables(seq_len, dim, dtype):
            inv_freq = 1.0 / 10000.0 ** (jnp.arange(0, dim, 2, dtype=dtype) / dim)
            t = jnp.arange(seq_len, dtype=dtype)
            freqs = t[:, None] * inv_freq[None, :]
            sin = jnp.repeat(jnp.sin(freqs), 2, axis=-1)
            cos = jnp.repeat(jnp.cos(freqs), 2, axis=-1)
            return (sin, cos)

        def _rotate_half(x):
            h = x.shape[-1] // 2
            return jnp.concatenate([-x[..., h:], x[..., :h]], axis=-1)
        key = jax.random.key(seed)
        ks = jax.random.split(key, 8)
        s_in = 1.0 / np.sqrt(DIM_Q)
        s_k = 1.0 / np.sqrt(K)
        s_cq = 1.0 / np.sqrt(D_CQ)
        s_c = 1.0 / np.sqrt(D_C)
        return {'hidden_q': jax.random.normal(ks[0], (B, S, DIM_Q), jnp.float32), 'kv_c': jax.random.normal(ks[1], (B, L, D_C), jnp.float32), 'Wq': jax.random.normal(ks[2], (H * K, DIM_Q), jnp.float32) * s_in, 'w_kc_q': jax.random.normal(ks[3], (H, K, D_CQ), jnp.float32) * s_k, 'w_kc_kv': jax.random.normal(ks[4], (H, K, D_C), jnp.float32) * s_k, 'W_qr': jax.random.normal(ks[5], (H, D_CQ, R), jnp.float32) * s_cq / np.sqrt(R), 'W_kr': jax.random.normal(ks[6], (H, D_C, R), jnp.float32) * s_c, 'Wo': jax.random.normal(ks[7], (DIM_Q, H * K), jnp.float32) * s_k}
    _L1_xattn_all = _L1_xattn_setup()
    _L1_xattn_in = {k: v for k, v in _L1_xattn_all.items() if k in ('Wq', 'w_kc_q', 'w_kc_kv', 'W_qr', 'W_kr', 'Wo')}
    del _L1_xattn_all

    def _L1_ffn_setup():
        import jax, jax.numpy as jnp
        import numpy as np
        R = 64
        RP = 2
        K = 8
        SCALING = 16.0 / K
        key = jax.random.key(seed)
        ks = jax.random.split(key, 5)
        B, S, Din, Dout = (8, 512, 256, 256)
        x = jax.random.normal(ks[0], (B, S, Din), dtype=jnp.float32)
        base_W = jax.random.normal(ks[1], (Dout, Din), dtype=jnp.float32) * Din ** (-0.5)
        router_W = jax.random.normal(ks[2], (R // RP, Din), dtype=jnp.float32) * Din ** (-0.5)
        A = jax.random.normal(ks[3], (R, Din), dtype=jnp.float32) * Din ** (-0.5)
        Bw = jax.random.normal(ks[4], (Dout, R), dtype=jnp.float32) * R ** (-0.5)
        biases = jnp.zeros((R,), dtype=jnp.float32)
        return {'x': x, 'base_W': base_W, 'router_W': router_W, 'A': A, 'B': Bw, 'biases': biases}
    _L1_ffn_all = _L1_ffn_setup()
    _L1_ffn_in = {k: v for k, v in _L1_ffn_all.items() if k in ('base_W', 'router_W', 'A', 'B', 'biases')}
    del _L1_ffn_all

    def _L2_xattn_setup():
        import jax, jax.numpy as jnp
        import numpy as np
        B, S, H = (8, 256, 64)
        key = jax.random.key(seed)
        kq, kk, kqc, kwq, kwk = jax.random.split(key, 5)
        q = jax.random.normal(kq, (B, S, H), dtype=jnp.float32)
        k = jax.random.normal(kk, (B, S, H), dtype=jnp.float32)
        qc_score = jax.random.uniform(kqc, (B, S, S), dtype=jnp.float32)
        attn_mask = jnp.triu(jnp.ones((S, S), dtype=bool), k=1)
        key_padding_mask = jnp.zeros((B, S), dtype=bool)
        scale = 1.0 / np.sqrt(H)
        Wq = jax.random.normal(kwq, (H, H), dtype=jnp.float32) * scale
        Wk = jax.random.normal(kwk, (H, H), dtype=jnp.float32) * scale
        bq = jnp.zeros((H,), dtype=jnp.float32)
        bk = jnp.zeros((H,), dtype=jnp.float32)
        return {'q': q, 'k': k, 'attn_mask': attn_mask, 'key_padding_mask': key_padding_mask, 'qc_score': qc_score, 'Wq': Wq, 'bq': bq, 'Wk': Wk, 'bk': bk}
    _L2_xattn_all = _L2_xattn_setup()
    _L2_xattn_in = {k: v for k, v in _L2_xattn_all.items() if k in ('Wq', 'bq', 'Wk', 'bk')}
    del _L2_xattn_all

    def _L2_ffn_setup():
        import jax, jax.numpy as jnp
        import numpy as np
        E = 8
        K = 2
        CAP = 64
        H = 256
        F = 1024
        key = jax.random.key(seed)
        ks = jax.random.split(key, 6)
        inp = {'hidden_states': jax.random.normal(ks[0], (2, 128, H), jnp.float32), 'router_w': jax.random.normal(ks[1], (E, H), jnp.float32) * (0.01 / np.sqrt(H)), 'w1': jax.random.normal(ks[2], (F, H), jnp.float32) * (1.0 / np.sqrt(H)), 'b1': jax.random.normal(ks[3], (F,), jnp.float32) * 0.01, 'w2': jax.random.normal(ks[4], (H, F), jnp.float32) * (1.0 / np.sqrt(F)), 'b2': jax.random.normal(ks[5], (H,), jnp.float32) * 0.01}
        return inp
    _L2_ffn_all = _L2_ffn_setup()
    _L2_ffn_in = {k: v for k, v in _L2_ffn_all.items() if k in ('router_w', 'w1', 'b1', 'w2', 'b2')}
    del _L2_ffn_all

    def _L3_xattn_setup():
        import jax, jax.numpy as jnp
        import numpy as np
        B, S, H, NH, L = (2, 256, 256, 16, 64)
        HD = H // NH
        key = jax.random.key(seed)
        k1, k2, k3, k4, k5 = jax.random.split(key, 5)
        scale = 0.02
        return {'q': jax.random.normal(k1, (B, S, H), dtype=jnp.float32), 'latent_kv': jax.random.normal(k2, (B, S, L), dtype=jnp.float32), 'Wq': jax.random.normal(k3, (H, H), dtype=jnp.float32) * scale, 'Wkv_expand': jax.random.normal(k4, (2 * H, L), dtype=jnp.float32) * scale, 'Wout': jax.random.normal(k5, (H, H), dtype=jnp.float32) * scale}
    _L3_xattn_all = _L3_xattn_setup()
    _L3_xattn_in = {k: v for k, v in _L3_xattn_all.items() if k in ('Wq', 'Wkv_expand', 'Wout')}
    del _L3_xattn_all

    def _L3_ffn_setup():
        import jax, jax.numpy as jnp
        import numpy as np
        TOPK = 2
        N_EXPERTS = 8
        ROUTE_SCALE = 1.0
        key = jax.random.key(seed)
        ks = jax.random.split(key, 7)
        B, T, C = (4, 256, 256)
        H = 176
        HS = 352
        E = N_EXPERTS
        s = 0.02
        return {'x': jax.random.normal(ks[0], (B, T, C), jnp.float32), 'gate_w': jax.random.normal(ks[1], (E, C), jnp.float32) * s, 'gate_bias': jnp.zeros((E,), jnp.float32), 'shared_gw': jax.random.normal(ks[2], (2 * HS, C), jnp.float32) * s, 'shared_dw': jax.random.normal(ks[3], (C, HS), jnp.float32) * s, 'up_w': jax.random.normal(ks[4], (E, 2 * H, C), jnp.float32) * s, 'down_w': jax.random.normal(ks[5], (E, C, H), jnp.float32) * s}
    _L3_ffn_all = _L3_ffn_setup()
    _L3_ffn_in = {k: v for k, v in _L3_ffn_all.items() if k in ('gate_w', 'gate_bias', 'shared_gw', 'shared_dw', 'up_w', 'down_w')}
    del _L3_ffn_all
    return {'x': x, 'ctx_512': ctx_512, 'mask_SxS2_bk1': mask_SxS2_bk1, 'mask_BxS2_bf0': mask_BxS2_bf0, 'g_xattn': g_xattn, 'g_ffn': g_ffn, 'L0_xattn_W0': _L0_xattn_in['W0'], 'L0_xattn_a_self0': _L0_xattn_in['a_self0'], 'L0_xattn_a_neigh0': _L0_xattn_in['a_neigh0'], 'L0_xattn_b0': _L0_xattn_in['b0'], 'L0_xattn_W1': _L0_xattn_in['W1'], 'L0_xattn_a_self1': _L0_xattn_in['a_self1'], 'L0_xattn_a_neigh1': _L0_xattn_in['a_neigh1'], 'L0_xattn_b1': _L0_xattn_in['b1'], 'L0_ffn_w_ln1': _L0_ffn_in['w_ln1'], 'L0_ffn_wq': _L0_ffn_in['wq'], 'L0_ffn_bq': _L0_ffn_in['bq'], 'L0_ffn_wk': _L0_ffn_in['wk'], 'L0_ffn_bk': _L0_ffn_in['bk'], 'L0_ffn_wv': _L0_ffn_in['wv'], 'L0_ffn_bv': _L0_ffn_in['bv'], 'L0_ffn_wo': _L0_ffn_in['wo'], 'L0_ffn_w_ln2': _L0_ffn_in['w_ln2'], 'L0_ffn_w_router': _L0_ffn_in['w_router'], 'L0_ffn_w_gate_e': _L0_ffn_in['w_gate_e'], 'L0_ffn_w_up_e': _L0_ffn_in['w_up_e'], 'L0_ffn_w_down_e': _L0_ffn_in['w_down_e'], 'L0_ffn_w_sh_gate': _L0_ffn_in['w_sh_gate'], 'L0_ffn_w_sh_up': _L0_ffn_in['w_sh_up'], 'L0_ffn_w_sh_down': _L0_ffn_in['w_sh_down'], 'L0_ffn_w_sh_eg': _L0_ffn_in['w_sh_eg'], 'L1_xattn_Wq': _L1_xattn_in['Wq'], 'L1_xattn_w_kc_q': _L1_xattn_in['w_kc_q'], 'L1_xattn_w_kc_kv': _L1_xattn_in['w_kc_kv'], 'L1_xattn_W_qr': _L1_xattn_in['W_qr'], 'L1_xattn_W_kr': _L1_xattn_in['W_kr'], 'L1_xattn_Wo': _L1_xattn_in['Wo'], 'L1_ffn_base_W': _L1_ffn_in['base_W'], 'L1_ffn_router_W': _L1_ffn_in['router_W'], 'L1_ffn_A': _L1_ffn_in['A'], 'L1_ffn_B': _L1_ffn_in['B'], 'L1_ffn_biases': _L1_ffn_in['biases'], 'L2_xattn_Wq': _L2_xattn_in['Wq'], 'L2_xattn_bq': _L2_xattn_in['bq'], 'L2_xattn_Wk': _L2_xattn_in['Wk'], 'L2_xattn_bk': _L2_xattn_in['bk'], 'L2_ffn_router_w': _L2_ffn_in['router_w'], 'L2_ffn_w1': _L2_ffn_in['w1'], 'L2_ffn_b1': _L2_ffn_in['b1'], 'L2_ffn_w2': _L2_ffn_in['w2'], 'L2_ffn_b2': _L2_ffn_in['b2'], 'L3_xattn_Wq': _L3_xattn_in['Wq'], 'L3_xattn_Wkv_expand': _L3_xattn_in['Wkv_expand'], 'L3_xattn_Wout': _L3_xattn_in['Wout'], 'L3_ffn_gate_w': _L3_ffn_in['gate_w'], 'L3_ffn_gate_bias': _L3_ffn_in['gate_bias'], 'L3_ffn_shared_gw': _L3_ffn_in['shared_gw'], 'L3_ffn_shared_dw': _L3_ffn_in['shared_dw'], 'L3_ffn_up_w': _L3_ffn_in['up_w'], 'L3_ffn_down_w': _L3_ffn_in['down_w']}

def reference(x, ctx_512, mask_SxS2_bk1, mask_BxS2_bf0, g_xattn, g_ffn, L0_xattn_W0, L0_xattn_a_self0, L0_xattn_a_neigh0, L0_xattn_b0, L0_xattn_W1, L0_xattn_a_self1, L0_xattn_a_neigh1, L0_xattn_b1, L0_ffn_w_ln1, L0_ffn_wq, L0_ffn_bq, L0_ffn_wk, L0_ffn_bk, L0_ffn_wv, L0_ffn_bv, L0_ffn_wo, L0_ffn_w_ln2, L0_ffn_w_router, L0_ffn_w_gate_e, L0_ffn_w_up_e, L0_ffn_w_down_e, L0_ffn_w_sh_gate, L0_ffn_w_sh_up, L0_ffn_w_sh_down, L0_ffn_w_sh_eg, L1_xattn_Wq, L1_xattn_w_kc_q, L1_xattn_w_kc_kv, L1_xattn_W_qr, L1_xattn_W_kr, L1_xattn_Wo, L1_ffn_base_W, L1_ffn_router_W, L1_ffn_A, L1_ffn_B, L1_ffn_biases, L2_xattn_Wq, L2_xattn_bq, L2_xattn_Wk, L2_xattn_bk, L2_ffn_router_w, L2_ffn_w1, L2_ffn_b1, L2_ffn_w2, L2_ffn_b2, L3_xattn_Wq, L3_xattn_Wkv_expand, L3_xattn_Wout, L3_ffn_gate_w, L3_ffn_gate_bias, L3_ffn_shared_gw, L3_ffn_shared_dw, L3_ffn_up_w, L3_ffn_down_w):
    import jax
    import jax.numpy as jnp

    def _L0_xattn_ref(feats, adj, W0, a_self0, a_neigh0, b0, W1, a_self1, a_neigh1, b1):
        import jax, jax.numpy as jnp
        import numpy as np
        LRELU_ALPHA = 0.2
        MASK_VAL = -10000000000.0
        B, N, F_IN = (4, 256, 64)
        H, F_OUT = (8, 32)
        F_HID = H * F_OUT

        def gat_layer(x, adj, W, a_self, a_neigh, b):
            feat = jnp.einsum('nf,hfo->hno', x, W)
            attn_self = jnp.einsum('hno,ho->hn', feat, a_self)
            attn_neigh = jnp.einsum('hno,ho->hn', feat, a_neigh)
            e = attn_self[:, :, None] + attn_neigh[:, None, :]
            e = jax.nn.leaky_relu(e, LRELU_ALPHA)
            e = e + MASK_VAL * (1.0 - adj)[None, :, :]
            alpha = jax.nn.softmax(e, axis=-1)
            out = jnp.einsum('hnm,hmo->hno', alpha, feat) + b[:, None, :]
            out = jnp.transpose(out, (1, 0, 2)).reshape(out.shape[1], -1)
            return jax.nn.elu(out)

        def per_graph(x, a):
            h = gat_layer(x, a, W0, a_self0, a_neigh0, b0)
            return gat_layer(h, a, W1, a_self1, a_neigh1, b1)
        return jax.vmap(per_graph)(feats, adj)

    def _L0_ffn_ref(x, w_ln1, wq, bq, wk, bk, wv, bv, wo, w_ln2, w_router, w_gate_e, w_up_e, w_down_e, w_sh_gate, w_sh_up, w_sh_down, w_sh_eg):
        import jax, jax.numpy as jnp
        import numpy as np
        HID = 256
        N_HEADS = 16
        N_KV = 16
        HEAD_DIM = HID // N_HEADS
        N_EXP = 8
        TOP_K = 2
        MOE_I = 176
        SH_I = 704
        EPS = 1e-06
        ROPE_THETA = 1000000.0

        def _rms(x, w):
            v = jnp.mean(jnp.square(x), axis=-1, keepdims=True)
            return x * jax.lax.rsqrt(v + EPS) * w

        def _rope(q, k):
            S, D = (q.shape[1], q.shape[-1])
            inv = 1.0 / ROPE_THETA ** (jnp.arange(0, D, 2, dtype=jnp.float32) / D)
            freqs = jnp.arange(S, dtype=jnp.float32)[:, None] * inv[None, :]
            emb = jnp.concatenate([freqs, freqs], axis=-1)
            cos = jnp.cos(emb)[None, :, None, :]
            sin = jnp.sin(emb)[None, :, None, :]

            def rot(t):
                t1, t2 = (t[..., :D // 2], t[..., D // 2:])
                return jnp.concatenate([-t2, t1], axis=-1)
            return (q * cos + rot(q) * sin, k * cos + rot(k) * sin)
        B, S, H = x.shape
        h = _rms(x, w_ln1)
        q = (h @ wq + bq).reshape(B, S, N_HEADS, HEAD_DIM)
        k = (h @ wk + bk).reshape(B, S, N_KV, HEAD_DIM)
        v = (h @ wv + bv).reshape(B, S, N_KV, HEAD_DIM)
        q, k = _rope(q, k)
        rep = N_HEADS // N_KV
        if rep > 1:
            k = jnp.repeat(k, rep, axis=2)
            v = jnp.repeat(v, rep, axis=2)
        scores = jnp.einsum('bqhd,bkhd->bhqk', q, k) * HEAD_DIM ** (-0.5)
        causal = jnp.tril(jnp.ones((S, S), bool))
        scores = jnp.where(causal[None, None], scores, jnp.finfo(scores.dtype).min)
        attn = jax.nn.softmax(scores, axis=-1)
        ctx = jnp.einsum('bhqk,bkhd->bqhd', attn, v).reshape(B, S, N_HEADS * HEAD_DIM)
        x = x + ctx @ wo
        h = _rms(x, w_ln2).reshape(B * S, H)
        logits = h @ w_router
        probs = jax.nn.softmax(logits, axis=-1)
        top_w, top_i = jax.lax.top_k(probs, TOP_K)
        combine = jnp.sum(jax.nn.one_hot(top_i, N_EXP, dtype=h.dtype) * top_w[..., None], axis=1)
        g = jnp.einsum('th,ehi->eti', h, w_gate_e)
        u = jnp.einsum('th,ehi->eti', h, w_up_e)
        y = jnp.einsum('eti,eih->eth', jax.nn.silu(g) * u, w_down_e)
        routed = jnp.einsum('eth,te->th', y, combine)
        sh = jax.nn.silu(h @ w_sh_gate) * (h @ w_sh_up) @ w_sh_down
        sh = sh * jax.nn.sigmoid(h @ w_sh_eg)
        x = x + (routed + sh).reshape(B, S, H)
        return x

    def _L1_xattn_ref(hidden_q, kv_c, Wq, w_kc_q, w_kc_kv, W_qr, W_kr, Wo):
        import jax, jax.numpy as jnp
        import numpy as np
        B, S, L = (2, 128, 128)
        DIM_Q, H, K, D_C, D_CQ, R = (256, 16, 128, 64, 192, 64)

        def _rope_tables(seq_len, dim, dtype):
            inv_freq = 1.0 / 10000.0 ** (jnp.arange(0, dim, 2, dtype=dtype) / dim)
            t = jnp.arange(seq_len, dtype=dtype)
            freqs = t[:, None] * inv_freq[None, :]
            sin = jnp.repeat(jnp.sin(freqs), 2, axis=-1)
            cos = jnp.repeat(jnp.cos(freqs), 2, axis=-1)
            return (sin, cos)

        def _rotate_half(x):
            h = x.shape[-1] // 2
            return jnp.concatenate([-x[..., h:], x[..., :h]], axis=-1)
        b, s, _ = hidden_q.shape
        l = kv_c.shape[1]
        q_hk = (hidden_q @ Wq.T).reshape(b, s, H, K)
        q_big = jnp.einsum('bshk,hkq->bshq', q_hk, w_kc_q)
        sin, cos = _rope_tables(l, D_C, kv_c.dtype)
        kv_rope = kv_c * cos[None] + _rotate_half(kv_c) * sin[None]
        q_r = jnp.einsum('bshq,hqr->bhsr', q_big, W_qr)
        k_r = jnp.einsum('bld,hdr->bhlr', kv_rope, W_kr)
        scores = jnp.einsum('bhsr,bhlr->bhsl', q_r, k_r)
        attn = jax.nn.softmax(scores, axis=-1)
        ctx_c = jnp.einsum('bhsl,bld->bhsd', attn, kv_rope)
        ctx_lat = jnp.einsum('bhsd,hkd->bshk', ctx_c, w_kc_kv)
        out = ctx_lat.reshape(b, s, H * K) @ Wo.T
        return out

    def _L1_ffn_ref(x, base_W, router_W, A, B, biases):
        import jax, jax.numpy as jnp
        import numpy as np
        R = 64
        RP = 2
        K = 8
        SCALING = 16.0 / K
        Bsz, S, Din = x.shape
        N = Bsz * S
        xf = x.reshape(N, Din)
        logits = jax.nn.sigmoid(xf @ router_W.T)
        logits = jnp.repeat(logits, RP, axis=-1) + biases
        top_v, top_i = jax.lax.top_k(logits, K)
        rows = jnp.arange(N)[:, None]
        sparse = jnp.zeros((N, R), dtype=x.dtype).at[rows, top_i].set(top_v)
        gating = sparse / jnp.sum(sparse, axis=-1, keepdims=True) * K
        mid = xf @ A.T
        lora_out = mid * gating @ B.T
        base = xf @ base_W.T
        out = base + SCALING * lora_out
        return out.reshape(Bsz, S, -1)

    def _L2_xattn_ref(q, k, attn_mask, key_padding_mask, qc_score, Wq, bq, Wk, bk):
        import jax, jax.numpy as jnp
        import numpy as np
        B, S, H = (8, 256, 64)
        qp = jnp.einsum('bsh,oh->bso', q, Wq) + bq
        kp = jnp.einsum('bth,oh->bto', k, Wk) + bk
        scaling = jnp.asarray(float(H) ** (-0.5), dtype=qp.dtype)
        scores = jnp.einsum('bsh,bth->bst', qp, kp) * scaling
        scores = scores * qc_score
        mask = attn_mask[None, :, :] | key_padding_mask[:, None, :]
        scores = jnp.where(mask, -jnp.inf, scores)
        return jax.nn.softmax(scores, axis=-1)

    def _L2_ffn_ref(hidden_states, router_w, w1, b1, w2, b2):
        import jax, jax.numpy as jnp
        import numpy as np
        E = 8
        K = 2
        CAP = 64
        H = 256
        F = 1024
        orig_shape = hidden_states.shape
        x = hidden_states.reshape(-1, H)
        N = x.shape[0]
        logits = x @ router_w.T
        probs = jax.nn.softmax(logits, axis=-1)
        top_p, top_i = jax.lax.top_k(probs, K)
        expert_flat = top_i.T.reshape(-1)
        probs_flat = top_p.T.reshape(-1)
        token_idx = jnp.tile(jnp.arange(N), K)
        onehot = (expert_flat[:, None] == jnp.arange(E)[None, :]).astype(jnp.int32)
        pos = jnp.take_along_axis(jnp.cumsum(onehot, axis=0), expert_flat[:, None], axis=1)[:, 0] - 1
        keep = pos < CAP
        dest = expert_flat * CAP + pos
        dest_m = jnp.where(keep, dest, E * CAP)
        buf = jnp.zeros((E * CAP, H), x.dtype).at[dest_m].set(x[token_idx], mode='drop')
        h = jax.nn.gelu(buf @ w1.T + b1, approximate=False) @ w2.T + b2
        gathered = jnp.where(keep[:, None], h[jnp.where(keep, dest, 0)], 0.0) * probs_flat[:, None]
        out = jnp.zeros_like(x).at[token_idx].add(gathered)
        return out.reshape(orig_shape)

    def _L3_xattn_ref(q, latent_kv, Wq, Wkv_expand, Wout):
        import jax, jax.numpy as jnp
        import numpy as np
        B, S, H, NH, L = (2, 256, 256, 16, 64)
        HD = H // NH
        b, sq, _ = q.shape
        sk = latent_kv.shape[1]
        qp = q @ Wq.T
        kv = latent_kv @ Wkv_expand.T
        k, v = jnp.split(kv, 2, axis=-1)
        qh = qp.reshape(b, sq, NH, HD).transpose(0, 2, 1, 3)
        kh = k.reshape(b, sk, NH, HD).transpose(0, 2, 1, 3)
        vh = v.reshape(b, sk, NH, HD).transpose(0, 2, 1, 3)
        inv_sqrt_d = 1.0 / jnp.sqrt(jnp.float32(HD))
        scores = jnp.einsum('bhqd,bhkd->bhqk', qh, kh) * inv_sqrt_d
        causal = jnp.tril(jnp.ones((sq, sk), dtype=bool))
        scores = jnp.where(causal, scores, jnp.finfo(scores.dtype).min)
        attn = jax.nn.softmax(scores, axis=-1)
        out = jnp.einsum('bhqk,bhkd->bhqd', attn, vh)
        out = out.transpose(0, 2, 1, 3).reshape(b, sq, H)
        return out @ Wout.T

    def _L3_ffn_ref(x, gate_w, gate_bias, shared_gw, shared_dw, up_w, down_w):
        import jax, jax.numpy as jnp
        import numpy as np
        TOPK = 2
        N_EXPERTS = 8
        ROUTE_SCALE = 1.0
        B, T, C = x.shape
        xf = x.reshape(-1, C)
        yg = xf @ shared_gw.T
        y, g = jnp.split(yg, 2, axis=-1)
        shared = jax.nn.silu(g) * y @ shared_dw.T
        scores = jax.nn.sigmoid(xf @ gate_w.T)
        _, topk_idx = jax.lax.top_k(scores + gate_bias, TOPK)
        w = jnp.take_along_axis(scores, topk_idx, axis=-1)
        w = w / jnp.sum(w, axis=-1, keepdims=True) * ROUTE_SCALE
        out = jnp.zeros_like(xf)
        for e in range(N_EXPERTS):
            we = jnp.sum(jnp.where(topk_idx == e, w, 0.0), axis=-1)
            gu = xf @ up_w[e].T
            g_e, u_e = jnp.split(gu, 2, axis=-1)
            h = jax.nn.silu(g_e) * u_e
            out = out + h @ down_w[e].T * we[:, None]
        return (shared + out).reshape(B, T, C)
    x = x + jnp.tanh(g_xattn[0]) * _L0_xattn_ref(ctx_512, _layernorm(x, axis=-1), L0_xattn_W0, L0_xattn_a_self0, L0_xattn_a_neigh0, L0_xattn_b0, L0_xattn_W1, L0_xattn_a_self1, L0_xattn_a_neigh1, L0_xattn_b1)
    x = x + jnp.tanh(g_ffn[0]) * _L0_ffn_ref(_layernorm(x, axis=-1), L0_ffn_w_ln1, L0_ffn_wq, L0_ffn_bq, L0_ffn_wk, L0_ffn_bk, L0_ffn_wv, L0_ffn_bv, L0_ffn_wo, L0_ffn_w_ln2, L0_ffn_w_router, L0_ffn_w_gate_e, L0_ffn_w_up_e, L0_ffn_w_down_e, L0_ffn_w_sh_gate, L0_ffn_w_sh_up, L0_ffn_w_sh_down, L0_ffn_w_sh_eg)
    x = x + jnp.tanh(g_xattn[1]) * _L1_xattn_ref(_layernorm(x, axis=-1), ctx_512, L1_xattn_Wq, L1_xattn_w_kc_q, L1_xattn_w_kc_kv, L1_xattn_W_qr, L1_xattn_W_kr, L1_xattn_Wo)
    x = x + jnp.tanh(g_ffn[1]) * _L1_ffn_ref(_layernorm(x, axis=-1), L1_ffn_base_W, L1_ffn_router_W, L1_ffn_A, L1_ffn_B, L1_ffn_biases)
    x = x + jnp.tanh(g_xattn[2]) * _L2_xattn_ref(ctx_512, ctx_512, mask_SxS2_bk1, mask_BxS2_bf0, _layernorm(x, axis=-1), L2_xattn_Wq, L2_xattn_bq, L2_xattn_Wk, L2_xattn_bk)
    x = x + jnp.tanh(g_ffn[2]) * _L2_ffn_ref(_layernorm(x, axis=-1), L2_ffn_router_w, L2_ffn_w1, L2_ffn_b1, L2_ffn_w2, L2_ffn_b2)
    x = x + jnp.tanh(g_xattn[3]) * _L3_xattn_ref(_layernorm(x, axis=-1), ctx_512, L3_xattn_Wq, L3_xattn_Wkv_expand, L3_xattn_Wout)
    x = x + jnp.tanh(g_ffn[3]) * _L3_ffn_ref(_layernorm(x, axis=-1), L3_ffn_gate_w, L3_ffn_gate_bias, L3_ffn_shared_gw, L3_ffn_shared_dw, L3_ffn_up_w, L3_ffn_down_w)
    return x

_drawn_inputs = setup_inputs


def setup_inputs(seed=0):
    import zlib

    import numpy as np

    out = dict(_drawn_inputs(seed))
    spreads = {'L0_xattn_b0': (0.0, 0.1),
     'L0_xattn_b1': (0.0, 0.1),
     'L0_ffn_w_ln1': (1.0, 0.2),
     'L0_ffn_bq': (0.0, 0.666),
     'L0_ffn_bk': (0.0, 0.8),
     'L0_ffn_bv': (0.0, 0.1),
     'L0_ffn_w_ln2': (1.0, 0.2),
     'L1_ffn_biases': (0.0, 0.1),
     'L2_xattn_bq': (0.0, 0.8),
     'L2_xattn_bk': (0.0, 2.0),
     'L3_ffn_gate_bias': (0.0, 0.8)}
    factors = {'L0_ffn_wq': 3.538,
     'L2_xattn_Wq': 5.664,
     'L2_xattn_Wk': 5.484,
     'L2_ffn_router_w': 3.259,
     'L2_ffn_b1': 8.0,
     'L2_ffn_b2': 8.0,
     'L3_xattn_Wq': 8.0,
     'L3_xattn_Wkv_expand': 4.365,
     'L3_xattn_Wout': 4.456,
     'L3_ffn_gate_w': 8.0,
     'L3_ffn_shared_gw': 5.281,
     'L3_ffn_shared_dw': 5.47,
     'L3_ffn_up_w': 8.0,
     'L3_ffn_down_w': 8.0}
    for name, (base, spread) in spreads.items():
        noise = np.random.default_rng([zlib.crc32(name.encode()), seed]).standard_normal(out[name].shape)
        drawn = base * np.exp(spread * noise) if base else spread * noise
        out[name] = jnp.asarray(drawn.astype(out[name].dtype))
    for name, factor in factors.items():
        out[name] = (out[name] * factor).astype(out[name].dtype)
    return out
```

```python
from contextlib import ExitStack

import numpy as np
import concourse.bass as bass
from concourse import mybir

F32 = mybir.dt.float32
F32R = mybir.dt.float32r
BF16 = mybir.dt.bfloat16
U8 = mybir.dt.uint8
ALU = mybir.AluOpType
ACT = mybir.ActivationFunctionType
AX = mybir.AxisListType

P = 128
B, S, C = 4, 256, 256
DC = 64
TT = 4
TOK = TT * P
PAIRS = B * S // TOK
KC = C // P
GH, GO = 8, 32
NH, HD = 16, 16
MH = 16
NE = 8
CAP = 64
MOE_I, SH_I = 176, 704
H3, HS3 = 176, 352
T0 = -(-(NE * MOE_I + SH_I) // P)
T3 = -(-(NE * H3 + HS3) // P)
T2 = 1024 // P
LR = 64
MASKED = -1.0e30

WCOLS = [
    ("gat0", GH * GO), ("gat1", KC * GH * GO),
    ("qk0", KC * 4 * C), ("v0", KC * C), ("o0", KC * C), ("rt0", KC * 16),
    ("l1f", KC * 352), ("l1b", C),
    ("qk2", 2 * P), ("rt2", KC * 8),
    ("q3", KC * C), ("k3", C), ("v3", C), ("o3", KC * C), ("rt3", KC * 8),
]
CCOLS = [
    ("ident", P), ("causal", P), ("headmask", 8), ("halfmask", 2), ("tri", P),
    ("ropec", S), ("ropes", S), ("kvc", 2 * DC), ("kvs", 2 * DC), ("lower", NE * NE), ("upper", NE * NE),
    ("ln1", KC), ("ln2", KC), ("qkb", 8), ("b1f", T2), ("qkb2", 2),
    ("aself0", 256), ("aneigh0", 256), ("aself1", 256), ("aneigh1", 256),
    ("gb0", 256), ("gb1", 256), ("bv0", 256), ("lora_b", LR), ("b2f", 256), ("gbias3", NE), ("gates", 8),
]


def offsets(cols):
    at, out = 0, {}
    for name, n in cols:
        out[name] = (at, n)
        at += n
    return out, at


WOFF, WTOT = offsets(WCOLS)
COFF, CTOT = offsets(CCOLS)
CHUNK = 1024
CHUNKS = -(-WTOT // CHUNK)
SEMS = range(99, 256)


def mm3(pe, out, left, right, first=True, last=True, skip=False):
    pe.matmul(out, left[0], right[0], start=first, stop=False, skip_group_check=skip)
    pe.matmul(out, left[0], right[1], start=False, stop=False, skip_group_check=skip)
    return pe.matmul(out, left[1], right[0], start=False, stop=last, skip_group_check=skip)


def build(nc, a, out):
    with ExitStack() as whole:
        def tensor(name, shape, dt=F32, stack=whole):
            return stack.enter_context(nc.sbuf_tensor(name, shape, dt))

        WH = tensor("WH", [P, CHUNKS * CHUNK], F32R)
        WL = tensor("WL", [P, CHUNKS * CHUNK], F32R)
        CP = tensor("CP", [P, CTOT])
        AH = tensor("AH", [P, KC, MH * DC], F32R)
        AL = tensor("AL", [P, KC, MH * DC], F32R)
        BH = tensor("BH", [P, MH // 2, C], F32R)
        BL = tensor("BL", [P, MH // 2, C], F32R)
        EH = tensor("EH", [P, 3, 16], F32R)
        EL = tensor("EL", [P, 3, 16], F32R)
        identb = tensor("identb", [P, P], BF16)
        causalb = tensor("causalb", [P, P], BF16)
        trib = tensor("trib", [P, P], BF16)
        onesb = tensor("onesb", [P, P], BF16)
        ones1 = tensor("ones1", [P, 80])
        halfneg = tensor("halfneg", [P, TT])
        gate = tensor("gate", [P, 8])
        XALL = tensor("XALL", [P, PAIRS * TT, C])
        OH = tensor("OH", [P, PAIRS * TT, 2 * NE], BF16)
        PW = tensor("PW", [P, PAIRS * TT, 2 * NE])
        COEF = tensor("COEF", [P, PAIRS * TT])
        COEF2 = tensor("COEF2", [P, TT])
        X = tensor("X", [P, TT, C])
        HN = tensor("HN", [P, TT, C])
        XN = tensor("XN", [P, TT, C])
        HH = tensor("HH", [P, KC, TOK], F32R)
        HL = tensor("HL", [P, KC, TOK], F32R)
        CTH = tensor("CTH", [P, TOK], F32R)
        CTL = tensor("CTL", [P, TOK], F32R)
        stats = tensor("stats", [P, TT, 6])
        mv = tensor("mv", [P, TT, 2])
        rstd = tensor("rstd", [P, TT])
        ssq = tensor("ssq", [P, TT])
        PS = whole.enter_context(nc.psum_tensor("PS", [P, 8, 512], F32))

        def const(name):
            at, n = COFF[name]
            return CP[:, at:at + n]

        def weight(name, k=1, t=0, lo=0, hi=None):
            at, n = WOFF[name]
            n //= k
            hi = n if hi is None else hi
            return WH[:, at + t * n + lo:at + t * n + hi], WL[:, at + t * n + lo:at + t * n + hi]

        def pair(hi, lo, *index):
            return hi[index], lo[index]

        ident = const("ident")

        class Phase:
            count = 0

            def __init__(self):
                self.stack = ExitStack()
                Phase.count += 1
                self.tag = f"p{Phase.count}_"

            def __enter__(self):
                return self

            def sem(self, names):
                return {n: self.stack.enter_context(nc.semaphore(self.tag + n)) for n in names.split()}

            def sems(self, name, n):
                return [self.stack.enter_context(nc.semaphore(f"{self.tag}{name}{i}")) for i in range(n)]

            def sb(self, name, shape, dt=F32):
                return tensor(self.tag + name, shape, dt, self.stack)

            def __exit__(self, *e):
                if e[0] is None:
                    nc.all_engine_barrier(sems_to_clear=SEMS)
                self.stack.close()

        LN = "ln_stats ln_aggr ln_eps ln_rstd ln_norm tr_done tr_hi tr_lo "

        def ln_vector(v, s):
            for t in range(TT):
                v.bn_stats(stats[:, t, :], X[:, t, :]).then_inc(s["ln_stats"], 1)
            for t in range(TT):
                v.wait_ge(s["ln_stats"], t + 1)
                v.bn_aggr(mv[:, t, :], stats[:, t, :]).then_inc(s["ln_aggr"], 1)
            v.wait_ge(s["ln_rstd"], 1)
            for t in range(TT):
                v.tensor_scalar(HN[:, t, :], X[:, t, :], mv[:, t, 0:1], rstd[:, t:t + 1],
                                ALU.subtract, ALU.mult).then_inc(s["ln_norm"], 1)

        def ln_gpsimd(g, s):
            g.wait_ge(s["ln_aggr"], TT)
            g.tensor_scalar(rstd[:, :], mv[:, :, 1], 1e-5, None, ALU.add).then_inc(s["ln_eps"], 1)
            g.wait_ge(s["ln_eps"], 1)
            g.tensor_tensor(rstd[:, :], rstd[:, :], halfneg[:, :], ALU.pow).then_inc(s["ln_rstd"], 1)

        def transpose_tensor(pe, src, ready, done, bank=0, tiles=KC):
            for t in range(TT):
                pe.wait_ge(ready, t + 1)
                for k in range(tiles):
                    m = pe.transpose(PS[:, bank + k, t * P:(t + 1) * P], src[:, t, k * P:(k + 1) * P], ident)
            m.then_inc(done, 1)

        def split_scalar(act, s, done, bank=0, hh=HH, tiles=KC, scale=None):
            act.wait_ge(done, 1)
            for k in range(tiles):
                if scale is None:
                    i = act.activation(hh[:, k, :], PS[:, bank + k, :], ACT.Copy)
                else:
                    i = act.activation(hh[:, k, :], PS[:, bank + k, :], ACT.Copy, scale=scale[:, k:k + 1])
                i.then_inc(s, 1)

        def split_vector(v, s_hi, s_lo, bank=0, hh=HH, hl=HL, tiles=KC, scale=None, base=0):
            for k in range(tiles):
                v.wait_ge(s_hi, base + k + 1)
                if scale is None:
                    i = v.tensor_tensor(hl[:, k, :], PS[:, bank + k, :], hh[:, k, :].bitcast(F32), ALU.subtract)
                else:
                    i = v.scalar_tensor_tensor(hl[:, k, :], PS[:, bank + k, :], scale[:, k:k + 1],
                                               hh[:, k, :].bitcast(F32), ALU.mult, ALU.subtract)
                i.then_inc(s_lo, 1)

        def rms_scalar(act, s, src, ready, junk):
            for t in range(TT):
                act.wait_ge(ready, t + 1)
                if t:
                    act.wait_ge(s["rms_sq"], t)
                act.activation(junk[:, :], src[:, t, :], ACT.Square, accum_out=ssq[:, t:t + 1]).then_inc(s["rms_sq"], 1)

        def rms_gpsimd(g, s):
            g.wait_ge(s["rms_sq"], TT)
            g.tensor_scalar(rstd[:, :], ssq[:, :], 1.0 / C, 1e-6, ALU.mult, ALU.add).then_inc(s["rms_eps"], 1)
            g.wait_ge(s["rms_eps"], 1)
            g.tensor_tensor(rstd[:, :], rstd[:, :], halfneg[:, :], ALU.pow).then_inc(s["rms_rstd"], 1)

        def rank_vector(v, s, buf, scores, n0):
            n = n0
            gt = buf[:, 0]
            ge = buf[:, 1]
            other = scores.unsqueeze(2).broadcast_to([P, TT, NE, NE])
            mine = scores.unsqueeze(3).broadcast_to([P, TT, NE, NE])
            up = const("upper").rearrange("p (a b) -> p a b", a=NE).unsqueeze(1).broadcast_to([P, TT, NE, NE])
            low = const("lower").rearrange("p (a b) -> p a b", a=NE).unsqueeze(1).broadcast_to([P, TT, NE, NE])
            for t in range(TT):
                v.tensor_tensor(gt[:, t], other[:, t], mine[:, t], ALU.is_gt).then_inc(s["rank"], 1)
                v.tensor_tensor(ge[:, t], other[:, t], mine[:, t], ALU.is_ge).then_inc(s["rank"], 1)
            n += 2 * TT
            v.wait_ge(s["rank"], n)
            for t in range(TT):
                v.tensor_tensor(gt[:, t], gt[:, t], up[:, t], ALU.mult).then_inc(s["rank"], 1)
                v.tensor_tensor(ge[:, t], ge[:, t], low[:, t], ALU.mult).then_inc(s["rank"], 1)
            n += 2 * TT
            v.wait_ge(s["rank"], n)
            v.tensor_tensor(gt, gt, ge, ALU.add).then_inc(s["rank"], 1)
            n += 1
            v.wait_ge(s["rank"], n)
            v.tensor_reduce(buf[:, 2, :, 0, :], gt, AX.X, ALU.add).then_inc(s["rank"], 1)
            n += 1
            v.wait_ge(s["rank"], n)
            return buf[:, 2, :, 0, :], n

        def setup_weights():
            with Phase() as ph:
                w_in = ph.sems("w_in", 4)
                s = ph.sem("xc_in w_hi w_lo c_set fold_in ext ext_hi ext_sp tanh")
                raw = ph.sb("raw", [P, 4, CHUNK])
                gat1w = ph.sb("gat1w", [P, 3, 256])
                extt = ph.sb("extt", [P, 6, 256])
                ext = ph.sb("ext", [P, 3, 16])
                with nc.Block() as block:
                    @block.sync
                    def _(sp):
                        sp.dma_start(CP[:, :], a["consts"]).then_inc(s["xc_in"], 16)
                        sp.dma_start(gat1w[:, :, :], a["wpack"][:, 0:768].rearrange("p (a b) -> p a b", a=3)).then_inc(s["xc_in"], 16)
                        sp.dma_start(XALL[:, :, :], a["x"].rearrange("(t p) c -> p t c", p=P)).then_inc(s["xc_in"], 16)
                        for i in range(CHUNKS):
                            if i >= 4:
                                sp.wait_ge(s["w_lo"], i - 3)
                            sp.dma_start(raw[:, i % 4, :], a["wpack"][:, i * CHUNK:(i + 1) * CHUNK]).then_inc(w_in[i % 4], 16)

                    @block.scalar
                    def _(act):
                        act.wait_ge(s["xc_in"], 48)
                        act.activation(gate[:, :], const("gates"), ACT.Tanh).then_inc(s["tanh"], 1)
                        act.wait_ge(s["ext"], 12)
                        act.activation(EH[:, :, :], ext[:, :, :], ACT.Copy).then_inc(s["ext_hi"], 1)
                        for i in range(CHUNKS):
                            act.wait_ge(w_in[i % 4], 16 * (i // 4 + 1))
                            act.activation(WH[:, i * CHUNK:(i + 1) * CHUNK], raw[:, i % 4, :], ACT.Copy).then_inc(s["w_hi"], 1)

                    @block.vector
                    def _(v):
                        v.memset(halfneg[:, :], -0.5).then_inc(s["c_set"], 1)
                        v.memset(ones1[:, :], 1.0).then_inc(s["c_set"], 1)
                        v.memset(onesb[:, :], 1.0).then_inc(s["c_set"], 1)
                        v.wait_ge(s["xc_in"], 48)
                        v.tensor_copy(identb[:, :], const("ident")).then_inc(s["c_set"], 1)
                        v.tensor_copy(causalb[:, :], const("causal")).then_inc(s["c_set"], 1)
                        v.tensor_copy(trib[:, :], const("tri")).then_inc(s["c_set"], 1)
                        for n, (k, c) in enumerate([(0, "aself0"), (0, "aneigh0"), (1, "aself1"), (1, "aneigh1"),
                                                    (2, "aself1"), (2, "aneigh1")]):
                            v.tensor_tensor(extt[:, n, :], gat1w[:, k, :], const(c), ALU.mult).then_inc(s["ext"], 1)
                        for n, k in enumerate([0, 0, 1, 1, 2, 2]):
                            v.wait_ge(s["ext"], 6)
                            v.tensor_reduce(ext[:, k, 8 * (n % 2):8 * (n % 2) + 8],
                                            extt[:, n, :].rearrange("p (h o) -> p h o", h=GH), AX.X, ALU.add).then_inc(s["ext"], 1)
                        v.wait_ge(s["ext_hi"], 1)
                        v.tensor_tensor(EL[:, :, :], ext[:, :, :], EH[:, :, :].bitcast(F32), ALU.subtract).then_inc(s["ext_sp"], 1)
                        for i in range(CHUNKS):
                            v.wait_ge(s["w_hi"], i + 1)
                            v.tensor_tensor(WL[:, i * CHUNK:(i + 1) * CHUNK], raw[:, i % 4, :],
                                            WH[:, i * CHUNK:(i + 1) * CHUNK].bitcast(F32), ALU.subtract).then_inc(s["w_lo"], 1)

        def setup_fold():
            with Phase() as ph:
                f_in = ph.sems("f_in", 4)
                s = ph.sem("m1 m1c m2 m2c ab ab_hi ab_lo")
                NF = 2 * P + 2 * DC + DC + C + DC + C
                fr = ph.sb("fr", [P, 4, NF])
                m1s = ph.sb("m1s", [P, 2, P])
                m2s = ph.sb("m2s", [P, 2, DC])
                with nc.Block() as block:
                    @block.sync
                    def _(sp):
                        for h in range(MH):
                            if h >= 4:
                                sp.wait_ge(s["ab"], h - 3)
                            sp.dma_start(fr[:, h % 4, :], a["fold"][h]).then_inc(f_in[h % 4], 16)

                    @block.tensor
                    def _(pe):
                        for h in range(MH):
                            r = fr[:, h % 4, :]
                            o = h % 2
                            pe.wait_ge(f_in[h % 4], 16 * (h // 4 + 1))
                            if h >= 2:
                                pe.wait_ge(s["m1c"], h - 1)
                            pe.matmul(PS[0:DC, o, 0:P], r[:, 256:320], r[:, 0:128], start=True, stop=False)
                            pe.matmul(PS[0:DC, o, 0:P], r[0:DC, 320:384], r[0:DC, 128:256], start=False, stop=True).then_inc(s["m1"], 1)
                            pe.wait_ge(s["m1c"], h + 1)
                            if h >= 2:
                                pe.wait_ge(s["m2c"], h - 1)
                            pe.matmul(PS[:, 2 + o, 0:DC], m1s[0:DC, o, :], r[0:DC, 384:448], start=True, stop=True).then_inc(s["m2"], 1)
                            pe.wait_ge(s["m2c"], h + 1)
                            if h >= 2:
                                pe.wait_ge(s["ab_lo"], 2 * (h - 1))
                            for k in range(KC):
                                pe.matmul(PS[:, 4 + o, k * DC:(k + 1) * DC], r[:, 448 + k * P:448 + (k + 1) * P], m2s[:, o, :],
                                          start=True, stop=True)
                            q = DC * o
                            pe.matmul(PS[q:q + DC, 6 + o, 0:C], r[:, 704:768], r[:, 768:1024], start=True, stop=True).then_inc(s["ab"], 1)

                    @block.scalar
                    def _(act):
                        for h in range(MH):
                            o, q = h % 2, DC * (h % 2)
                            act.wait_ge(s["ab"], h + 1)
                            act.activation(AH[:, :, h * DC:(h + 1) * DC],
                                           PS[:, 4 + o, 0:KC * DC].rearrange("p (k d) -> p k d", k=KC), ACT.Copy).then_inc(s["ab_hi"], 1)
                            act.activation(BH[q:q + DC, h // 2, :], PS[q:q + DC, 6 + o, 0:C], ACT.Copy).then_inc(s["ab_hi"], 1)

                    @block.vector
                    def _(v):
                        def small(h):
                            o = h % 2
                            v.wait_ge(s["m1"], h + 1)
                            v.tensor_copy(m1s[0:DC, o, :], PS[0:DC, o, 0:P]).then_inc(s["m1c"], 1)
                            v.wait_ge(s["m2"], h + 1)
                            v.tensor_copy(m2s[:, o, :], PS[:, 2 + o, 0:DC]).then_inc(s["m2c"], 1)

                        small(0)
                        for h in range(MH):
                            o, q = h % 2, DC * (h % 2)
                            if h + 1 < MH:
                                small(h + 1)
                            v.wait_ge(s["ab_hi"], 2 * h + 2)
                            v.tensor_tensor(AL[:, :, h * DC:(h + 1) * DC],
                                            PS[:, 4 + o, 0:KC * DC].rearrange("p (k d) -> p k d", k=KC),
                                            AH[:, :, h * DC:(h + 1) * DC].bitcast(F32), ALU.subtract).then_inc(s["ab_lo"], 1)
                            v.tensor_tensor(BL[q:q + DC, h // 2, :], PS[q:q + DC, 6 + o, 0:C],
                                            BH[q:q + DC, h // 2, :].bitcast(F32), ALU.subtract).then_inc(s["ab_lo"], 1)

        def load_pair(i, routed=False):
            with Phase() as ph:
                s = ph.sem("ct_in ct_hi x_cp")
                ctr = ph.sb("ctr", [P, TOK])
                with nc.Block() as block:
                    @block.sync
                    def _(sp):
                        sp.dma_start(ctr[:, :], a["ctxT"][:, bass.ts(i, TOK)]).then_inc(s["ct_in"], 16)
                        sp.wait_ge(s["ct_in"], 16)

                    @block.scalar
                    def _(act):
                        act.wait_ge(s["ct_in"], 16)
                        act.activation(CTH[:, :], ctr[:, :], ACT.Copy).then_inc(s["ct_hi"], 1)

                    @block.vector
                    def _(v):
                        v.tensor_copy(X[:, :, :], XALL[:, bass.ts(i, TT), :]).then_inc(s["x_cp"], 1)
                        if routed:
                            v.tensor_copy(COEF2[:, :], COEF[:, bass.ts(i, TT)]).then_inc(s["x_cp"], 1)
                        v.wait_ge(s["ct_hi"], 1)
                        v.tensor_tensor(CTL[:, :], ctr[:, :], CTH[:, :].bitcast(F32), ALU.subtract).then_inc(s["x_cp"], 1)

        def store_pair(i):
            with Phase() as ph:
                s = ph.sem("x_st")
                with nc.Block() as block:
                    @block.vector
                    def _(v):
                        v.tensor_copy(XALL[:, bass.ts(i, TT), :], X[:, :, :]).then_inc(s["x_st"], 1)

        def graph_attention():
            with Phase() as ph:
                s = ph.sem(LN + "adj base feat featc nb z lr e neg p pt pts pv o_r o_c y_b y_m y_e h1 tr1 hi1 lo1 one ft_s")
                BASE = ph.sb("BASE", [P, TT, S])
                FT = ph.sb("FT", [P, TT, GH, GO + 1])
                SV = ph.sb("SV", [P, TT, GH])
                Z = ph.sb("Z", [P, 2, 4, S])
                E = ph.sb("E", [P, 2, 4, S])
                PR = ph.sb("PR", [P, 2, 4, S])
                PTS = ph.sb("PTS", [P, 2, 2, 2, 2, P])
                mx = ph.sb("mx", [P, 2, 4])
                rin = ph.sb("rin", [P, 2, 4])
                O = ph.sb("O", [P, TT, GH, GO])
                YM = ph.sb("YM", [P, TT, C])
                YR = ph.sb("YR", [P, TT, C])
                NG = 2 * TT

                with nc.Block() as block:
                    @block.gpsimd
                    def _(g):
                        ln_gpsimd(g, s)

                    @block.tensor
                    def _(pe):
                        def pv(n, l):
                            hg, t = divmod(n % NG, TT)
                            pe.wait_ge(s["pts"], n + 1)
                            if n >= 2:
                                pe.wait_ge(s["o_c"], n - 1)
                            for hh in range(4):
                                for mt in range(2):
                                    m = pe.matmul(PS[:, 6 + n % 2, hh * 33:hh * 33 + 33], PTS[:, n % 2, hh // 2, hh % 2, mt, :],
                                                  FT[:, 2 * (t // 2) + mt, 4 * hg + hh, :], start=(mt == 0), stop=(mt == 1))
                            m.then_inc(s["pv"], 1)

                        for l in range(2):
                            def left(k, lo, hi):
                                return pair(CTH, CTL, slice(None), slice(lo, hi)) if l == 0 else \
                                    pair(HH, HL, slice(None), k, slice(lo, hi))
                            kt = 1 if l == 0 else KC
                            if l == 1:
                                pe.wait_ge(s["lo1"], KC)
                                pe.wait_ge(s["o_c"], NG)
                                pe.wait_ge(s["pts"], NG)
                            for t in range(TT):
                                for k in range(kt):
                                    mm3(pe, PS[:, 4 + t, 0:256], left(k, t * P, t * P + P), weight("gat%d" % l, kt, k), k == 0, k == kt - 1)
                                for k in range(kt):
                                    m = mm3(pe, PS[:, 4 + t, 256:264], left(k, t * P, t * P + P),
                                            pair(EH, EL, slice(None), l + k, slice(0, 8)), k == 0, k == kt - 1)
                                m.then_inc(s["feat"], 1)
                            def neighbours(hg):
                                if l + hg:
                                    pe.wait_ge(s["z"], NG * l + TT * hg)
                                for hh in range(4):
                                    h = 8 + 4 * hg + hh
                                    for k in range(kt):
                                        w = (EH[:, l + k, h:h + 1].broadcast_to([P, P]), EL[:, l + k, h:h + 1].broadcast_to([P, P]))
                                        m = mm3(pe, PS[:, hh, :], w, left(k, 0, TOK), k == 0, k == kt - 1)
                                m.then_inc(s["nb"], 1)

                            neighbours(0)
                            pe.wait_ge(s["featc"], 2 * TT * (l + 1))
                            for hg in range(2):
                                for t in range(TT):
                                    n = NG * l + TT * hg + t
                                    if hg == 0 and t == TT - 2:
                                        neighbours(1)
                                    pe.wait_ge(s["p"], n + 1)
                                    if n >= 1:
                                        pe.wait_ge(s["pts"], n)
                                    for hh in range(4):
                                        for mt in range(2):
                                            m = pe.transpose(PS[:, 4 + hh // 2, (hh % 2) * 256 + mt * P:(hh % 2) * 256 + mt * P + P],
                                                             PR[:, n % 2, hh, mt * P:mt * P + P], ident)
                                    m.then_inc(s["pt"], 1)
                                    if n > NG * l:
                                        pv(n - 1, l)
                            pv(NG * (l + 1) - 1, l)
                            if l == 0:
                                pe.wait_ge(s["z"], NG)
                                transpose_tensor(pe, YM, s["h1"], s["tr1"])

                    @block.scalar
                    def _(act):
                        for l in range(2):
                            for t in range(TT):
                                act.wait_ge(s["feat"], TT * l + t + 1)
                                if l:
                                    act.wait_ge(s["pv"], NG)
                                act.activation(FT[:, t, :, 0:GO], PS[:, 4 + t, 0:256].rearrange("p (h o) -> p h o", h=GH),
                                               ACT.Copy).then_inc(s["featc"], 1)
                                act.activation(SV[:, t, :], PS[:, 4 + t, 256:264], ACT.Copy).then_inc(s["featc"], 1)

                            def zs(n):
                                hg, t = divmod(n % NG, TT)
                                act.wait_ge(s["nb"], n // TT + 1)
                                act.wait_ge(s["featc"], 2 * TT * (l + 1))
                                if n >= 2:
                                    act.wait_ge(s["lr"], n - 1)
                                for hh in range(4):
                                    i = act.activation(Z[:, n % 2, hh, :], PS[:, hh, (t // 2) * S:(t // 2 + 1) * S], ACT.Identity,
                                                       bias=SV[:, t, 4 * hg + hh:4 * hg + hh + 1])
                                i.then_inc(s["z"], 1)

                            zs(NG * l)
                            zs(NG * l + 1)
                            for n in range(NG * l, NG * (l + 1)):
                                act.wait_ge(s["neg"], n + 1)
                                if n >= 2:
                                    act.wait_ge(s["pt"], n - 1)
                                for hh in range(4):
                                    i = act.activation(PR[:, n % 2, hh, :], E[:, n % 2, hh, :], ACT.Exp, bias=mx[:, n % 2, hh:hh + 1])
                                i.then_inc(s["p"], 1)
                                if n + 2 < NG * (l + 1):
                                    zs(n + 2)
                            for t in range(TT):
                                act.wait_ge(s["y_m"], TT * l + t + 1)
                                act.activation(YM[:, t, :], YM[:, t, :], ACT.Exp).then_inc(s["y_e"], 1)
                                act.activation(YR[:, t, :], YR[:, t, :], ACT.Relu).then_inc(s["y_e"], 1)
                            if l == 0:
                                split_scalar(act, s["hi1"], s["tr1"])

                    @block.vector
                    def _(v):
                        ln_vector(v, s)
                        for t in range(TT):
                            v.wait_ge(s["ln_norm"], t + 1)
                            v.tensor_scalar(BASE[:, t, :], HN[:, t, :], -1.0, 1.0, ALU.mult, ALU.add).then_inc(s["adj"], 1)
                        for t in range(TT):
                            v.wait_ge(s["adj"], t + 1)
                            v.tensor_scalar(BASE[:, t, :], BASE[:, t, :], -1.0e10, None, ALU.mult).then_inc(s["base"], 1)
                        v.tensor_copy(FT[:, :, :, GO:GO + 1], ones1[:, 0:32].rearrange("p (a b c) -> p a b c", a=TT, b=GH)).then_inc(s["one"], 1)
                        v.wait_ge(s["base"], TT)
                        v.wait_ge(s["one"], 1)
                        for l in range(2):
                            def scores(n):
                                hg, t = divmod(n % NG, TT)
                                b = n % 2
                                v.wait_ge(s["z"], n + 1)
                                if n >= 2:
                                    v.wait_ge(s["p"], n - 1)
                                v.scalar_tensor_tensor(E[:, b], Z[:, b], 0.2, Z[:, b], ALU.mult, ALU.max).then_inc(s["lr"], 1)
                                v.wait_ge(s["lr"], n + 1)
                                for hh in range(4):
                                    v.tensor_tensor_reduce(E[:, b, hh, :], E[:, b, hh, :], BASE[:, t, :], 1.0, -3.0e38,
                                                           ALU.add, ALU.max, mx[:, b, hh:hh + 1]).then_inc(s["e"], 1)
                                v.wait_ge(s["e"], 4 * (n + 1))
                                v.tensor_scalar(mx[:, b, :], mx[:, b, :], -1.0, None, ALU.mult).then_inc(s["neg"], 1)

                            def outputs(n):
                                hg, t = divmod(n % NG, TT)
                                b = n % 2
                                v.wait_ge(s["pv"], n + 1)
                                o = PS[:, 6 + b, 0:132].rearrange("p (h o) -> p h o", h=4)
                                v.reciprocal(rin[:, b, :], o[:, :, GO]).then_inc(s["o_r"], 1)
                                v.wait_ge(s["o_r"], n + 1)
                                v.tensor_tensor(O[:, t, 4 * hg:4 * hg + 4, :], o[:, :, 0:GO],
                                                rin[:, b, :].unsqueeze(2).broadcast_to([P, 4, GO]), ALU.mult).then_inc(s["o_c"], 1)

                            scores(NG * l)
                            for n in range(NG * l, NG * (l + 1)):
                                if n + 1 < NG * (l + 1):
                                    scores(n + 1)
                                v.wait_ge(s["pt"], n + 1)
                                if n >= 2:
                                    v.wait_ge(s["pv"], n - 1)
                                v.tensor_copy(PTS[:, n % 2].rearrange("p a b c d -> p (a b c d)"),
                                              PS[:, 4:6, :].rearrange("p a b -> p (a b)")).then_inc(s["pts"], 1)
                                if n > NG * l:
                                    outputs(n - 1)
                            outputs(NG * (l + 1) - 1)
                            for t in range(TT):
                                v.wait_ge(s["o_c"], NG * l + TT + t + 1)
                                if l:
                                    v.wait_ge(s["tr1"], 1)
                                v.tensor_tensor(YR[:, t, :], O[:, t].rearrange("p h o -> p (h o)"), const("gb%d" % l), ALU.add).then_inc(s["y_b"], 1)
                                v.wait_ge(s["y_b"], TT * l + t + 1)
                                v.tensor_scalar(YM[:, t, :], YR[:, t, :], 0.0, None, ALU.min).then_inc(s["y_m"], 1)
                            for t in range(TT):
                                v.wait_ge(s["y_e"], 2 * (TT * l + t + 1))
                                v.scalar_tensor_tensor(YM[:, t, :], YM[:, t, :], -1.0, YR[:, t, :], ALU.add, ALU.add).then_inc(s["h1"], 1)
                            if l == 0:
                                split_vector(v, s["hi1"], s["lo1"])
                        for t in range(TT):
                            v.wait_ge(s["h1"], TT + t + 1)
                            v.scalar_tensor_tensor(X[:, t, :], YM[:, t, :], gate[:, 0:1], X[:, t, :], ALU.mult, ALU.add).then_inc(s["y_b"], 1)

        def small_attention(layer):
            own = layer == 0
            with Phase() as ph:
                s = ph.sem(LN + "rms_sq rms_eps rms_rstd scaled qk q_ab q_sum qk_hi qk_lo vp v_c one km_hi km_lo "
                           "sc mxd sub ex pt pts pv rec o_c tr2 hi2 lo2 proj res")
                HX = ph.sb("HX", [P, TT, C])
                QKH = ph.sb("QKH", [P, 4, TOK], F32R)
                QKL = ph.sb("QKL", [P, 4, TOK], F32R)
                KMH = ph.sb("KMH", [P, NH, S], F32R)
                KML = ph.sb("KML", [P, NH, S], F32R)
                V = ph.sb("V", [P, TT, NH, HD + 1])
                E = ph.sb("E", [P, 2, 768])
                PTS = ph.sb("PTS", [P, 2, 2, 384])
                mx = ph.sb("mx", [P, 2, 4])
                rin = ph.sb("rin", [P, 2, 4])
                CTX = HX[:, :, :].rearrange("p t (h d) -> p t h d", h=NH)
                RA = E[:, :, :].rearrange("p a b -> p (a b)")[:, 0:2 * TOK].rearrange("p (a b) -> p a b", a=2)
                RB = PTS[:, :, :, :].rearrange("p a b c -> p (a b c)")[:, 0:2 * TOK].rearrange("p (a b) -> p a b", a=2)
                NG = 2 * NH // 2
                scale = HD ** -0.5
                mask = const("headmask")
                wo = "o0" if own else "o3"

                with nc.Block() as block:
                    @block.gpsimd
                    def _(g):
                        ln_gpsimd(g, s)
                        if own:
                            rms_gpsimd(g, s)
                        g.wait_ge(s["qk_hi"], 4)
                        for n in range(NG):
                            j, hp = divmod(n, NH // 2)
                            if j:
                                g.wait_ge(s["sc"], hp + 1)
                            for h in (2 * hp, 2 * hp + 1):
                                g.tensor_scalar(KMH[:, h, :], QKH[:, 2 + h // 8, j * S:(j + 1) * S].bitcast(F32),
                                                mask[:, h % 8:h % 8 + 1], 1.0, ALU.mult, ALU.mult).then_inc(s["km_hi"], 1)

                    @block.tensor
                    def _(pe):
                        transpose_tensor(pe, HX if own else HN, s["scaled"] if own else s["ln_norm"], s["tr_done"])
                        pe.wait_ge(s["tr_lo"], KC)
                        if own:
                            for i in range(4):
                                for r in range(2):
                                    lo = (i // 2) * 512 + r * 256 + (i % 2) * P
                                    for k in range(KC):
                                        m = mm3(pe, PS[:, 2 * i + r, :], weight("qk0", KC, k, lo, lo + P),
                                                pair(HH, HL, slice(None), k), k == 0, k == KC - 1)
                                m.then_inc(s["qk"], 1)
                        else:
                            for i in range(4):
                                for k in range(KC if i < 2 else 1):
                                    w = weight("q3", KC, k, i * P, i * P + P) if i < 2 else weight("k3", 1, 0, (i - 2) * P, (i - 1) * P)
                                    r = pair(HH, HL, slice(None), k) if i < 2 else (CTH[:, :], CTL[:, :])
                                    m = mm3(pe, PS[:, 2 * i, :], w, r, k == 0, k == (KC if i < 2 else 1) - 1)
                                m.then_inc(s["qk"], 1)
                        pe.wait_ge(s["qk_lo"], 1)
                        if own:
                            pe.wait_ge(s["q_ab"], 2)
                        for t in range(TT):
                            o = PS[:, t // 2, (t % 2) * C:(t % 2 + 1) * C]
                            if own:
                                for k in range(KC):
                                    m = mm3(pe, o, pair(HH, HL, slice(None), k, slice(t * P, t * P + P)), weight("v0", KC, k), k == 0, k == KC - 1)
                            else:
                                m = mm3(pe, o, (CTH[:, t * P:t * P + P], CTL[:, t * P:t * P + P]), weight("v3"))
                        m.then_inc(s["vp"], 1)
                        pe.wait_ge(s["qk_lo"], 4)
                        pe.wait_ge(s["v_c"], TT)

                        def scores(n):
                            j, hp = divmod(n, NH // 2)
                            b = n % 2
                            pe.wait_ge(s["km_hi"], 2 * (n + 1))
                            pe.wait_ge(s["km_lo"], 2 * (n + 1))
                            if n >= 2:
                                pe.wait_ge(s["sub"], 2 * (n - 1))
                            for hh in range(2):
                                h = 2 * hp + hh
                                for qt in (1, 0):
                                    nk = P * (qt + 1)
                                    q0 = j * S + qt * P
                                    o = PS[:, 2 * b, hh * S:hh * S + S] if qt else PS[:, 2 * b + 1, hh * P:hh * P + P]
                                    mm3(pe, o, pair(QKH, QKL, slice(None), h // 8, slice(q0, q0 + P)),
                                        pair(KMH, KML, slice(None), h, slice(0, nk)), True, False, skip=True)
                                    m = pe.matmul(o[:, nk - P:nk], identb[:, :], causalb[:, :], start=False, stop=True, skip_group_check=True)
                            m.then_inc(s["sc"], 1)

                        def values(n):
                            j, hp = divmod(n, NH // 2)
                            pe.wait_ge(s["pts"], n + 1)
                            if n >= 2:
                                pe.wait_ge(s["o_c"], n - 1)
                            for hh in range(2):
                                for qt in range(2):
                                    at = (2 * qt + hh) * (HD + 1)
                                    for kt in range(qt + 1):
                                        c = kt if qt else 2
                                        m = pe.matmul(PS[:, 6 + n % 2, at:at + HD + 1], PTS[:, n % 2, hh, c * P:c * P + P],
                                                      V[:, 2 * j + kt, 2 * hp + hh, :], start=(kt == 0), stop=(kt == qt))
                            m.then_inc(s["pv"], 1)

                        scores(0)
                        scores(1)
                        for n in range(NG):
                            pe.wait_ge(s["ex"], n + 1)
                            if n >= 1:
                                pe.wait_ge(s["pts"], n)
                            for hh in range(2):
                                for c, at in enumerate((hh * S, hh * S + P, 512 + hh * P)):
                                    m = pe.transpose(PS[:, 4 + hh, c * P:c * P + P], E[:, n % 2, at:at + P], ident)
                            m.then_inc(s["pt"], 1)
                            if n + 2 < NG:
                                scores(n + 2)
                            if n:
                                values(n - 1)
                        values(NG - 1)
                        pe.wait_ge(s["sub"], 2 * NG)
                        pe.wait_ge(s["o_c"], NG)
                        for t in range(TT):
                            for k in range(KC):
                                m = pe.transpose(PS[:, k, t * P:(t + 1) * P], CTX[:, t].rearrange("p h d -> p (h d)")[:, k * P:(k + 1) * P], ident)
                        m.then_inc(s["tr2"], 1)
                        pe.wait_ge(s["lo2"], KC)
                        for t in range(TT):
                            for k in range(KC):
                                m = mm3(pe, PS[:, 4 + t, 0:C], pair(HH, HL, slice(None), k, slice(t * P, t * P + P)), weight(wo, KC, k), k == 0, k == KC - 1)
                            m.then_inc(s["proj"], 1)

                    @block.scalar
                    def _(act):
                        if own:
                            rms_scalar(act, s, HN, s["ln_norm"], RA[:, 0, 0:C])
                            split_scalar(act, s["tr_hi"], s["tr_done"], scale=const("ln1"))
                        else:
                            split_scalar(act, s["tr_hi"], s["tr_done"])
                        for i in range(4):
                            if own:
                                act.wait_ge(s["q_sum"], i + 1)
                                act.activation(QKH[:, i, :], RA[:, i % 2, :], ACT.Copy).then_inc(s["qk_hi"], 1)
                            else:
                                act.wait_ge(s["qk"], i + 1)
                                act.activation(QKH[:, i, :], PS[:, 2 * i, :], ACT.Copy).then_inc(s["qk_hi"], 1)

                        def exps(n):
                            act.wait_ge(s["sub"], 2 * (n + 1))
                            act.activation(E[:, n % 2, :], E[:, n % 2, :], ACT.Exp, scale=scale).then_inc(s["ex"], 1)

                        exps(0)
                        for n in range(NG):
                            if n + 1 < NG:
                                exps(n + 1)
                            act.wait_ge(s["pt"], n + 1)
                            if n >= 2:
                                act.wait_ge(s["pv"], n - 1)
                            act.activation(PTS[:, n % 2], PS[:, 4:6, 0:384], ACT.Copy).then_inc(s["pts"], 1)
                        split_scalar(act, s["hi2"], s["tr2"])

                    @block.vector
                    def _(v):
                        ln_vector(v, s)
                        if own:
                            v.wait_ge(s["rms_rstd"], 1)
                            for t in range(TT):
                                v.tensor_scalar(HX[:, t, :], HN[:, t, :], rstd[:, t:t + 1], None, ALU.mult).then_inc(s["scaled"], 1)
                            split_vector(v, s["tr_hi"], s["tr_lo"], scale=const("ln1"))
                        else:
                            split_vector(v, s["tr_hi"], s["tr_lo"])
                        v.tensor_copy(V[:, :, :, HD:HD + 1], ones1[:, 0:64].rearrange("p (a b c) -> p a b c", a=TT, b=NH)).then_inc(s["one"], 1)
                        def low(i):
                            v.wait_ge(s["qk_hi"], i + 1)
                            src = RA[:, i % 2, :] if own else PS[:, 2 * i, :]
                            v.tensor_tensor(QKL[:, i, :], src, QKH[:, i, :].bitcast(F32), ALU.subtract).then_inc(s["qk_lo"], 1)

                        for i in range(4):
                            if own:
                                b = i % 2
                                v.wait_ge(s["qk"], i + 1)
                                if i >= 2:
                                    v.wait_ge(s["qk_lo"], i - 1)
                                for r, (dst, tab) in enumerate(((RA, "ropec"), (RB, "ropes"))):
                                    c = 4 * (i // 2) + 2 * r + i % 2
                                    v.scalar_tensor_tensor(dst[:, b, :].rearrange("p (j q) -> p j q", j=2),
                                                           PS[:, 2 * i + r, :].rearrange("p (j q) -> p j q", j=2),
                                                           const("qkb")[:, c:c + 1],
                                                           const(tab).unsqueeze(1).broadcast_to([P, 2, S]), ALU.add, ALU.mult).then_inc(s["q_ab"], 1)
                                v.wait_ge(s["q_ab"], 2 * (i + 1))
                                v.tensor_tensor(RA[:, b, :], RA[:, b, :], RB[:, b, :], ALU.add).then_inc(s["q_sum"], 1)
                            if i:
                                low(i - 1)
                        low(3)
                        v.wait_ge(s["vp"], 1)
                        for t in range(TT):
                            src = PS[:, t // 2, (t % 2) * C:(t % 2 + 1) * C].rearrange("p (h d) -> p h d", h=NH)
                            if own:
                                v.tensor_tensor(V[:, t, :, 0:HD], src, const("bv0").rearrange("p (h d) -> p h d", h=NH), ALU.add).then_inc(s["v_c"], 1)
                            else:
                                v.tensor_copy(V[:, t, :, 0:HD], src).then_inc(s["v_c"], 1)

                        def masks(n):
                            j, hp = divmod(n, NH // 2)
                            if j:
                                v.wait_ge(s["sc"], hp + 1)
                            else:
                                v.wait_ge(s["qk_lo"], 4)
                            for h in (2 * hp, 2 * hp + 1):
                                v.tensor_scalar(KML[:, h, :], QKL[:, 2 + h // 8, j * S:(j + 1) * S].bitcast(F32),
                                                mask[:, h % 8:h % 8 + 1], None, ALU.mult).then_inc(s["km_lo"], 1)

                        def shift(n):
                            b = n % 2
                            v.wait_ge(s["sc"], n + 1)
                            q1 = PS[:, 2 * b, :].rearrange("p (h k) -> p h k", h=2)
                            q0 = PS[:, 2 * b + 1, 0:256].rearrange("p (h k) -> p h k", h=2)
                            v.tensor_reduce(mx[:, b, 0:2], q1, AX.X, ALU.max).then_inc(s["mxd"], 1)
                            v.tensor_reduce(mx[:, b, 2:4], q0, AX.X, ALU.max).then_inc(s["mxd"], 1)
                            if n >= 2:
                                v.wait_ge(s["pt"], n - 1)
                            v.wait_ge(s["mxd"], 2 * n + 1)
                            v.tensor_tensor(E[:, b, 0:512].rearrange("p (h k) -> p h k", h=2), q1,
                                            mx[:, b, 0:2].unsqueeze(2).broadcast_to([P, 2, S]), ALU.subtract).then_inc(s["sub"], 1)
                            v.wait_ge(s["mxd"], 2 * n + 2)
                            v.tensor_tensor(E[:, b, 512:768].rearrange("p (h k) -> p h k", h=2), q0,
                                            mx[:, b, 2:4].unsqueeze(2).broadcast_to([P, 2, P]), ALU.subtract).then_inc(s["sub"], 1)

                        def outputs(n):
                            j, hp = divmod(n, NH // 2)
                            b = n % 2
                            v.wait_ge(s["pv"], n + 1)
                            o = PS[:, 6 + b, 0:4 * (HD + 1)].rearrange("p (a d) -> p a d", a=4)
                            v.reciprocal(rin[:, b, :], o[:, :, HD]).then_inc(s["rec"], 1)
                            v.wait_ge(s["rec"], n + 1)
                            v.tensor_tensor(CTX[:, 2 * j:2 * j + 2, 2 * hp:2 * hp + 2, :],
                                            o[:, :, 0:HD].rearrange("p (q h) d -> p q h d", q=2),
                                            rin[:, b, :].rearrange("p (q h) -> p q h", q=2).unsqueeze(3).broadcast_to([P, 2, 2, HD]),
                                            ALU.mult).then_inc(s["o_c"], 1)

                        for n in range(4):
                            masks(n)
                        shift(0)
                        for n in range(NG):
                            if n + 1 < NG:
                                shift(n + 1)
                            if n >= 2:
                                outputs(n - 2)
                            if n + 4 < NG:
                                masks(n + 4)
                        outputs(NG - 2)
                        outputs(NG - 1)
                        split_vector(v, s["hi2"], s["lo2"])
                        for t in range(TT):
                            v.wait_ge(s["proj"], t + 1)
                            if own:
                                v.tensor_tensor(XN[:, t, :], PS[:, 4 + t, 0:C], HN[:, t, :], ALU.add).then_inc(s["res"], 1)
                            else:
                                v.scalar_tensor_tensor(X[:, t, :], PS[:, 4 + t, 0:C], gate[:, 6:7], X[:, t, :], ALU.mult, ALU.add).then_inc(s["res"], 1)

        def experts(layer):
            tiles = {0: T0, 2: T2, 3: T3}[layer]
            glu = layer != 2
            src = {0: "moe0", 2: "ffn2", 3: "moe3"}[layer]
            WC = 896 if glu else 640
            UP, DOWN, SEL = (256, 512, 768) if glu else (0, 256, 512)
            RAW, RING, LAG = 3, 4, 2
            with Phase() as ph:
                w_in = ph.sems("w_in", RAW)
                s = ph.sem(LN + "rms_sq rms_eps rms_rstd scaled lg smx ssub sexp ssum rank g_z g_set g_ok gtr g_hi g_lo "
                           "w_hi w_lo gu silu au ag a_hi a_lo dn y_t y_x")
                HX = ph.sb("HX", [P, TT, C])
                junk = ph.sb("junk", [P, C])
                raw = ph.sb("raw", [P, RAW, WC])
                WMH = ph.sb("WMH", [P, RING, WC], F32R)
                WML = ph.sb("WML", [P, RING, SEL], F32R)
                LG = ph.sb("LG", [P, TT, 16])
                RK = ph.sb("RK", [P, 3, TT, NE, NE])
                G = ph.sb("G", [P, TT, 16])
                sm = ph.sb("sm", [P, 3, TT])
                GS = ph.sb("GS", [P, TOK], F32R)
                SG = ph.sb("SG", [P, 2, TOK])
                A = ph.sb("A", [P, 2, TOK])
                AHI = ph.sb("AHI", [P, 3, TOK], F32R)
                ALO = ph.sb("ALO", [P, 3, TOK], F32R)
                YT = HX
                NL = 16 if layer == 0 else 8

                with nc.Block() as block:
                    @block.sync
                    def _(sp):
                        for i in range(tiles):
                            if i >= RAW:
                                sp.wait_ge(s["w_hi"], i - RAW + 1)
                                sp.wait_ge(s["w_lo"], i - RAW + 1)
                            sp.dma_start(raw[:, i % RAW, :], a[src][i][:, 0:WC]).then_inc(w_in[i % RAW], 16)

                    @block.gpsimd
                    def _(g):
                        if layer == 0:
                            rms_gpsimd(g, s)
                        else:
                            ln_gpsimd(g, s)
                        for i in range(tiles):
                            g.wait_ge(s["w_hi"], i + 1)
                            if i >= RING:
                                g.wait_ge(s["dn"], i - RING + 1)
                            g.tensor_tensor(WML[:, i % RING, :], raw[:, i % RAW, 0:SEL], WMH[:, i % RING, 0:SEL].bitcast(F32),
                                            ALU.subtract).then_inc(s["w_lo"], 1)

                    @block.tensor
                    def _(pe):
                        transpose_tensor(pe, HX if layer == 0 else HN, s["scaled"] if layer == 0 else s["ln_norm"], s["tr_done"])
                        pe.wait_ge(s["tr_lo"], KC)
                        if glu:
                            for t in range(TT):
                                for k in range(KC):
                                    m = mm3(pe, PS[:, 7, t * 16:t * 16 + NL], pair(HH, HL, slice(None), k, slice(t * P, t * P + P)),
                                            weight("rt%d" % layer, KC, k), k == 0, k == KC - 1)
                            m.then_inc(s["lg"], 1)

                        def gates():
                            pe.wait_ge(s["g_ok"], 1)
                            for t in range(TT):
                                m = pe.transpose(PS[0:16, 6, t * P:t * P + P], G[:, t, :], ident)
                            m.then_inc(s["gtr"], 1)
                            pe.wait_ge(s["g_lo"], 1)

                        def hidden(i):
                            b, w = i % 2, i % RING
                            pe.wait_ge(s["w_hi"], i + 1)
                            pe.wait_ge(s["w_lo"], i + 1)
                            if i >= 2:
                                pe.wait_ge(s["ag"], i - 1)
                            for k in range(KC):
                                m = mm3(pe, PS[:, b, :], pair(WMH, WML, slice(None), w, slice(k * P, k * P + P)),
                                        pair(HH, HL, slice(None), k), k == 0, k == KC - 1)
                            if glu:
                                for k in range(KC):
                                    mm3(pe, PS[:, 2 + b, :], pair(WMH, WML, slice(None), w, slice(UP + k * P, UP + k * P + P)),
                                        pair(HH, HL, slice(None), k), k == 0, k == KC - 1)
                                if i == 0:
                                    gates()
                                m = pe.matmul(PS[:, 4 + b, :], WMH[:, w, SEL:SEL + P], GS[:, :], start=True, stop=True)
                            m.then_inc(s["gu"], 1)

                        def down(i):
                            pe.wait_ge(s["a_lo"], i + 1)
                            for t in range(TT):
                                m = mm3(pe, PS[:, 6 + t // 2, (t % 2) * C:(t % 2 + 1) * C], pair(AHI, ALO, slice(None), i % 3, slice(t * P, t * P + P)),
                                        pair(WMH, WML, slice(None), i % RING, slice(DOWN, DOWN + C)), i == 0 and t % 2 == 0, i == tiles - 1, skip=True)
                            m.then_inc(s["dn"], 1)

                        for i in range(tiles + LAG):
                            if i < tiles:
                                hidden(i)
                            if i >= LAG:
                                down(i - LAG)

                    @block.scalar
                    def _(act):
                        def weights(i):
                            act.wait_ge(w_in[i % RAW], 16 * (i // RAW + 1))
                            if i >= RING:
                                act.wait_ge(s["dn"], i - RING + 1)
                            act.activation(WMH[:, i % RING, :], raw[:, i % RAW, :], ACT.Copy).then_inc(s["w_hi"], 1)

                        if layer == 0:
                            rms_scalar(act, s, XN, s["g_z"], junk)
                            split_scalar(act, s["tr_hi"], s["tr_done"], scale=const("ln2"))
                        else:
                            split_scalar(act, s["tr_hi"], s["tr_done"])
                        weights(0)
                        weights(1)
                        if layer == 0:
                            act.wait_ge(s["ssub"], 1)
                            act.activation(LG[:, :, 0:8], LG[:, :, 0:8], ACT.Exp).then_inc(s["sexp"], 1)
                            act.activation(LG[:, :, 8:9], LG[:, :, 8:9], ACT.Exp, scale=-1.0).then_inc(s["sexp"], 1)
                        elif layer == 3:
                            act.wait_ge(s["lg"], 1)
                            act.activation(LG[:, :, 0:8], PS[:, 7, 0:64].rearrange("p (t e) -> p t e", t=TT)[:, :, 0:8],
                                           ACT.Exp, scale=-1.0).then_inc(s["sexp"], 1)
                        if glu:
                            act.wait_ge(s["gtr"], 1)
                            act.wait_ge(s["g_z"], 1 + TT)
                            act.activation(GS[0:16, :], PS[0:16, 6, :], ACT.Copy).then_inc(s["g_hi"], 1)
                        for i in range(tiles):
                            b = i % 2
                            act.wait_ge(s["gu"], i + 1)
                            if glu:
                                if i >= 2:
                                    act.wait_ge(s["au"], i - 1)
                                act.activation(SG[:, b, :], PS[:, b, :], ACT.Silu).then_inc(s["silu"], 1)
                            else:
                                if i >= 2:
                                    act.wait_ge(s["a_lo"], i - 1)
                                act.activation(A[:, b, :], PS[:, b, :], ACT.Gelu, bias=const("b1f")[:, i:i + 1]).then_inc(s["ag"], 1)
                            if i + 2 < tiles:
                                weights(i + 2)
                            act.wait_ge(s["ag"], i + 1)
                            if i >= 3:
                                act.wait_ge(s["dn"], i - 2)
                            act.activation(AHI[:, i % 3, :], A[:, b, :], ACT.Copy).then_inc(s["a_hi"], 1)

                    @block.vector
                    def _(v):
                        v.memset(GS[:, :].bitcast(F32), 0.0).then_inc(s["g_z"], 1)
                        for t in range(TT):
                            v.memset(G[:, t, :], 0.0).then_inc(s["g_z"], 1)
                        if layer == 0:
                            v.wait_ge(s["rms_rstd"], 1)
                            for t in range(TT):
                                v.tensor_scalar(HX[:, t, :], XN[:, t, :], rstd[:, t:t + 1], None, ALU.mult).then_inc(s["scaled"], 1)
                            split_vector(v, s["tr_hi"], s["tr_lo"], scale=const("ln2"))
                        else:
                            ln_vector(v, s)
                            split_vector(v, s["tr_hi"], s["tr_lo"])
                        lgp = PS[:, 7, 0:64].rearrange("p (t e) -> p t e", t=TT)

                        def wide(x):
                            return x.unsqueeze(2).broadcast_to([P, TT, NE])

                        if layer == 0:
                            v.wait_ge(s["lg"], 1)
                            v.tensor_reduce(sm[:, 0, :], lgp[:, :, 0:8], AX.X, ALU.max).then_inc(s["smx"], 1)
                            v.tensor_copy(LG[:, :, 8:9], lgp[:, :, 8:9]).then_inc(s["smx"], 1)
                            v.wait_ge(s["smx"], 2)
                            v.tensor_tensor(LG[:, :, 0:8], lgp[:, :, 0:8], wide(sm[:, 0, :]), ALU.subtract).then_inc(s["ssub"], 1)
                            v.wait_ge(s["sexp"], 2)
                            v.tensor_reduce(sm[:, 1, :], LG[:, :, 0:8], AX.X, ALU.add).then_inc(s["ssum"], 1)
                            v.tensor_scalar(LG[:, :, 8:9], LG[:, :, 8:9], 1.0, None, ALU.add).then_inc(s["ssum"], 1)
                            v.wait_ge(s["ssum"], 2)
                            v.reciprocal(sm[:, 2, :], sm[:, 1, :]).then_inc(s["ssum"], 1)
                            v.wait_ge(s["ssum"], 3)
                            v.wait_ge(s["g_z"], 1 + TT)
                            v.reciprocal(G[:, :, 8:9], LG[:, :, 8:9]).then_inc(s["g_set"], 1)
                            v.tensor_tensor(LG[:, :, 0:8], LG[:, :, 0:8], wide(sm[:, 2, :]), ALU.mult).then_inc(s["ssum"], 1)
                            v.wait_ge(s["ssum"], 4)
                            rank, n = rank_vector(v, s, RK, LG[:, :, 0:8], 0)
                            v.scalar_tensor_tensor(G[:, :, 0:8], rank, 2.0, LG[:, :, 0:8], ALU.is_lt, ALU.mult).then_inc(s["g_set"], 1)
                            v.wait_ge(s["g_set"], 2)
                            v.tensor_copy(G[:, :, 15:16], G[:, :, 14:15]).then_inc(s["g_ok"], 1)
                        elif layer == 3:
                            v.wait_ge(s["sexp"], 1)
                            v.tensor_scalar(LG[:, :, 0:8], LG[:, :, 0:8], 1.0, None, ALU.add).then_inc(s["ssum"], 1)
                            v.wait_ge(s["ssum"], 1)
                            v.reciprocal(LG[:, :, 0:8], LG[:, :, 0:8]).then_inc(s["ssum"], 1)
                            v.wait_ge(s["ssum"], 2)
                            v.tensor_tensor(LG[:, :, 8:16], LG[:, :, 0:8], const("gbias3").unsqueeze(1).broadcast_to([P, TT, NE]), ALU.add).then_inc(s["ssum"], 1)
                            v.wait_ge(s["ssum"], 3)
                            rank, n = rank_vector(v, s, RK, LG[:, :, 8:16], 0)
                            v.scalar_tensor_tensor(LG[:, :, 0:8], rank, 2.0, LG[:, :, 0:8], ALU.is_lt, ALU.mult).then_inc(s["ssum"], 1)
                            v.wait_ge(s["ssum"], 4)
                            v.tensor_reduce(sm[:, 0, :], LG[:, :, 0:8], AX.X, ALU.add).then_inc(s["ssum"], 1)
                            v.wait_ge(s["ssum"], 5)
                            v.reciprocal(sm[:, 1, :], sm[:, 0, :]).then_inc(s["ssum"], 1)
                            v.wait_ge(s["ssum"], 6)
                            v.wait_ge(s["g_z"], 1 + TT)
                            v.tensor_tensor(G[:, :, 0:8], LG[:, :, 0:8], wide(sm[:, 1, :]), ALU.mult).then_inc(s["g_set"], 1)
                            v.tensor_copy(G[:, :, 8:9], ones1[:, 0:TT].unsqueeze(2)).then_inc(s["g_set"], 1)
                            v.wait_ge(s["g_set"], 2)
                            v.tensor_copy(G[:, :, 15:16], G[:, :, 14:15]).then_inc(s["g_ok"], 1)
                        if glu:
                            v.wait_ge(s["g_hi"], 1)
                            v.tensor_tensor(GS[32:48, :], PS[0:16, 6, :], GS[0:16, :].bitcast(F32), ALU.subtract).then_inc(s["g_lo"], 1)
                        for i in range(tiles):
                            b = i % 2
                            if glu:
                                v.wait_ge(s["silu"], i + 1)
                                v.tensor_tensor(SG[:, b, :], SG[:, b, :], PS[:, 2 + b, :], ALU.mult).then_inc(s["au"], 1)
                                if i >= 2:
                                    v.wait_ge(s["a_lo"], i - 1)
                                v.wait_ge(s["au"], i + 1)
                                v.tensor_tensor(A[:, b, :], SG[:, b, :], PS[:, 4 + b, :], ALU.mult).then_inc(s["ag"], 1)
                            v.wait_ge(s["a_hi"], i + 1)
                            if i >= 3:
                                v.wait_ge(s["dn"], i - 2)
                            v.tensor_tensor(ALO[:, i % 3, :], A[:, b, :], AHI[:, i % 3, :].bitcast(F32), ALU.subtract).then_inc(s["a_lo"], 1)
                        v.wait_ge(s["dn"], tiles)
                        for t in range(TT):
                            y = PS[:, 6 + t // 2, (t % 2) * C:(t % 2 + 1) * C]
                            if layer == 3:
                                v.scalar_tensor_tensor(X[:, t, :], y, gate[:, 7:8], X[:, t, :], ALU.mult, ALU.add).then_inc(s["y_x"], 1)
                            else:
                                v.tensor_tensor(YT[:, t, :], y, XN[:, t, :] if layer == 0 else const("b2f"), ALU.add).then_inc(s["y_t"], 1)
                                v.wait_ge(s["y_t"], t + 1)
                                g = gate[:, 1:2] if layer == 0 else COEF2[:, t:t + 1]
                                v.scalar_tensor_tensor(X[:, t, :], YT[:, t, :], g, X[:, t, :], ALU.mult, ALU.add).then_inc(s["y_x"], 1)

        def latent_attention(pi):
            with Phase() as ph:
                s = ph.sem(LN + "kv_in kv_ab kv_r kv2 kvt kb_hi kb_lo qp q_hi q_lo sc mxd sub ex pt pts pv rec o_c ct c_hi c_lo proj res")
                KV = ph.sb("KV", [P, TT, DC])
                KA = ph.sb("KA", [P, TT, DC])
                KB = ph.sb("KB", [P, TT, DC])
                KV2 = ph.sb("KV2", [P, TT, 2 * DC + 2])
                KBH = ph.sb("KBH", [P, 2, TOK], F32R)
                KBL = ph.sb("KBL", [P, 2, TOK], F32R)
                QH = ph.sb("QH", [P, 8, TOK], F32R)
                QL = ph.sb("QL", [P, 8, TOK], F32R)
                E = [XN[:, :, :].rearrange("p t c -> p (t c)"), HN[:, :, :].rearrange("p t c -> p (t c)")]
                PTS = ph.sb("PTS", [P, 2, 1024])
                mx = ph.sb("mx", [P, 2, 4])
                rin = ph.sb("rin", [P, 2, 4])
                CTX = ph.sb("CTX", [P, TT, MH, DC])
                MT = MH // 2
                NG = 2 * MT

                with nc.Block() as block:
                    @block.sync
                    def _(sp):
                        sp.dma_start(KV[:, :, :], a["ctx"][bass.ts(pi, TOK), :].rearrange("(t p) d -> p t d", p=P)).then_inc(s["kv_in"], 16)

                    @block.gpsimd
                    def _(g):
                        ln_gpsimd(g, s)

                    @block.tensor
                    def _(pe):
                        transpose_tensor(pe, KV2, s["kv2"], s["kvt"], bank=2, tiles=1)
                        transpose_tensor(pe, HN, s["ln_norm"], s["tr_done"])
                        pe.wait_ge(s["tr_lo"], KC)
                        pe.wait_ge(s["kb_lo"], 2)
                        for m in range(MT):
                            for k in range(KC):
                                i = mm3(pe, PS[:, m, :], pair(AH, AL, slice(None), k, slice(m * P, m * P + P)),
                                        pair(HH, HL, slice(None), k), k == 0, k == KC - 1)
                            i.then_inc(s["qp"], 1)

                        def scores(n):
                            j, m = divmod(n, MT)
                            b = n % 2
                            pe.wait_ge(s["q_lo"], m + 1 if j == 0 and n >= 2 else 4 if j == 0 else MT)
                            if n >= 2:
                                pe.wait_ge(s["sub"], n - 1)
                            for qt in range(2):
                                for hh in range(2):
                                    q0 = j * S + qt * P
                                    i = mm3(pe, PS[:, 2 * b + qt, hh * S:hh * S + S], pair(QH, QL, slice(None), m, slice(q0, q0 + P)),
                                            pair(KBH, KBL, slice(None), hh, slice(j * S, j * S + S)))
                            i.then_inc(s["sc"], 1)

                        def values(n):
                            j, m = divmod(n, MT)
                            pe.wait_ge(s["pts"], n + 1)
                            if n >= 2:
                                pe.wait_ge(s["o_c"], n - 1)
                            for qt in range(2):
                                for hh in range(2):
                                    at = (2 * qt + hh) * (DC + 1)
                                    for kt in range(2):
                                        c = qt * 512 + hh * S + kt * P
                                        i = pe.matmul(PS[:, 6 + n % 2, at:at + DC + 1], PTS[:, n % 2, c:c + P],
                                                      KV2[:, 2 * j + kt, DC:2 * DC + 1], start=(kt == 0), stop=(kt == 1))
                            i.then_inc(s["pv"], 1)

                        scores(0)
                        scores(1)
                        pe.wait_ge(s["q_lo"], MT)
                        for n in range(NG):
                            pe.wait_ge(s["ex"], n + 1)
                            if n >= 1:
                                pe.wait_ge(s["pts"], n)
                            for qt in range(2):
                                for c in range(4):
                                    i = pe.transpose(PS[:, 4 + qt, c * P:c * P + P], E[n % 2][:, qt * 512 + c * P:qt * 512 + c * P + P], ident)
                            i.then_inc(s["pt"], 1)
                            if n + 2 < NG:
                                scores(n + 2)
                            if n:
                                values(n - 1)
                        values(NG - 1)
                        pe.wait_ge(s["sub"], NG)
                        pe.wait_ge(s["o_c"], NG)
                        for m in range(MT):
                            if m >= 4:
                                pe.wait_ge(s["c_lo"], m - 3)
                            for t in range(TT):
                                i = pe.transpose(PS[:, m % 4, t * P:t * P + P], CTX[:, t].rearrange("p h d -> p (h d)")[:, m * P:m * P + P], ident)
                            i.then_inc(s["ct"], 1)
                        pe.wait_ge(s["c_lo"], MT)
                        for t in range(TT):
                            for m in range(MT):
                                i = mm3(pe, PS[:, 4 + t, 0:C], pair(QH, QL, slice(None), m, slice(t * P, t * P + P)),
                                        pair(BH, BL, slice(None), m), m == 0, m == MT - 1)
                            i.then_inc(s["proj"], 1)

                    @block.scalar
                    def _(act):
                        act.wait_ge(s["kvt"], 1)
                        for r in range(2):
                            act.activation(KBH[:, r, :], PS[:, 2, :], ACT.Copy, scale=const("halfmask")[:, r:r + 1]).then_inc(s["kb_hi"], 1)
                        split_scalar(act, s["tr_hi"], s["tr_done"])
                        for m in range(MT):
                            act.wait_ge(s["qp"], m + 1)
                            act.activation(QH[:, m, :], PS[:, m, :], ACT.Copy).then_inc(s["q_hi"], 1)

                        def exps(n):
                            act.wait_ge(s["sub"], n + 1)
                            act.activation(E[n % 2], E[n % 2], ACT.Exp).then_inc(s["ex"], 1)

                        exps(0)
                        for n in range(NG):
                            if n + 1 < NG:
                                exps(n + 1)
                            act.wait_ge(s["pt"], n + 1)
                            if n >= 2:
                                act.wait_ge(s["pv"], n - 1)
                            act.activation(PTS[:, n % 2, :], PS[:, 4:6, :].rearrange("p a b -> p (a b)"), ACT.Copy).then_inc(s["pts"], 1)
                        for m in range(MT):
                            act.wait_ge(s["ct"], m + 1)
                            act.activation(QH[:, m, :], PS[:, m % 4, :], ACT.Copy).then_inc(s["c_hi"], 1)

                    @block.vector
                    def _(v):
                        v.wait_ge(s["kv_in"], 16)
                        H = DC // 2
                        for j in range(2):
                            kv = KV[:, 2 * j:2 * j + 2, :]
                            cos = const("kvc").rearrange("p (q d) -> p q d", q=2)
                            sin = const("kvs").rearrange("p (q d) -> p q d", q=2)
                            v.tensor_tensor(KA[:, 2 * j:2 * j + 2, :], kv, cos, ALU.mult).then_inc(s["kv_ab"], 1)
                            v.tensor_tensor(KB[:, 2 * j:2 * j + 2, 0:H], kv[:, :, H:DC], sin[:, :, 0:H], ALU.mult).then_inc(s["kv_ab"], 1)
                            v.tensor_tensor(KB[:, 2 * j:2 * j + 2, H:DC], kv[:, :, 0:H], sin[:, :, H:DC], ALU.mult).then_inc(s["kv_ab"], 1)
                        v.tensor_copy(KV2[:, :, 2 * DC:2 * DC + 1], ones1[:, 0:TT].unsqueeze(2)).then_inc(s["kv_r"], 1)
                        v.wait_ge(s["kv_ab"], 6)
                        v.tensor_tensor(KV2[:, :, 0:DC], KA[:, :, :], KB[:, :, :], ALU.add).then_inc(s["kv_r"], 1)
                        v.tensor_tensor(KV2[:, :, DC:2 * DC], KA[:, :, :], KB[:, :, :], ALU.add).then_inc(s["kv_r"], 1)
                        v.wait_ge(s["kv_r"], 3)
                        v.nop().then_inc(s["kv2"], TT)
                        ln_vector(v, s)
                        for r in range(2):
                            v.wait_ge(s["kb_hi"], r + 1)
                            if r == 0:
                                v.wait_ge(s["kb_hi"], 2)
                            v.scalar_tensor_tensor(KBL[:, r, :], PS[:, 2, :], const("halfmask")[:, r:r + 1], KBH[:, r, :].bitcast(F32),
                                                   ALU.mult, ALU.subtract).then_inc(s["kb_lo"], 1)
                        split_vector(v, s["tr_hi"], s["tr_lo"])
                        for m in range(MT):
                            v.wait_ge(s["q_hi"], m + 1)
                            v.tensor_tensor(QL[:, m, :], PS[:, m, :], QH[:, m, :].bitcast(F32), ALU.subtract).then_inc(s["q_lo"], 1)

                        def shift(n):
                            b = n % 2
                            v.wait_ge(s["sc"], n + 1)
                            sc = PS[:, 2 * b:2 * b + 2, :].rearrange("p a (h k) -> p (a h) k", h=2)
                            v.tensor_reduce(mx[:, b, :], sc, AX.X, ALU.max).then_inc(s["mxd"], 1)
                            if n >= 2:
                                v.wait_ge(s["pt"], n - 1)
                            v.wait_ge(s["mxd"], n + 1)
                            v.tensor_tensor(E[b].rearrange("p (a k) -> p a k", a=4), sc,
                                            mx[:, b, :].unsqueeze(2).broadcast_to([P, 4, S]), ALU.subtract).then_inc(s["sub"], 1)

                        def outputs(n):
                            j, m = divmod(n, MT)
                            b = n % 2
                            v.wait_ge(s["pv"], n + 1)
                            o = PS[:, 6 + b, 0:4 * (DC + 1)].rearrange("p (a d) -> p a d", a=4)
                            v.reciprocal(rin[:, b, :], o[:, :, DC]).then_inc(s["rec"], 1)
                            v.wait_ge(s["rec"], n + 1)
                            v.tensor_tensor(CTX[:, 2 * j:2 * j + 2, 2 * m:2 * m + 2, :],
                                            o[:, :, 0:DC].rearrange("p (q h) d -> p q h d", q=2),
                                            rin[:, b, :].rearrange("p (q h) -> p q h", q=2).unsqueeze(3).broadcast_to([P, 2, 2, DC]),
                                            ALU.mult).then_inc(s["o_c"], 1)

                        shift(0)
                        for n in range(NG):
                            if n + 1 < NG:
                                shift(n + 1)
                            if n >= 2:
                                outputs(n - 2)
                        outputs(NG - 2)
                        outputs(NG - 1)
                        for m in range(MT):
                            v.wait_ge(s["c_hi"], m + 1)
                            v.tensor_tensor(QL[:, m, :], PS[:, m % 4, :], QH[:, m, :].bitcast(F32), ALU.subtract).then_inc(s["c_lo"], 1)
                        for t in range(TT):
                            v.wait_ge(s["proj"], t + 1)
                            v.scalar_tensor_tensor(X[:, t, :], PS[:, 4 + t, 0:C], gate[:, 2:3], X[:, t, :], ALU.mult, ALU.add).then_inc(s["res"], 1)

        def low_rank():
            with Phase() as ph:
                s = ph.sem(LN + "pr ex la lr lb top mr ne sp su rs ga mz mt m_hi m_lo lo_ res")
                L = ph.sb("L", [P, TT, 32])
                LB = ph.sb("LB", [P, TT, LR])
                LM = ph.sb("LM", [P, TT, LR])
                top = ph.sb("top", [P, TT, 8])
                sm = ph.sb("sm", [P, 2, TT])
                M = ph.sb("M", [P, TT, P])
                MHI = ph.sb("MHI", [P, 1, TOK], F32R)
                MLO = ph.sb("MLO", [P, 1, TOK], F32R)
                with nc.Block() as block:
                    @block.gpsimd
                    def _(g):
                        ln_gpsimd(g, s)
                        g.memset(M[:, :, LR:P], 0.0).then_inc(s["mz"], 1)

                    @block.tensor
                    def _(pe):
                        transpose_tensor(pe, HN, s["ln_norm"], s["tr_done"])
                        pe.wait_ge(s["tr_lo"], KC)
                        for t in range(TT):
                            for k in range(KC):
                                m = mm3(pe, PS[:, 4 + t, 0:352], pair(HH, HL, slice(None), k, slice(t * P, t * P + P)),
                                        weight("l1f", KC, k), k == 0, k == KC - 1)
                            m.then_inc(s["pr"], 1)
                        pe.wait_ge(s["mz"], 1)
                        transpose_tensor(pe, M, s["ga"], s["mt"], bank=2, tiles=1)
                        pe.wait_ge(s["m_lo"], 1)
                        for t in range(TT):
                            mm3(pe, PS[:, t % 2, (t // 2) * C:(t // 2 + 1) * C], (MHI[:, 0, t * P:t * P + P], MLO[:, 0, t * P:t * P + P]),
                                weight("l1b")).then_inc(s["lo_"], 1)

                    @block.scalar
                    def _(act):
                        split_scalar(act, s["tr_hi"], s["tr_done"])
                        for t in range(TT):
                            act.wait_ge(s["pr"], t + 1)
                            act.activation(L[:, t, :], PS[:, 4 + t, 320:352], ACT.Exp, scale=-1.0).then_inc(s["ex"], 1)
                        split_scalar(act, s["m_hi"], s["mt"], bank=2, hh=MHI, tiles=1)

                    @block.vector
                    def _(v):
                        ln_vector(v, s)
                        split_vector(v, s["tr_hi"], s["tr_lo"])
                        v.wait_ge(s["ex"], TT)
                        v.tensor_scalar(L[:, :, :], L[:, :, :], 1.0, None, ALU.add).then_inc(s["la"], 1)
                        v.wait_ge(s["la"], 1)
                        v.reciprocal(L[:, :, :], L[:, :, :]).then_inc(s["lr"], 1)
                        v.wait_ge(s["lr"], 1)
                        for t in range(TT):
                            v.tensor_tensor(LB[:, t, :].rearrange("p (a b) -> p a b", b=2), L[:, t, :].unsqueeze(2).broadcast_to([P, 32, 2]),
                                            const("lora_b").rearrange("p (a b) -> p a b", b=2), ALU.add).then_inc(s["lb"], 1)
                        for t in range(TT):
                            v.wait_ge(s["lb"], t + 1)
                            v.max(top[:, t, :], LB[:, t, :]).then_inc(s["top"], 1)
                        for t in range(TT):
                            v.wait_ge(s["top"], t + 1)
                            v.match_replace(LM[:, t, :], top[:, t, :], LB[:, t, :], -3.0e38).then_inc(s["mr"], 1)
                        v.wait_ge(s["mr"], TT)
                        v.tensor_tensor(LM[:, :, :], LM[:, :, :], LB[:, :, :], ALU.not_equal).then_inc(s["ne"], 1)
                        v.wait_ge(s["ne"], 1)
                        v.tensor_tensor(LM[:, :, :], LM[:, :, :], LB[:, :, :], ALU.mult).then_inc(s["sp"], 1)
                        v.wait_ge(s["sp"], 1)
                        v.tensor_reduce(sm[:, 0, :], LM[:, :, :], AX.X, ALU.add).then_inc(s["su"], 1)
                        v.wait_ge(s["su"], 1)
                        v.reciprocal(sm[:, 1, :], sm[:, 0, :]).then_inc(s["su"], 1)
                        v.wait_ge(s["su"], 2)
                        v.tensor_scalar(sm[:, 1, :], sm[:, 1, :], 8.0 * 2.0, None, ALU.mult).then_inc(s["rs"], 1)
                        v.wait_ge(s["rs"], 1)
                        for t in range(TT):
                            v.scalar_tensor_tensor(M[:, t, 0:LR], LM[:, t, :], sm[:, 1, t:t + 1], PS[:, 4 + t, 256:320],
                                                   ALU.mult, ALU.mult).then_inc(s["ga"], 1)
                        split_vector(v, s["m_hi"], s["m_lo"], bank=2, hh=MHI, hl=MLO, tiles=1)
                        for t in range(TT):
                            v.scalar_tensor_tensor(X[:, t, :], PS[:, 4 + t, 0:C], gate[:, 3:4], X[:, t, :], ALU.mult, ALU.add).then_inc(s["res"], 1)
                        v.wait_ge(s["lo_"], TT)
                        v.wait_ge(s["res"], TT)
                        for t in range(TT):
                            v.scalar_tensor_tensor(X[:, t, :], PS[:, t % 2, (t // 2) * C:(t // 2 + 1) * C], gate[:, 3:4], X[:, t, :],
                                                   ALU.mult, ALU.add).then_inc(s["res"], 1)

        def score_attention(pi):
            with Phase() as ph:
                s = ph.sem(LN + "mk_in mk qp qk_b q_hi q_lo sc e1 e2 e3 neg ex rc rg res")
                MU = ph.sb("MU", [P, 2, S], U8)
                MB = ph.sb("MB", [P, 2, S], U8)
                MF = ph.sb("MF", [P, 2, S])
                MG = ph.sb("MG", [P, 2, S])
                Q = ph.sb("Q", [P, 2, TOK])
                QH = ph.sb("QH", [P, 2, TOK], F32R)
                QL = ph.sb("QL", [P, 2, TOK], F32R)
                E = ph.sb("E", [P, TT, S])
                mx = ph.sb("mx", [P, TT])
                live = ph.sb("live", [P, TT])
                sm = ph.sb("sm", [P, 3, TT])
                with nc.Block() as block:
                    @block.sync
                    def _(sp):
                        sp.dma_start(MU[:, :, :], a["maskS"].rearrange("(q p) k -> p q k", p=P)).then_inc(s["mk_in"], 16)
                        sp.dma_start(MB[:, :, :].rearrange("p a b -> p (a b)"), a["maskB"][:, bass.ts(pi, TOK)].broadcast_to([P, TOK])).then_inc(s["mk_in"], 16)

                    @block.gpsimd
                    def _(g):
                        ln_gpsimd(g, s)

                    @block.tensor
                    def _(pe):
                        for r in range(2):
                            m = mm3(pe, PS[:, r, :], weight("qk2", 2, r), (CTH[:, :], CTL[:, :]))
                            m.then_inc(s["qp"], 1)
                        pe.wait_ge(s["q_lo"], 2)
                        for t in range(TT):
                            j = t // 2
                            mm3(pe, PS[:, 2 + t, 0:S], pair(QH, QL, slice(None), 0, slice(t * P, t * P + P)),
                                pair(QH, QL, slice(None), 1, slice(j * S, j * S + S))).then_inc(s["sc"], 1)

                    @block.scalar
                    def _(act):
                        for r in range(2):
                            act.wait_ge(s["qp"], r + 1)
                            act.activation(Q[:, r, :], PS[:, r, :], ACT.Identity, bias=const("qkb2")[:, r:r + 1]).then_inc(s["qk_b"], 1)
                            act.wait_ge(s["qk_b"], r + 1)
                            act.activation(QH[:, r, :], Q[:, r, :], ACT.Copy).then_inc(s["q_hi"], 1)
                        for t in range(TT):
                            act.wait_ge(s["neg"], t + 1)
                            act.activation(E[:, t, :], E[:, t, :], ACT.Exp, bias=mx[:, t:t + 1], accum_out=sm[:, 0, t:t + 1]).then_inc(s["ex"], 1)

                    @block.vector
                    def _(v):
                        ln_vector(v, s)
                        for r in range(2):
                            v.wait_ge(s["q_hi"], r + 1)
                            v.tensor_tensor(QL[:, r, :], Q[:, r, :], QH[:, r, :].bitcast(F32), ALU.subtract).then_inc(s["q_lo"], 1)
                        v.wait_ge(s["mk_in"], 32)
                        v.tensor_scalar(MF[:, :, :], MU[:, :, :], -1.0e38, None, ALU.mult).then_inc(s["mk"], 1)
                        v.tensor_scalar(MG[:, :, :], MB[:, :, :], -1.0e38, None, ALU.mult).then_inc(s["mk"], 1)
                        v.wait_ge(s["ln_norm"], TT)
                        v.wait_ge(s["mk"], 2)
                        for t in range(TT):
                            v.wait_ge(s["sc"], t + 1)
                            v.scalar_tensor_tensor(E[:, t, :], PS[:, 2 + t, 0:S], DC ** -0.5, HN[:, t, :], ALU.mult, ALU.mult).then_inc(s["e1"], 1)
                        for t in range(TT):
                            v.wait_ge(s["e1"], t + 1)
                            v.tensor_tensor(E[:, t, :], E[:, t, :], MF[:, t % 2, :], ALU.add).then_inc(s["e2"], 1)
                        for t in range(TT):
                            v.wait_ge(s["e2"], t + 1)
                            v.tensor_tensor(E[:, t, :], E[:, t, :], MG[:, t // 2, :], ALU.add).then_inc(s["e3"], 1)
                        for t in range(TT):
                            v.wait_ge(s["e3"], t + 1)
                            v.tensor_reduce(mx[:, t:t + 1], E[:, t, :], AX.X, ALU.max, negate=True).then_inc(s["neg"], 1)
                        v.wait_ge(s["neg"], TT)
                        v.tensor_scalar(live[:, :], mx[:, :], 1.0e37, None, ALU.is_lt).then_inc(s["rc"], 1)
                        v.wait_ge(s["ex"], TT)
                        v.wait_ge(s["rc"], 1)
                        v.tensor_tensor(sm[:, 0, :], sm[:, 0, :], live[:, :], ALU.mult).then_inc(s["rc"], 1)
                        v.wait_ge(s["rc"], 2)
                        v.reciprocal(sm[:, 1, :], sm[:, 0, :]).then_inc(s["rc"], 1)
                        v.wait_ge(s["rc"], 3)
                        v.scalar_tensor_tensor(sm[:, 2, :], sm[:, 1, :], gate[:, 4:5], live[:, :], ALU.mult, ALU.mult).then_inc(s["rg"], 1)
                        v.wait_ge(s["rg"], 1)
                        for t in range(TT):
                            v.scalar_tensor_tensor(X[:, t, :], E[:, t, :], sm[:, 2, t:t + 1], X[:, t, :], ALU.mult, ALU.add).then_inc(s["res"], 1)

        def router(pi):
            with Phase() as ph:
                s = ph.sem(LN + "lg smx ssub sexp ssum rank oh pw st")
                LG = ph.sb("LG", [P, TT, 8])
                RK = ph.sb("RK", [P, 3, TT, NE, NE])
                sm = ph.sb("sm", [P, 3, TT])
                HOT = ph.sb("HOT", [P, TT, 2 * NE])
                PWP = ph.sb("PWP", [P, TT, 2 * NE])
                with nc.Block() as block:
                    @block.gpsimd
                    def _(g):
                        ln_gpsimd(g, s)

                    @block.tensor
                    def _(pe):
                        transpose_tensor(pe, HN, s["ln_norm"], s["tr_done"])
                        pe.wait_ge(s["tr_lo"], KC)
                        for t in range(TT):
                            for k in range(KC):
                                m = mm3(pe, PS[:, 2, t * 8:t * 8 + 8], pair(HH, HL, slice(None), k, slice(t * P, t * P + P)),
                                        weight("rt2", KC, k), k == 0, k == KC - 1)
                        m.then_inc(s["lg"], 1)

                    @block.scalar
                    def _(act):
                        split_scalar(act, s["tr_hi"], s["tr_done"])
                        act.wait_ge(s["ssub"], 1)
                        act.activation(LG[:, :, :], LG[:, :, :], ACT.Exp).then_inc(s["sexp"], 1)

                    @block.vector
                    def _(v):
                        ln_vector(v, s)
                        split_vector(v, s["tr_hi"], s["tr_lo"])
                        lgp = PS[:, 2, 0:32].rearrange("p (t e) -> p t e", t=TT)

                        def wide(x):
                            return x.unsqueeze(2).broadcast_to([P, TT, NE])
                        v.wait_ge(s["lg"], 1)
                        v.tensor_reduce(sm[:, 0, :], lgp, AX.X, ALU.max).then_inc(s["smx"], 1)
                        v.wait_ge(s["smx"], 1)
                        v.tensor_tensor(LG[:, :, :], lgp, wide(sm[:, 0, :]), ALU.subtract).then_inc(s["ssub"], 1)
                        v.wait_ge(s["sexp"], 1)
                        v.tensor_reduce(sm[:, 1, :], LG[:, :, :], AX.X, ALU.add).then_inc(s["ssum"], 1)
                        v.wait_ge(s["ssum"], 1)
                        v.reciprocal(sm[:, 2, :], sm[:, 1, :]).then_inc(s["ssum"], 1)
                        v.wait_ge(s["ssum"], 2)
                        v.tensor_tensor(LG[:, :, :], LG[:, :, :], wide(sm[:, 2, :]), ALU.mult).then_inc(s["ssum"], 1)
                        v.wait_ge(s["ssum"], 3)
                        rank, n = rank_vector(v, s, RK, LG[:, :, :], 0)
                        for r in range(2):
                            v.tensor_scalar(HOT[:, :, NE * r:NE * r + NE], rank, float(r), None, ALU.is_equal).then_inc(s["oh"], 1)
                            v.wait_ge(s["oh"], r + 1)
                            v.tensor_tensor(PWP[:, :, NE * r:NE * r + NE], HOT[:, :, NE * r:NE * r + NE], LG[:, :, :], ALU.mult).then_inc(s["pw"], 1)
                        v.wait_ge(s["pw"], 2)
                        v.tensor_copy(OH[:, bass.ts(pi, TT), :], HOT[:, :, :]).then_inc(s["st"], 1)
                        v.tensor_copy(PW[:, bass.ts(pi, TT), :], PWP[:, :, :]).then_inc(s["st"], 1)

        def capacity():
            NT = PAIRS * TT
            with Phase() as ph:
                s = ph.sem("cm tot run cnt kp kw kr")
                RUN = ph.sb("RUN", [P, NT + 1, 2 * NE])
                CNT = ph.sb("CNT", [P, NT, 2 * NE])
                with nc.Block() as block:
                    @block.tensor
                    def _(pe):
                        ohs = OH[:, :, :].rearrange("p t e -> p (t e)")
                        pe.matmul(PS[:, 0, 0:NT * 16], trib[:, :], ohs, start=True, stop=True).then_inc(s["cm"], 1)
                        pe.matmul(PS[:, 1, 0:NT * 16], onesb[:, :], ohs, start=True, stop=True).then_inc(s["tot"], 1)

                    @block.vector
                    def _(v):
                        within = PS[:, 0, 0:NT * 16].rearrange("p (t e) -> p t e", t=NT)
                        total = PS[:, 1, 0:NT * 16].rearrange("p (t e) -> p t e", t=NT)
                        v.memset(RUN[:, 0, :], 0.0).then_inc(s["run"], 1)
                        v.wait_ge(s["tot"], 1)
                        for t in range(NT):
                            v.wait_ge(s["run"], t + 1)
                            v.tensor_tensor(RUN[:, t + 1, :], RUN[:, t, :], total[:, t, :], ALU.add).then_inc(s["run"], 1)
                        v.wait_ge(s["run"], NT + 1)
                        v.wait_ge(s["cm"], 1)
                        v.tensor_tensor(CNT[:, :, :], within, RUN[:, 0:NT, :], ALU.add).then_inc(s["cnt"], 1)
                        v.wait_ge(s["cnt"], 1)
                        v.tensor_tensor(CNT[:, :, NE:2 * NE], CNT[:, :, NE:2 * NE],
                                        RUN[:, NT, 0:NE].unsqueeze(1).broadcast_to([P, NT, NE]), ALU.add).then_inc(s["cnt"], 1)
                        v.wait_ge(s["cnt"], 2)
                        v.tensor_scalar(CNT[:, :, :], CNT[:, :, :], float(CAP), None, ALU.is_le).then_inc(s["kp"], 1)
                        v.wait_ge(s["kp"], 1)
                        v.tensor_tensor(CNT[:, :, :], CNT[:, :, :], PW[:, :, :], ALU.mult).then_inc(s["kw"], 1)
                        v.wait_ge(s["kw"], 1)
                        v.tensor_reduce(COEF[:, :], CNT[:, :, :], AX.X, ALU.add).then_inc(s["kr"], 1)
                        v.wait_ge(s["kr"], 1)
                        v.tensor_scalar(COEF[:, :], COEF[:, :], gate[:, 5:6], None, ALU.mult).then_inc(s["kr"], 1)

        setup_weights()
        setup_fold()
        with nc.Fori(0, PAIRS) as i:
            load_pair(i)
            graph_attention()
            small_attention(0)
            experts(0)
            latent_attention(i)
            low_rank()
            score_attention(i)
            router(i)
            store_pair(i)
        capacity()
        with nc.Fori(0, PAIRS) as i:
            load_pair(i, routed=True)
            experts(2)
            small_attention(3)
            experts(3)
            store_pair(i)
        with Phase() as ph:
            s = ph.sem("stored")
            with nc.Block() as block:
                @block.sync
                def _(sp):
                    sp.dma_start(out.rearrange("(t p) c -> p t c", p=P), XALL[:, :, :]).then_inc(s["stored"], 16)
                    sp.wait_ge(s["stored"], 16)


def _rows(w, n=P):
    w = np.asarray(w)
    return np.concatenate([w, np.zeros((n - w.shape[0],) + w.shape[1:], w.dtype)]) if w.shape[0] < n else w


def _ktiles(w):
    return np.concatenate([w[:P], w[P:]], axis=1)


def _swap8(w):
    n = w.shape[-1]
    return np.ascontiguousarray(w.reshape(w.shape[:-1] + (n // 16, 2, 8))[..., ::-1, :]).reshape(w.shape)


def _pad_cols(w, n):
    return np.concatenate([w, np.zeros(w.shape[:-1] + (n - w.shape[-1],), w.dtype)], axis=-1)


def _hidden_tiles(gate, up, down, tiles, sizes=()):
    n = tiles * P
    gate, up = _pad_cols(gate, n), _pad_cols(up, n)
    down = _rows(down, n)
    g = gate.reshape(KC, P, tiles, P).transpose(2, 1, 0, 3).reshape(tiles, P, KC * P)
    u = up.reshape(KC, P, tiles, P).transpose(2, 1, 0, 3).reshape(tiles, P, KC * P)
    sel = _selector(sizes, tiles).reshape(P, tiles, P).transpose(1, 0, 2)
    return np.ascontiguousarray(np.concatenate([g, u, down.reshape(tiles, P, C), sel], axis=2))


def _selector(sizes, tiles):
    owner = np.concatenate([np.full(n, e) for e, n in enumerate(sizes)] + [np.full(tiles * P - sum(sizes), -1)])
    sel = np.zeros((P, tiles * P), np.float32)
    for e in range(len(sizes)):
        sel[e] = owner == e
        sel[32 + e] = owner == e
    return sel


def _layout(i):
    g = {k: np.asarray(v) for k, v in i.items()}
    f = np.float32
    arrays = {}
    arrays["x"] = g["x"].reshape(B * S, C)
    ctx = g["ctx_512"]
    arrays["ctx"] = ctx.reshape(B * S, DC)
    arrays["ctxT"] = _rows(np.ascontiguousarray(ctx.reshape(B * S, DC).T))
    arrays["maskS"] = g["mask_SxS2_bk1"]
    arrays["maskB"] = g["mask_BxS2_bf0"].reshape(1, B * S)

    wq, wk = g["L0_ffn_wq"], g["L0_ffn_wk"]
    rt0 = _pad_cols(np.concatenate([g["L0_ffn_w_router"], g["L0_ffn_w_sh_eg"]], axis=1), 16)
    l1 = np.concatenate([g["L1_ffn_base_W"].T, g["L1_ffn_A"].T, g["L1_ffn_router_W"].T], axis=1)
    W = {
        "gat0": _rows(g["L0_xattn_W0"].transpose(1, 0, 2).reshape(DC, 256)),
        "gat1": _ktiles(g["L0_xattn_W1"].transpose(1, 0, 2).reshape(256, 256)),
        "qk0": _ktiles(np.concatenate([wq, _swap8(wq), wk, _swap8(wk)], axis=1)),
        "v0": _ktiles(g["L0_ffn_wv"]), "o0": _ktiles(g["L0_ffn_wo"]), "rt0": _ktiles(rt0),
        "l1f": _ktiles(l1), "l1b": _rows(g["L1_ffn_B"].T),
        "qk2": _rows(np.concatenate([_pad_cols(g["L2_xattn_Wq"].T, P), _pad_cols(g["L2_xattn_Wk"].T, P)], axis=1)),
        "rt2": _ktiles(g["L2_ffn_router_w"].T),
        "q3": _ktiles(g["L3_xattn_Wq"].T), "k3": _rows(g["L3_xattn_Wkv_expand"][:C].T),
        "v3": _rows(g["L3_xattn_Wkv_expand"][C:].T), "o3": _ktiles(g["L3_xattn_Wout"].T),
        "rt3": _ktiles(g["L3_ffn_gate_w"].T),
    }
    for name, n in WCOLS:
        assert W[name].shape == (P, n), (name, W[name].shape, n)
    arrays["wpack"] = _pad_cols(np.concatenate([W[n] for n, _ in WCOLS], axis=1), CHUNKS * CHUNK)

    def spread(v):
        return np.broadcast_to(np.asarray(v).reshape(1, -1), (P, np.asarray(v).size))

    def columns(v, n):
        return np.ascontiguousarray(v.reshape(n, P).T)

    feat, pos = np.arange(P), np.arange(S)
    inv = (1.0 / f(1000000.0) ** (np.arange(0, 16, 2, dtype=f) / f(16))).astype(f)
    ang = (pos[None, :].astype(f) * inv[feat % 8][:, None]).astype(f).astype(np.float64)
    sign = np.where(feat % 16 < 8, -1.0, 1.0)[:, None]
    inv2 = (1.0 / f(10000.0) ** (np.arange(0, DC, 2, dtype=f) / f(DC))).astype(f)
    ang2 = np.repeat((pos[:, None].astype(f) * inv2[None, :]).astype(f), 2, axis=1).astype(np.float64)
    sign2 = np.where(np.arange(DC) < DC // 2, -1.0, 1.0)[None, :]
    e0, e1 = np.meshgrid(np.arange(NE), np.arange(NE), indexing="ij")
    bq, bk = g["L0_ffn_bq"], g["L0_ffn_bk"]
    CC = {
        "ident": np.eye(P), "causal": np.where(feat[None, :] > feat[:, None], MASKED, 0.0),
        "headmask": (feat[:, None] // 16 == np.arange(8)[None, :]),
        "halfmask": (feat[:, None] // 64 == np.arange(2)[None, :]),
        "tri": feat[:, None] <= feat[None, :],
        "ropec": np.cos(ang), "ropes": np.sin(ang) * sign,
        "kvc": np.cos(ang2).reshape(2, P, DC).transpose(1, 0, 2).reshape(P, 2 * DC),
        "kvs": (np.sin(ang2) * sign2).reshape(2, P, DC).transpose(1, 0, 2).reshape(P, 2 * DC),
        "lower": spread((e1 < e0).astype(f)), "upper": spread((e1 > e0).astype(f)),
        "ln1": columns(g["L0_ffn_w_ln1"], KC), "ln2": columns(g["L0_ffn_w_ln2"], KC),
        "qkb": np.concatenate([columns(b, KC) for b in (bq, _swap8(bq), bk, _swap8(bk))], axis=1),
        "b1f": columns(g["L2_ffn_b1"], T2),
        "qkb2": _rows(np.stack([g["L2_xattn_bq"], g["L2_xattn_bk"]], axis=1)),
        "aself0": spread(g["L0_xattn_a_self0"]), "aneigh0": spread(g["L0_xattn_a_neigh0"]),
        "aself1": spread(g["L0_xattn_a_self1"]), "aneigh1": spread(g["L0_xattn_a_neigh1"]),
        "gb0": spread(g["L0_xattn_b0"]), "gb1": spread(g["L0_xattn_b1"]), "bv0": spread(g["L0_ffn_bv"]),
        "lora_b": spread(g["L1_ffn_biases"]), "b2f": spread(g["L2_ffn_b2"]), "gbias3": spread(g["L3_ffn_gate_bias"]),
        "gates": spread(np.stack([g["g_xattn"], g["g_ffn"]], axis=1)),
    }
    arrays["consts"] = np.ascontiguousarray(np.concatenate([CC[n].astype(f) for n, _ in CCOLS], axis=1))

    kcq = g["L1_xattn_w_kc_q"].transpose(0, 2, 1)
    wqr = g["L1_xattn_W_qr"]
    def two(w):
        lo = np.concatenate([w[:, P:], np.zeros((MH, 2 * P - w.shape[1], w.shape[2]), w.dtype)], axis=1)
        return np.concatenate([w[:, :P], lo], axis=2)
    wkr = g["L1_xattn_W_kr"].transpose(0, 2, 1)
    wkr = np.concatenate([wkr, np.zeros_like(wkr)], axis=1)
    wq1 = g["L1_xattn_Wq"].reshape(MH, P, C)
    wo1 = g["L1_xattn_Wo"].T.reshape(MH, P, C)
    arrays["fold"] = np.ascontiguousarray(np.concatenate([two(kcq), two(wqr), wkr, wq1, g["L1_xattn_w_kc_kv"], wo1], axis=2))

    def cat(w):
        return w.transpose(1, 0, 2).reshape(w.shape[1], -1)
    arrays["moe0"] = _hidden_tiles(
        np.concatenate([cat(g["L0_ffn_w_gate_e"]), g["L0_ffn_w_sh_gate"]], axis=1),
        np.concatenate([cat(g["L0_ffn_w_up_e"]), g["L0_ffn_w_sh_up"]], axis=1),
        np.concatenate([g["L0_ffn_w_down_e"].reshape(-1, C), g["L0_ffn_w_sh_down"]], axis=0), T0, [MOE_I] * NE + [SH_I])
    up, sg = g["L3_ffn_up_w"].transpose(0, 2, 1), g["L3_ffn_shared_gw"].T
    arrays["moe3"] = _hidden_tiles(
        np.concatenate([cat(up[:, :, :H3]), sg[:, HS3:]], axis=1),
        np.concatenate([cat(up[:, :, H3:]), sg[:, :HS3]], axis=1),
        np.concatenate([g["L3_ffn_down_w"].transpose(0, 2, 1).reshape(-1, C), g["L3_ffn_shared_dw"].T], axis=0), T3, [H3] * NE + [HS3])
    w1 = g["L2_ffn_w1"].T
    arrays["ffn2"] = np.ascontiguousarray(_hidden_tiles(w1, w1, g["L2_ffn_w2"].T, T2)[:, :, [*range(256), *range(512, 896)]])
    return {k: np.ascontiguousarray(v) for k, v in arrays.items()}


def kernel(**inputs):
    import concourse.bacc as bacc
    from concourse.bass_utils import run_bass_kernel_spmd

    nc = bacc.Bacc("TRN2", target_bir_lowering=False, num_devices=1)
    arrays = _layout(inputs)
    feeds, aps = {}, {}
    for name, array in arrays.items():
        feeds[f"in_{name}"] = array
        aps[name] = nc.dram_tensor(f"in_{name}", array.shape, mybir.dt.from_np(array.dtype), kind="ExternalInput").ap()
    out = nc.dram_tensor("out_0", (B * S, C), F32, kind="ExternalOutput").ap()
    build(nc, aps, out)
    result = run_bass_kernel_spmd(nc, [feeds], core_ids=[0])
    return result.results[0]["out_0"].reshape(B, S, C)
```

```python
from contextlib import ExitStack

import numpy as np
import concourse.bass as bass
from concourse import mybir

F32 = mybir.dt.float32
F32R = mybir.dt.float32r
BF16 = mybir.dt.bfloat16
U8 = mybir.dt.uint8
ALU = mybir.AluOpType
ACT = mybir.ActivationFunctionType
AX = mybir.AxisListType

P = 128
B, S, C = 4, 256, 256
DC = 64
TT = 4
TOK = TT * P
PAIRS = B * S // TOK
KC = C // P
GH, GO = 8, 32
NH, HD = 16, 16
MH = 16
NE = 8
CAP = 64
MOE_I, SH_I = 176, 704
H3, HS3 = 176, 352
T0 = -(-(NE * MOE_I + SH_I) // P)
T3 = -(-(NE * H3 + HS3) // P)
T2 = 1024 // P
LR = 64
MASKED = -1.0e30

WCOLS = [
    ("gat0", GH * GO), ("gat1", KC * GH * GO),
    ("qk0", KC * 4 * C), ("v0", KC * C), ("o0", KC * C), ("rt0", KC * 16),
    ("l1f", KC * 352), ("l1b", C),
    ("qk2", 2 * P), ("rt2", KC * 8),
    ("q3", KC * C), ("k3", C), ("v3", C), ("o3", KC * C), ("rt3", KC * 8),
]
CCOLS = [
    ("ident", P), ("causal", P), ("headmask", 8), ("halfmask", 2), ("tri", P),
    ("ropec", S), ("ropes", S), ("kvc", 2 * DC), ("kvs", 2 * DC), ("lower", NE * NE), ("upper", NE * NE),
    ("ln1", KC), ("ln2", KC), ("qkb", 8), ("b1f", T2), ("qkb2", 2),
    ("aself0", 256), ("aneigh0", 256), ("aself1", 256), ("aneigh1", 256),
    ("gb0", 256), ("gb1", 256), ("bv0", 256), ("lora_b", LR), ("b2f", 256), ("gbias3", NE), ("gates", 8),
]


def offsets(cols):
    at, out = 0, {}
    for name, n in cols:
        out[name] = (at, n)
        at += n
    return out, at


WOFF, WTOT = offsets(WCOLS)
COFF, CTOT = offsets(CCOLS)
CHUNK = 1024
CHUNKS = -(-WTOT // CHUNK)
SEMS = range(99, 256)
WARM = {"own": 12, "rms": 4, "att": 4, "latent": 4, "split": 8,
        "start": 4, "group": 3, "elu": 8}


def mm3(pe, out, left, right, first=True, last=True, skip=False):
    pe.matmul(out, left[0], right[0], start=first, stop=False, skip_group_check=skip)
    pe.matmul(out, left[0], right[1], start=False, stop=False, skip_group_check=skip)
    return pe.matmul(out, left[1], right[0], start=False, stop=last, skip_group_check=skip)


def build(nc, a, out):
    with ExitStack() as whole:
        def tensor(name, shape, dt=F32, stack=whole):
            return stack.enter_context(nc.sbuf_tensor(name, shape, dt))

        WH = tensor("WH", [P, CHUNKS * CHUNK], F32R)
        WL = tensor("WL", [P, CHUNKS * CHUNK], F32R)
        CP = tensor("CP", [P, CTOT])
        AH = tensor("AH", [P, KC, MH * DC], F32R)
        AL = tensor("AL", [P, KC, MH * DC], F32R)
        BH = tensor("BH", [P, MH // 2, C], F32R)
        BL = tensor("BL", [P, MH // 2, C], F32R)
        EH = tensor("EH", [P, 3, 16], F32R)
        EL = tensor("EL", [P, 3, 16], F32R)
        PICK = tensor("PICK", [P, 16], F32R)
        identb = tensor("identb", [P, P], BF16)
        causalb = tensor("causalb", [P, P], BF16)
        trib = tensor("trib", [P, P], BF16)
        onesb = tensor("onesb", [P, P], BF16)
        ones1 = tensor("ones1", [P, 80])
        halfneg = tensor("halfneg", [P, TT])
        gate = tensor("gate", [P, 8])
        XALL = tensor("XALL", [P, PAIRS * TT, C])
        OH = tensor("OH", [P, PAIRS * TT, 2 * NE], BF16)
        PW = tensor("PW", [P, PAIRS * TT, 2 * NE])
        COEF = tensor("COEF", [P, PAIRS * TT])
        COEF2 = tensor("COEF2", [P, TT])
        X = tensor("X", [P, TT, C])
        HN = tensor("HN", [P, TT, C])
        XN = tensor("XN", [P, TT, C])
        HH = tensor("HH", [P, KC, TOK], F32R)
        HL = tensor("HL", [P, KC, TOK], F32R)
        CTN = tensor("CTN", [P, PAIRS * TT, DC])
        CTH = tensor("CTH", [P, TOK], F32R)
        CTL = tensor("CTL", [P, TOK], F32R)
        stats = tensor("stats", [P, TT, 6])
        mv = tensor("mv", [P, TT, 2])
        rstd = tensor("rstd", [P, TT])
        ssq = tensor("ssq", [P, TT])
        PS = whole.enter_context(nc.psum_tensor("PS", [P, 8, 512], F32))

        def const(name):
            at, n = COFF[name]
            return CP[:, at:at + n]

        def weight(name, k=1, t=0, lo=0, hi=None):
            at, n = WOFF[name]
            n //= k
            hi = n if hi is None else hi
            return WH[:, at + t * n + lo:at + t * n + hi], WL[:, at + t * n + lo:at + t * n + hi]

        def pair(hi, lo, *index):
            return hi[index], lo[index]

        ident = const("ident")

        class Phase:
            count = 0

            def __init__(self):
                self.stack = ExitStack()
                Phase.count += 1
                self.tag = f"p{Phase.count}_"

            def __enter__(self):
                return self

            def sem(self, names):
                return {n: self.stack.enter_context(nc.semaphore(self.tag + n)) for n in names.split()}

            def sems(self, name, n):
                return [self.stack.enter_context(nc.semaphore(f"{self.tag}{name}{i}")) for i in range(n)]

            def sb(self, name, shape, dt=F32):
                return tensor(self.tag + name, shape, dt, self.stack)

            def __exit__(self, *e):
                if e[0] is None:
                    nc.all_engine_barrier(sems_to_clear=SEMS)
                self.stack.close()

        STATS = "ln_stats ln_aggr ln_eps ln_rstd "
        LN = "ln_norm tr_done tr_hi tr_lo " + STATS

        def stats_vector(v, s, t, ready, n):
            v.wait_ge(s[ready], n)
            v.bn_stats(stats[:, t, :], X[:, t, :]).then_inc(s["ln_stats"], 1)

        def stats_done(v, s):
            for t in range(TT):
                v.wait_ge(s["ln_stats"], t + 1)
                v.bn_aggr(mv[:, t, :], stats[:, t, :]).then_inc(s["ln_aggr"], 1)

        def stats_gpsimd(g, s):
            g.wait_ge(s["ln_aggr"], TT)
            g.tensor_scalar(rstd[:, :], mv[:, :, 1], 1e-5, None, ALU.add).then_inc(s["ln_eps"], 1)
            g.wait_ge(s["ln_eps"], 1)
            g.tensor_tensor(rstd[:, :], rstd[:, :], halfneg[:, :], ALU.pow).then_inc(s["ln_rstd"], 1)

        def ln_vector(v, s):
            for t in range(TT):
                v.tensor_scalar(HN[:, t, :], X[:, t, :], mv[:, t, 0:1], rstd[:, t:t + 1],
                                ALU.subtract, ALU.mult).then_inc(s["ln_norm"], 1)

        def warm(pe, n, bank=7):
            for i in range(n):
                pe.matmul(PS[:, bank, :], identb[:, :], onesb[:, :].unsqueeze(1).broadcast_to([P, 4, P]), start=True, stop=True)

        def transpose_tensor(pe, src, ready, done, bank=0, tiles=KC):
            for t in range(TT):
                pe.wait_ge(ready, t + 1)
                for k in range(tiles):
                    m = pe.transpose(PS[:, bank + k, t * P:(t + 1) * P], src[:, t, k * P:(k + 1) * P], ident)
            m.then_inc(done, 1)

        def split_scalar(act, s, done, bank=0, hh=HH, tiles=KC, scale=None):
            act.wait_ge(done, 1)
            for k in range(tiles):
                if scale is None:
                    i = act.activation(hh[:, k, :], PS[:, bank + k, :], ACT.Copy)
                else:
                    i = act.activation(hh[:, k, :], PS[:, bank + k, :], ACT.Copy, scale=scale[:, k:k + 1])
                i.then_inc(s, 1)

        def split_vector(v, s_hi, s_lo, bank=0, hh=HH, hl=HL, tiles=KC, scale=None, base=0):
            for k in range(tiles):
                v.wait_ge(s_hi, base + k + 1)
                if scale is None:
                    i = v.tensor_tensor(hl[:, k, :], PS[:, bank + k, :], hh[:, k, :].bitcast(F32), ALU.subtract)
                else:
                    i = v.scalar_tensor_tensor(hl[:, k, :], PS[:, bank + k, :], scale[:, k:k + 1],
                                               hh[:, k, :].bitcast(F32), ALU.mult, ALU.subtract)
                i.then_inc(s_lo, 1)

        def rms_scalar(act, s, src, ready, junk, sq="rms_sq"):
            for t in range(TT):
                act.wait_ge(ready, t + 1)
                if t:
                    act.wait_ge(s[sq], t)
                act.activation(junk[:, :], src[:, t, :], ACT.Square, accum_out=ssq[:, t:t + 1]).then_inc(s[sq], 1)

        def rms_gpsimd(g, s, sq="rms_sq", eps="rms_eps", done="rms_rstd"):
            g.wait_ge(s[sq], TT)
            g.tensor_scalar(rstd[:, :], ssq[:, :], 1.0 / C, 1e-6, ALU.mult, ALU.add).then_inc(s[eps], 1)
            g.wait_ge(s[eps], 1)
            g.tensor_tensor(rstd[:, :], rstd[:, :], halfneg[:, :], ALU.pow).then_inc(s[done], 1)

        def rank_vector(v, s, buf, scores, n0):
            n = n0
            gt = buf[:, 0]
            ge = buf[:, 1]
            other = scores.unsqueeze(2).broadcast_to([P, TT, NE, NE])
            mine = scores.unsqueeze(3).broadcast_to([P, TT, NE, NE])
            up = const("upper").rearrange("p (a b) -> p a b", a=NE).unsqueeze(1).broadcast_to([P, TT, NE, NE])
            low = const("lower").rearrange("p (a b) -> p a b", a=NE).unsqueeze(1).broadcast_to([P, TT, NE, NE])
            v.tensor_tensor(gt, other, mine, ALU.is_gt).then_inc(s["rank"], 1)
            v.tensor_tensor(ge, other, mine, ALU.is_ge).then_inc(s["rank"], 1)
            n += 2
            v.wait_ge(s["rank"], n)
            v.tensor_tensor(gt, gt, up, ALU.mult).then_inc(s["rank"], 1)
            v.tensor_tensor(ge, ge, low, ALU.mult).then_inc(s["rank"], 1)
            n += 2
            v.wait_ge(s["rank"], n)
            v.tensor_tensor(gt, gt, ge, ALU.add).then_inc(s["rank"], 1)
            n += 1
            v.wait_ge(s["rank"], n)
            v.tensor_reduce(buf[:, 2, :, 0, :], gt, AX.X, ALU.add).then_inc(s["rank"], 1)
            n += 1
            v.wait_ge(s["rank"], n)
            return buf[:, 2, :, 0, :], n

        def setup():
            with Phase() as ph:
                FR = 8
                w_in = ph.sems("w_in", 4)
                f_in = ph.sems("f_in", FR)
                s = ph.sem("xc_in w_hi w_lo c_set ext ext_hi ext_sp tanh m1 m1c m2 m2c ab ab_hi ab_lo")
                raw = ph.sb("raw", [P, 4, CHUNK])
                gat1w = ph.sb("gat1w", [P, 3, 256])
                extt = ph.sb("extt", [P, 6, 256])
                ext = ph.sb("ext", [P, 3, 16])
                NF = 2 * P + 2 * DC + DC + C + DC + C
                fr = ph.sb("fr", [P, FR, NF])
                m1s = ph.sb("m1s", [P, 2, P])
                m2s = ph.sb("m2s", [P, 2, DC])
                with nc.Block() as block:
                    @block.sync
                    def _(sp):
                        for i in range(max(CHUNKS, MH)):
                            if i < MH:
                                if i >= FR:
                                    sp.wait_ge(s["ab"], i - FR + 1)
                                sp.dma_start(fr[:, i % FR, :], a["fold"][i]).then_inc(f_in[i % FR], 16)
                            if i < CHUNKS:
                                if i >= 4:
                                    sp.wait_ge(s["w_lo"], i - 3)
                                sp.dma_start(raw[:, i % 4, :], a["wpack"][:, i * CHUNK:(i + 1) * CHUNK]).then_inc(w_in[i % 4], 16)
                            if i == 4:
                                sp.dma_start(CTN[:, :, :], a["ctx"].rearrange("(t p) d -> p t d", p=P)).then_inc(s["xc_in"], 16)
                            if i == 3:
                                sp.dma_start(CP[:, :], a["consts"]).then_inc(s["xc_in"], 16)
                                sp.dma_start(gat1w[:, :, :], a["wpack"][:, 0:768].rearrange("p (a b) -> p a b", a=3)).then_inc(s["xc_in"], 16)
                                sp.dma_start(XALL[:, :, :], a["x"].rearrange("(t p) c -> p t c", p=P)).then_inc(s["xc_in"], 16)

                    @block.tensor
                    def _(pe):
                        def first(h):
                            r, o = fr[:, h % FR, :], h % 2
                            pe.wait_ge(f_in[h % FR], 16 * (h // FR + 1))
                            if h >= 2:
                                pe.wait_ge(s["m1c"], h - 1)
                            pe.matmul(PS[0:DC, o, 0:P], r[:, 256:320], r[:, 0:128], start=True, stop=False)
                            pe.matmul(PS[0:DC, o, 0:P], r[0:DC, 320:384], r[0:DC, 128:256], start=False, stop=True).then_inc(s["m1"], 1)

                        def second(h):
                            r, o = fr[:, h % FR, :], h % 2
                            pe.wait_ge(s["m1c"], h + 1)
                            if h >= 2:
                                pe.wait_ge(s["m2c"], h - 1)
                            pe.matmul(PS[:, 2 + o, 0:DC], m1s[0:DC, o, :], r[0:DC, 384:448], start=True, stop=True).then_inc(s["m2"], 1)

                        def third(h):
                            r, o, q = fr[:, h % FR, :], h % 2, DC * (h % 2)
                            pe.wait_ge(s["m2c"], h + 1)
                            if h >= 2:
                                pe.wait_ge(s["ab_lo"], 2 * (h - 1))
                            for k in range(KC):
                                pe.matmul(PS[:, 4 + o, k * DC:(k + 1) * DC], r[:, 448 + k * P:448 + (k + 1) * P], m2s[:, o, :],
                                          start=True, stop=True)
                            pe.matmul(PS[q:q + DC, 6 + o, 0:C], r[:, 704:768], r[:, 768:1024], start=True, stop=True).then_inc(s["ab"], 1)

                        for h in range(MH + 2):
                            if h < MH:
                                first(h)
                            if 1 <= h <= MH:
                                second(h - 1)
                            if h >= 2:
                                third(h - 2)

                    @block.scalar
                    def _(act):
                        def fold_hi(h):
                            o, q = h % 2, DC * (h % 2)
                            act.wait_ge(s["ab"], h + 1)
                            act.activation(AH[:, :, h * DC:(h + 1) * DC],
                                           PS[:, 4 + o, 0:KC * DC].rearrange("p (k d) -> p k d", k=KC), ACT.Copy).then_inc(s["ab_hi"], 1)
                            act.activation(BH[q:q + DC, h // 2, :], PS[q:q + DC, 6 + o, 0:C], ACT.Copy).then_inc(s["ab_hi"], 1)

                        def weights_hi(i):
                            act.wait_ge(w_in[i % 4], 16 * (i // 4 + 1))
                            act.activation(WH[:, i * CHUNK:(i + 1) * CHUNK], raw[:, i % 4, :], ACT.Copy).then_inc(s["w_hi"], 1)

                        for h in range(MH + 2):
                            if h < MH:
                                act.wait_ge(s["m1"], h + 1)
                                act.activation(m1s[0:DC, h % 2, :], PS[0:DC, h % 2, 0:P], ACT.Copy).then_inc(s["m1c"], 1)
                            if 1 <= h <= MH:
                                act.wait_ge(s["m2"], h)
                                act.activation(m2s[:, (h - 1) % 2, :], PS[:, 2 + (h - 1) % 2, 0:DC], ACT.Copy).then_inc(s["m2c"], 1)
                            if h < CHUNKS:
                                weights_hi(h)
                            if h >= 2:
                                fold_hi(h - 2)
                        for i in range(MH + 2, CHUNKS):
                            weights_hi(i)
                        act.wait_ge(s["ext"], 12)
                        act.activation(EH[:, :, :], ext[:, :, :], ACT.Copy).then_inc(s["ext_hi"], 1)
                        act.wait_ge(s["xc_in"], 64)
                        act.activation(gate[:, :], const("gates"), ACT.Tanh).then_inc(s["tanh"], 1)

                    @block.vector
                    def _(v):
                        def fold_lo(h):
                            o, q = h % 2, DC * (h % 2)
                            v.wait_ge(s["ab_hi"], 2 * h + 2)
                            v.tensor_tensor(AL[:, :, h * DC:(h + 1) * DC],
                                            PS[:, 4 + o, 0:KC * DC].rearrange("p (k d) -> p k d", k=KC),
                                            AH[:, :, h * DC:(h + 1) * DC].bitcast(F32), ALU.subtract).then_inc(s["ab_lo"], 1)
                            v.tensor_tensor(BL[q:q + DC, h // 2, :], PS[q:q + DC, 6 + o, 0:C],
                                            BH[q:q + DC, h // 2, :].bitcast(F32), ALU.subtract).then_inc(s["ab_lo"], 1)

                        def weights_lo(i):
                            v.wait_ge(s["w_hi"], i + 1)
                            v.tensor_tensor(WL[:, i * CHUNK:(i + 1) * CHUNK], raw[:, i % 4, :],
                                            WH[:, i * CHUNK:(i + 1) * CHUNK].bitcast(F32), ALU.subtract).then_inc(s["w_lo"], 1)

                        v.memset(halfneg[:, :], -0.5).then_inc(s["c_set"], 1)
                        v.memset(ones1[:, :], 1.0).then_inc(s["c_set"], 1)
                        v.memset(onesb[:, :], 1.0).then_inc(s["c_set"], 1)
                        for h in range(MH + 2):
                            if h < CHUNKS:
                                weights_lo(h)
                            if h == MH - 2:
                                v.wait_ge(s["xc_in"], 64)
                                v.tensor_copy(identb[:, :], const("ident")).then_inc(s["c_set"], 1)
                                v.tensor_tensor(PICK[:, :], ident[:, 0:16], ident[:, 32:48], ALU.add).then_inc(s["c_set"], 1)
                                v.tensor_copy(causalb[:, :], const("causal")).then_inc(s["c_set"], 1)
                                v.tensor_copy(trib[:, :], const("tri")).then_inc(s["c_set"], 1)
                                for n, (k, c) in enumerate([(0, "aself0"), (0, "aneigh0"), (1, "aself1"), (1, "aneigh1"),
                                                            (2, "aself1"), (2, "aneigh1")]):
                                    v.tensor_tensor(extt[:, n, :], gat1w[:, k, :], const(c), ALU.mult).then_inc(s["ext"], 1)
                                v.wait_ge(s["ext"], 6)
                                for n, k in enumerate([0, 0, 1, 1, 2, 2]):
                                    v.tensor_reduce(ext[:, k, 8 * (n % 2):8 * (n % 2) + 8],
                                                    extt[:, n, :].rearrange("p (h o) -> p h o", h=GH), AX.X, ALU.add).then_inc(s["ext"], 1)
                            if h >= 2:
                                fold_lo(h - 2)
                        for i in range(MH + 2, CHUNKS):
                            weights_lo(i)
                        v.wait_ge(s["ext_hi"], 1)
                        v.tensor_tensor(EL[:, :, :], ext[:, :, :], EH[:, :, :].bitcast(F32), ALU.subtract).then_inc(s["ext_sp"], 1)

        def load_pair(i, routed=False):
            with Phase() as ph:
                s = ph.sem(STATS + "ct_in ct_hi x_cp")
                ctr = ph.sb("ctr", [P, TOK])
                with nc.Block() as block:
                    @block.sync
                    def _(sp):
                        sp.dma_start(ctr[:, :], a["ctxT"][:, bass.ts(i, TOK)]).then_inc(s["ct_in"], 16)
                        sp.wait_ge(s["ct_in"], 16)

                    @block.gpsimd
                    def _(g):
                        stats_gpsimd(g, s)

                    @block.scalar
                    def _(act):
                        act.wait_ge(s["ct_in"], 16)
                        act.activation(CTH[:, :], ctr[:, :], ACT.Copy).then_inc(s["ct_hi"], 1)

                    @block.vector
                    def _(v):
                        v.tensor_copy(X[:, :, :], XALL[:, bass.ts(i, TT), :]).then_inc(s["x_cp"], 1)
                        if routed:
                            v.tensor_copy(COEF2[:, :], COEF[:, bass.ts(i, TT)]).then_inc(s["x_cp"], 1)
                        for t in range(TT):
                            stats_vector(v, s, t, "x_cp", 1)
                        stats_done(v, s)
                        v.wait_ge(s["ct_hi"], 1)
                        v.tensor_tensor(CTL[:, :], ctr[:, :], CTH[:, :].bitcast(F32), ALU.subtract).then_inc(s["x_cp"], 1)

        def store_pair(i):
            with Phase() as ph:
                s = ph.sem("x_st")
                with nc.Block() as block:
                    @block.vector
                    def _(v):
                        v.tensor_copy(XALL[:, bass.ts(i, TT), :], X[:, :, :]).then_inc(s["x_st"], 1)

        def graph_attention():
            with Phase() as ph:
                s = ph.sem(LN + "adj base self selfc nt nz ns_hi ns_lo feat featc nb z lr e neg p pt pts_v pts_a pv o_r o_c y_b y_m y_e y_x h1 tr1 hi1 lo1 one ft_s")
                BASE = ph.sb("BASE", [P, TT, S])
                FT = ph.sb("FT", [P, TT, GH, GO + 1])
                SV = ph.sb("SV", [P, TT, 2 * GH])
                NS = ph.sb("NS", [P, TOK], F32R)
                Z = ph.sb("Z", [P, 2, 4, S])
                E = ph.sb("E", [P, 2, 4, S])
                PR = ph.sb("PR", [P, 2, 4, S])
                PTS = ph.sb("PTS", [P, 2, 2, 2, 2, P])
                mx = ph.sb("mx", [P, 2, 4])
                rin = ph.sb("rin", [P, 2, 4])
                O = ph.sb("O", [P, TT, GH, GO])
                YM = ph.sb("YM", [P, TT, C])
                YR = ph.sb("YR", [P, TT, C])
                NG = 2 * TT

                with nc.Block() as block:
                    @block.gpsimd
                    def _(g):
                        stats_gpsimd(g, s)

                    @block.tensor
                    def _(pe):
                        for l in range(2):
                            kt = 1 if l == 0 else KC

                            def left(k, lo, hi):
                                return pair(CTH, CTL, slice(None), slice(lo, hi)) if l == 0 else \
                                    pair(HH, HL, slice(None), k, slice(lo, hi))

                            def neighbours(hg):
                                if l + hg:
                                    pe.wait_ge(s["z"], NG * l + TT * hg)
                                for hh in range(4):
                                    h = GH + 4 * hg + hh
                                    m = pe.matmul(PS[:, hh, :], PICK[:, h:h + 1].broadcast_to([P, P]), NS[:, :], start=True, stop=True)
                                m.then_inc(s["nb"], 1)

                            def pv(n):
                                hg, t = divmod(n % NG, TT)
                                pe.wait_ge(s["pts_v"], n + 1)
                                pe.wait_ge(s["pts_a"], n + 1)
                                if n >= 2:
                                    pe.wait_ge(s["o_c"], n - 1)
                                for hh in range(4):
                                    for mt in range(2):
                                        m = pe.matmul(PS[:, 6 + n % 2, hh * 33:hh * 33 + 33], PTS[:, n % 2, hh // 2, hh % 2, mt, :],
                                                      FT[:, 2 * (t // 2) + mt, 4 * hg + hh, :], start=(mt == 0), stop=(mt == 1))
                                m.then_inc(s["pv"], 1)

                            if l == 0:
                                warm(pe, WARM["start"])
                            else:
                                pe.wait_ge(s["lo1"], KC)
                                pe.wait_ge(s["o_c"], NG)
                                pe.wait_ge(s["pts_v"], NG)
                                pe.wait_ge(s["pts_a"], NG)
                            for t in range(TT):
                                for k in range(kt):
                                    m = mm3(pe, PS[:, 7, 16 * t:16 * t + 16], left(k, t * P, t * P + P),
                                            pair(EH, EL, slice(None), l + k), k == 0, k == kt - 1)
                            m.then_inc(s["self"], 1)
                            pe.wait_ge(s["selfc"], l + 1)
                            for t in range(TT):
                                m = pe.transpose(PS[0:16, 6, t * P:t * P + P], SV[:, t, :], ident)
                            m.then_inc(s["nt"], 1)
                            for t in (0, 1, 3, 2):
                                if t == 2:
                                    pe.wait_ge(s["ns_lo"], l + 1)
                                    neighbours(0)
                                for k in range(kt):
                                    m = mm3(pe, PS[:, 4 + t, 0:256], left(k, t * P, t * P + P), weight("gat%d" % l, kt, k), k == 0, k == kt - 1)
                                m.then_inc(s["feat"], 1)
                            pe.wait_ge(s["featc"], TT * (l + 1))
                            for n in range(NG * l, NG * (l + 1)):
                                if n % NG == TT - 2:
                                    neighbours(1)
                                if n > NG * l:
                                    pe.wait_ge(s["pts_v"], n)
                                    warm(pe, WARM["group"], bank=4)
                                    pe.wait_ge(s["pts_a"], n)
                                pe.wait_ge(s["p"], n + 1)
                                for hh in range(4):
                                    for mt in range(2):
                                        m = pe.transpose(PS[:, 4 + hh // 2, (hh % 2) * 256 + mt * P:(hh % 2) * 256 + mt * P + P],
                                                         PR[:, n % 2, hh, mt * P:mt * P + P], ident)
                                m.then_inc(s["pt"], 1)
                                if n > NG * l:
                                    pv(n - 1)
                            pv(NG * (l + 1) - 1)
                            if l == 0:
                                pe.wait_ge(s["z"], NG)
                                warm(pe, WARM["elu"], bank=3)
                                transpose_tensor(pe, YM, s["h1"], s["tr1"])
                                warm(pe, WARM["split"], bank=3)

                    @block.scalar
                    def _(act):
                        for l in range(2):
                            def zs(n):
                                hg, t = divmod(n % NG, TT)
                                act.wait_ge(s["nb"], n // TT + 1)
                                act.wait_ge(s["selfc"], l + 1)
                                if n >= 2:
                                    act.wait_ge(s["lr"], n - 1)
                                for hh in range(4):
                                    i = act.activation(Z[:, n % 2, hh, :], PS[:, hh, (t // 2) * S:(t // 2 + 1) * S], ACT.Identity,
                                                       bias=SV[:, t, 4 * hg + hh:4 * hg + hh + 1])
                                i.then_inc(s["z"], 1)

                            def weights(n):
                                act.wait_ge(s["pt"], n + 1)
                                if n >= 2:
                                    act.wait_ge(s["pv"], n - 1)
                                act.activation(PTS[:, n % 2, 1].rearrange("p b c d -> p (b c d)"), PS[:, 5, :], ACT.Copy).then_inc(s["pts_a"], 1)

                            def elu(t):
                                act.wait_ge(s["y_m"], TT * l + t + 1)
                                act.activation(YM[:, t, :], YM[:, t, :], ACT.Exp).then_inc(s["y_e"], 1)
                                act.activation(YR[:, t, :], YR[:, t, :], ACT.Relu).then_inc(s["y_e"], 1)

                            act.wait_ge(s["self"], l + 1)
                            act.activation(SV[:, :, :], PS[:, 7, 0:16 * TT].rearrange("p (t h) -> p t h", t=TT), ACT.Copy).then_inc(s["selfc"], 1)
                            act.wait_ge(s["nt"], l + 1)
                            if l == 0:
                                act.wait_ge(s["nz"], 1)
                            act.activation(NS[0:16, :], PS[0:16, 6, :], ACT.Copy).then_inc(s["ns_hi"], 1)
                            zs(NG * l)
                            zs(NG * l + 1)
                            if l:
                                act.wait_ge(s["pv"], NG)
                            for t in range(TT):
                                act.wait_ge(s["feat"], TT * l + (1, 2, 4, 3)[t])
                                act.activation(FT[:, t, :, 0:GO], PS[:, 4 + t, 0:256].rearrange("p (h o) -> p h o", h=GH),
                                               ACT.Copy).then_inc(s["featc"], 1)
                            for n in range(NG * l, NG * (l + 1)):
                                if n > NG * l:
                                    weights(n - 1)
                                act.wait_ge(s["neg"], n + 1)
                                if n >= 2:
                                    act.wait_ge(s["pt"], n - 1)
                                for hh in range(4):
                                    i = act.activation(PR[:, n % 2, hh, :], E[:, n % 2, hh, :], ACT.Exp, bias=mx[:, n % 2, hh:hh + 1])
                                i.then_inc(s["p"], 1)
                                if n + 2 < NG * (l + 1):
                                    zs(n + 2)
                                if n % NG >= TT + 2:
                                    elu(n % NG - TT - 2)
                            weights(NG * (l + 1) - 1)
                            elu(TT - 2)
                            elu(TT - 1)
                            if l == 0:
                                split_scalar(act, s["hi1"], s["tr1"])

                    @block.vector
                    def _(v):
                        def neighbours_lo(l):
                            v.wait_ge(s["ns_hi"], l + 1)
                            v.tensor_tensor(NS[32:48, :], PS[0:16, 6, :], NS[0:16, :].bitcast(F32), ALU.subtract).then_inc(s["ns_lo"], 1)

                        v.memset(NS[:, :].bitcast(F32), 0.0).then_inc(s["nz"], 1)
                        ln_vector(v, s)
                        neighbours_lo(0)
                        for t in range(TT):
                            v.wait_ge(s["ln_norm"], t + 1)
                            v.tensor_scalar(BASE[:, t, :], HN[:, t, :], -1.0, 1.0, ALU.mult, ALU.add).then_inc(s["adj"], 1)
                        for t in range(TT):
                            v.wait_ge(s["adj"], t + 1)
                            v.tensor_scalar(BASE[:, t, :], BASE[:, t, :], -1.0e10, None, ALU.mult).then_inc(s["base"], 1)
                        v.tensor_copy(FT[:, :, :, GO:GO + 1], ones1[:, 0:32].rearrange("p (a b c) -> p a b c", a=TT, b=GH)).then_inc(s["one"], 1)
                        v.wait_ge(s["base"], TT)
                        v.wait_ge(s["one"], 1)
                        for l in range(2):
                            def scores(n):
                                hg, t = divmod(n % NG, TT)
                                b = n % 2
                                v.wait_ge(s["z"], n + 1)
                                if n >= 2:
                                    v.wait_ge(s["p"], n - 1)
                                v.scalar_tensor_tensor(E[:, b], Z[:, b], 0.2, Z[:, b], ALU.mult, ALU.max).then_inc(s["lr"], 1)
                                v.wait_ge(s["lr"], n + 1)
                                for hh in range(4):
                                    v.tensor_tensor_reduce(E[:, b, hh, :], E[:, b, hh, :], BASE[:, t, :], 1.0, -3.0e38,
                                                           ALU.add, ALU.max, mx[:, b, hh:hh + 1]).then_inc(s["e"], 1)
                                v.wait_ge(s["e"], 4 * (n + 1))
                                v.tensor_scalar(mx[:, b, :], mx[:, b, :], -1.0, None, ALU.mult).then_inc(s["neg"], 1)

                            def outputs(n):
                                hg, t = divmod(n % NG, TT)
                                b = n % 2
                                v.wait_ge(s["pv"], n + 1)
                                o = PS[:, 6 + b, 0:132].rearrange("p (h o) -> p h o", h=4)
                                v.reciprocal(rin[:, b, :], o[:, :, GO]).then_inc(s["o_r"], 1)
                                v.wait_ge(s["o_r"], n + 1)
                                v.tensor_tensor(O[:, t, 4 * hg:4 * hg + 4, :], o[:, :, 0:GO],
                                                rin[:, b, :].unsqueeze(2).broadcast_to([P, 4, GO]), ALU.mult).then_inc(s["o_c"], 1)
                                if hg:
                                    v.wait_ge(s["o_c"], n + 1)
                                    v.tensor_tensor(YR[:, t, :], O[:, t].rearrange("p h o -> p (h o)"), const("gb%d" % l), ALU.add).then_inc(s["y_b"], 1)
                                    if l:
                                        v.wait_ge(s["tr1"], 1)
                                    v.wait_ge(s["y_b"], TT * l + t + 1)
                                    v.tensor_scalar(YM[:, t, :], YR[:, t, :], 0.0, None, ALU.min).then_inc(s["y_m"], 1)

                            def elu(t):
                                v.wait_ge(s["y_e"], 2 * (TT * l + t + 1))
                                v.scalar_tensor_tensor(YM[:, t, :], YM[:, t, :], -1.0, YR[:, t, :], ALU.add, ALU.add).then_inc(s["h1"], 1)
                                if l:
                                    v.wait_ge(s["h1"], TT + t + 1)
                                    v.scalar_tensor_tensor(X[:, t, :], YM[:, t, :], gate[:, 0:1], X[:, t, :], ALU.mult, ALU.add).then_inc(s["y_x"], 1)
                                    stats_vector(v, s, t, "y_x", t + 1)

                            if l:
                                neighbours_lo(1)
                            scores(NG * l)
                            for n in range(NG * l, NG * (l + 1)):
                                if n + 1 < NG * (l + 1):
                                    scores(n + 1)
                                v.wait_ge(s["pt"], n + 1)
                                if n >= 2:
                                    v.wait_ge(s["pv"], n - 1)
                                v.tensor_copy(PTS[:, n % 2, 0].rearrange("p b c d -> p (b c d)"), PS[:, 4, :]).then_inc(s["pts_v"], 1)
                                if n > NG * l:
                                    outputs(n - 1)
                                if n % NG >= TT + 3:
                                    elu(n % NG - TT - 3)
                            elu(TT - 3)
                            outputs(NG * (l + 1) - 1)
                            elu(TT - 2)
                            elu(TT - 1)
                            if l == 0:
                                split_vector(v, s["hi1"], s["lo1"])
                        stats_done(v, s)

        def small_attention(layer):
            own = layer == 0
            with Phase() as ph:
                s = ph.sem(LN + "rms_sq rms_eps rms_rstd rms2_sq rms2_eps rms2_rstd scaled qk q_ab q_sum qk_hi qk_lo vp v_c one km_hi km_lo "
                           "sc mxd sub ex pt pts pv rec o_c tr2 hi2 lo2 proj res")
                HX = ph.sb("HX", [P, TT, C])
                QKH = ph.sb("QKH", [P, 4, TOK], F32R)
                QKL = ph.sb("QKL", [P, 4, TOK], F32R)
                KMH = ph.sb("KMH", [P, NH, S], F32R)
                KML = ph.sb("KML", [P, NH, S], F32R)
                V = ph.sb("V", [P, TT, NH, HD + 1])
                E = ph.sb("E", [P, 2, 768])
                PTS = ph.sb("PTS", [P, 2, 2, 384])
                mx = ph.sb("mx", [P, 2, 4])
                rin = ph.sb("rin", [P, 2, 4])
                CTX = HX[:, :, :].rearrange("p t (h d) -> p t h d", h=NH)
                RA = E[:, :, :].rearrange("p a b -> p (a b)")[:, 0:2 * TOK].rearrange("p (a b) -> p a b", a=2)
                RB = PTS[:, :, :, :].rearrange("p a b c -> p (a b c)")[:, 0:2 * TOK].rearrange("p (a b) -> p a b", a=2)
                NG = 2 * NH // 2
                scale = HD ** -0.5
                mask = const("headmask")
                wo = "o0" if own else "o3"

                ORDER = (2, 3, 0, 1)

                with nc.Block() as block:
                    @block.gpsimd
                    def _(g):
                        if own:
                            rms_gpsimd(g, s)
                        g.wait_ge(s["qk_hi"], 2)
                        for n in range(NG):
                            j, hp = divmod(n, NH // 2)
                            if j:
                                g.wait_ge(s["sc"], hp + 1)
                            for h in (2 * hp, 2 * hp + 1):
                                g.tensor_scalar(KMH[:, h, :], QKH[:, 2 + h // 8, j * S:(j + 1) * S].bitcast(F32),
                                                mask[:, h % 8:h % 8 + 1], 1.0, ALU.mult, ALU.mult).then_inc(s["km_hi"], 1)
                        if own:
                            rms_gpsimd(g, s, "rms2_sq", "rms2_eps", "rms2_rstd")
                        else:
                            stats_gpsimd(g, s)

                    @block.tensor
                    def _(pe):
                        warm(pe, WARM["own"] if own else WARM["att"])
                        transpose_tensor(pe, HX if own else HN, s["scaled"] if own else s["ln_norm"], s["tr_done"])
                        warm(pe, WARM["split"])
                        pe.wait_ge(s["tr_lo"], KC)
                        def values_in():
                            pe.wait_ge(s["qk_lo"], 1)
                            if own:
                                pe.wait_ge(s["q_ab"], 2)
                            for t in range(TT):
                                o = PS[:, t // 2, (t % 2) * C:(t % 2 + 1) * C]
                                if own:
                                    for k in range(KC):
                                        m = mm3(pe, o, pair(HH, HL, slice(None), k, slice(t * P, t * P + P)), weight("v0", KC, k), k == 0, k == KC - 1)
                                else:
                                    m = mm3(pe, o, (CTH[:, t * P:t * P + P], CTL[:, t * P:t * P + P]), weight("v3"))
                            m.then_inc(s["vp"], 1)

                        for p, i in enumerate(ORDER):
                            if own:
                                for r in range(2):
                                    lo = (i // 2) * 512 + r * 256 + (i % 2) * P
                                    for k in range(KC):
                                        m = mm3(pe, PS[:, 2 * p + r, :], weight("qk0", KC, k, lo, lo + P),
                                                pair(HH, HL, slice(None), k), k == 0, k == KC - 1)
                            else:
                                for k in range(KC if i < 2 else 1):
                                    w = weight("q3", KC, k, i * P, i * P + P) if i < 2 else weight("k3", 1, 0, (i - 2) * P, (i - 1) * P)
                                    r = pair(HH, HL, slice(None), k) if i < 2 else (CTH[:, :], CTL[:, :])
                                    m = mm3(pe, PS[:, 2 * p, :], w, r, k == 0, k == (KC if i < 2 else 1) - 1)
                            m.then_inc(s["qk"], 1)
                        values_in()
                        pe.wait_ge(s["qk_lo"], 4)

                        def scores(n):
                            j, hp = divmod(n, NH // 2)
                            b = 1 - n % 2
                            pe.wait_ge(s["km_hi"], 2 * (n + 1))
                            pe.wait_ge(s["km_lo"], 2 * (n + 1))
                            if n >= 2:
                                pe.wait_ge(s["sub"], 2 * (n - 1))
                            for qt in (1, 0):
                                nk = P * (qt + 1)
                                q0 = j * S + qt * P
                                o = PS[:, 2 * b + 1 - qt, 0:2 * nk].rearrange("p (h k) -> p h k", h=2)
                                mm3(pe, o, pair(QKH, QKL, slice(None), hp // 4, slice(q0, q0 + P)),
                                    pair(KMH, KML, slice(None), slice(2 * hp, 2 * hp + 2), slice(0, nk)), True, False, skip=True)
                                m = pe.matmul(o[:, :, nk - P:nk], identb[:, :], causalb[:, :].unsqueeze(1).broadcast_to([P, 2, P]),
                                              start=False, stop=True, skip_group_check=True)
                            m.then_inc(s["sc"], 1)

                        def values(n):
                            j, hp = divmod(n, NH // 2)
                            pe.wait_ge(s["pts"], n + 1)
                            if n >= 2:
                                pe.wait_ge(s["o_c"], n - 1)
                            for hh in range(2):
                                for qt in range(2):
                                    at = (2 * qt + hh) * (HD + 1)
                                    for kt in range(qt + 1):
                                        c = kt if qt else 2
                                        m = pe.matmul(PS[:, 6 + n % 2, at:at + HD + 1], PTS[:, n % 2, hh, c * P:c * P + P],
                                                      V[:, 2 * j + kt, 2 * hp + hh, :], start=(kt == 0), stop=(kt == qt))
                            m.then_inc(s["pv"], 1)

                        scores(0)
                        pe.wait_ge(s["v_c"], TT)
                        scores(1)
                        for n in range(NG):
                            pe.wait_ge(s["ex"], n + 1)
                            if n >= 1:
                                pe.wait_ge(s["pts"], n)
                            for hh in range(2):
                                for c, at in enumerate((hh * S, hh * S + P, 512 + hh * P)):
                                    m = pe.transpose(PS[:, 4 + hh, c * P:c * P + P], E[:, n % 2, at:at + P], ident)
                            m.then_inc(s["pt"], 1)
                            if n + 2 < NG:
                                scores(n + 2)
                            if n:
                                values(n - 1)
                        values(NG - 1)
                        pe.wait_ge(s["sub"], 2 * NG)
                        pe.wait_ge(s["o_c"], NG)
                        for t in range(TT):
                            for k in range(KC):
                                m = pe.transpose(PS[:, k, t * P:(t + 1) * P], CTX[:, t].rearrange("p h d -> p (h d)")[:, k * P:(k + 1) * P], ident)
                        m.then_inc(s["tr2"], 1)
                        pe.wait_ge(s["lo2"], KC)
                        for t in range(TT):
                            for k in range(KC):
                                m = mm3(pe, PS[:, 4 + t, 0:C], pair(HH, HL, slice(None), k, slice(t * P, t * P + P)), weight(wo, KC, k), k == 0, k == KC - 1)
                            m.then_inc(s["proj"], 1)

                    @block.scalar
                    def _(act):
                        if own:
                            rms_scalar(act, s, HN, s["ln_norm"], RA[:, 0, 0:C])
                            split_scalar(act, s["tr_hi"], s["tr_done"], scale=const("ln1"))
                        else:
                            split_scalar(act, s["tr_hi"], s["tr_done"])
                        def masks(n):
                            j, hp = divmod(n, NH // 2)
                            act.wait_ge(s["qk_lo"], 2)
                            if j:
                                act.wait_ge(s["sc"], hp + 1)
                            for h in (2 * hp, 2 * hp + 1):
                                act.activation(KML[:, h, :], QKL[:, 2 + h // 8, j * S:(j + 1) * S].bitcast(F32), ACT.Copy,
                                               scale=mask[:, h % 8:h % 8 + 1]).then_inc(s["km_lo"], 1)

                        for p, i in enumerate(ORDER):
                            if p == 3:
                                masks(0)
                                masks(1)
                            if own:
                                act.wait_ge(s["q_sum"], p + 1)
                                act.activation(QKH[:, i, :], RA[:, p % 2, :], ACT.Copy).then_inc(s["qk_hi"], 1)
                            else:
                                act.wait_ge(s["qk"], p + 1)
                                act.activation(QKH[:, i, :], PS[:, 2 * p, :], ACT.Copy).then_inc(s["qk_hi"], 1)

                        def exps(n):
                            act.wait_ge(s["sub"], 2 * (n + 1))
                            act.activation(E[:, n % 2, :], E[:, n % 2, :], ACT.Exp, scale=scale).then_inc(s["ex"], 1)

                        masks(2)
                        masks(3)
                        exps(0)
                        for n in range(NG):
                            if n + 1 < NG:
                                exps(n + 1)
                            act.wait_ge(s["pt"], n + 1)
                            if n >= 2:
                                act.wait_ge(s["pv"], n - 1)
                            act.activation(PTS[:, n % 2], PS[:, 4:6, 0:384], ACT.Copy).then_inc(s["pts"], 1)
                            if n + 4 < NG:
                                masks(n + 4)
                        split_scalar(act, s["hi2"], s["tr2"])
                        if own:
                            rms_scalar(act, s, XN, s["res"], RA[:, 0, 0:C], "rms2_sq")

                    @block.vector
                    def _(v):
                        ln_vector(v, s)
                        if own:
                            v.wait_ge(s["rms_rstd"], 1)
                            for t in range(TT):
                                v.tensor_scalar(HX[:, t, :], HN[:, t, :], rstd[:, t:t + 1], None, ALU.mult).then_inc(s["scaled"], 1)
                            split_vector(v, s["tr_hi"], s["tr_lo"], scale=const("ln1"))
                        else:
                            split_vector(v, s["tr_hi"], s["tr_lo"])
                        v.tensor_copy(V[:, :, :, HD:HD + 1], ones1[:, 0:64].rearrange("p (a b c) -> p a b c", a=TT, b=NH)).then_inc(s["one"], 1)
                        def low(p):
                            i = ORDER[p]
                            v.wait_ge(s["qk_hi"], p + 1)
                            src = RA[:, p % 2, :] if own else PS[:, 2 * p, :]
                            v.tensor_tensor(QKL[:, i, :], src, QKH[:, i, :].bitcast(F32), ALU.subtract).then_inc(s["qk_lo"], 1)

                        for p, i in enumerate(ORDER):
                            if own:
                                b = p % 2
                                v.wait_ge(s["qk"], p + 1)
                                if p >= 2:
                                    v.wait_ge(s["qk_lo"], p - 1)
                                for r, (dst, tab) in enumerate(((RA, "ropec"), (RB, "ropes"))):
                                    c = 4 * (i // 2) + 2 * r + i % 2
                                    v.scalar_tensor_tensor(dst[:, b, :].rearrange("p (j q) -> p j q", j=2),
                                                           PS[:, 2 * p + r, :].rearrange("p (j q) -> p j q", j=2),
                                                           const("qkb")[:, c:c + 1],
                                                           const(tab).unsqueeze(1).broadcast_to([P, 2, S]), ALU.add, ALU.mult).then_inc(s["q_ab"], 1)
                                v.wait_ge(s["q_ab"], 2 * (p + 1))
                                v.tensor_tensor(RA[:, b, :], RA[:, b, :], RB[:, b, :], ALU.add).then_inc(s["q_sum"], 1)
                            if p:
                                low(p - 1)
                        low(3)
                        def shift(n):
                            b = n % 2
                            v.wait_ge(s["sc"], n + 1)
                            q1 = PS[:, 2 * (1 - b), :].rearrange("p (h k) -> p h k", h=2)
                            q0 = PS[:, 2 * (1 - b) + 1, 0:256].rearrange("p (h k) -> p h k", h=2)
                            v.tensor_reduce(mx[:, b, 0:2], q1, AX.X, ALU.max).then_inc(s["mxd"], 1)
                            v.tensor_reduce(mx[:, b, 2:4], q0, AX.X, ALU.max).then_inc(s["mxd"], 1)
                            if n >= 2:
                                v.wait_ge(s["pt"], n - 1)
                            v.wait_ge(s["mxd"], 2 * n + 1)
                            v.tensor_tensor(E[:, b, 0:512].rearrange("p (h k) -> p h k", h=2), q1,
                                            mx[:, b, 0:2].unsqueeze(2).broadcast_to([P, 2, S]), ALU.subtract).then_inc(s["sub"], 1)
                            v.wait_ge(s["mxd"], 2 * n + 2)
                            v.tensor_tensor(E[:, b, 512:768].rearrange("p (h k) -> p h k", h=2), q0,
                                            mx[:, b, 2:4].unsqueeze(2).broadcast_to([P, 2, P]), ALU.subtract).then_inc(s["sub"], 1)

                        def outputs(n):
                            j, hp = divmod(n, NH // 2)
                            b = n % 2
                            v.wait_ge(s["pv"], n + 1)
                            o = PS[:, 6 + b, 0:4 * (HD + 1)].rearrange("p (a d) -> p a d", a=4)
                            v.reciprocal(rin[:, b, :], o[:, :, HD]).then_inc(s["rec"], 1)
                            v.wait_ge(s["rec"], n + 1)
                            v.tensor_tensor(CTX[:, 2 * j:2 * j + 2, 2 * hp:2 * hp + 2, :],
                                            o[:, :, 0:HD].rearrange("p (q h) d -> p q h d", q=2),
                                            rin[:, b, :].rearrange("p (q h) -> p q h", q=2).unsqueeze(3).broadcast_to([P, 2, 2, HD]),
                                            ALU.mult).then_inc(s["o_c"], 1)

                        v.wait_ge(s["vp"], 1)
                        for t in range(TT):
                            src = PS[:, t // 2, (t % 2) * C:(t % 2 + 1) * C].rearrange("p (h d) -> p h d", h=NH)
                            if own:
                                v.tensor_tensor(V[:, t, :, 0:HD], src, const("bv0").rearrange("p (h d) -> p h d", h=NH), ALU.add).then_inc(s["v_c"], 1)
                            else:
                                v.tensor_copy(V[:, t, :, 0:HD], src).then_inc(s["v_c"], 1)
                        shift(0)
                        for n in range(NG):
                            if n + 1 < NG:
                                shift(n + 1)
                            if n >= 2:
                                outputs(n - 2)
                        outputs(NG - 2)
                        outputs(NG - 1)
                        split_vector(v, s["hi2"], s["lo2"])
                        for t in range(TT):
                            v.wait_ge(s["proj"], t + 1)
                            if own:
                                v.tensor_tensor(XN[:, t, :], PS[:, 4 + t, 0:C], HN[:, t, :], ALU.add).then_inc(s["res"], 1)
                            else:
                                v.scalar_tensor_tensor(X[:, t, :], PS[:, 4 + t, 0:C], gate[:, 6:7], X[:, t, :], ALU.mult, ALU.add).then_inc(s["res"], 1)
                                stats_vector(v, s, t, "res", t + 1)
                        if not own:
                            stats_done(v, s)

        def experts(layer):
            tiles = {0: T0, 2: T2, 3: T3}[layer]
            glu = layer != 2
            src = {0: "moe0", 2: "ffn2", 3: "moe3"}[layer]
            WC = 896 if glu else 640
            UP, DOWN, SEL = (256, 512, 768) if glu else (0, 256, 512)
            RAW, RING, LAG = 3, 4, 2
            with Phase() as ph:
                w_in = ph.sems("w_in", RAW)
                s = ph.sem(LN + "scaled lg smx ssub sexp ssum rank g_z g_set g_ok gtr g_hi g_lo "
                           "w_hi w_lo gu gs pre silu au ag a_hi a_lo dn dn_t y_t y_x")
                HX = ph.sb("HX", [P, TT, C])
                junk = ph.sb("junk", [P, 1])
                raw = ph.sb("raw", [P, RAW, WC])
                WMH = ph.sb("WMH", [P, RING, WC], F32R)
                WML = ph.sb("WML", [P, RING, SEL], F32R)
                LG = ph.sb("LG", [P, TT, 16])
                RK = ph.sb("RK", [P, 3, TT, NE, NE])
                G = ph.sb("G", [P, TT, 16])
                sm = ph.sb("sm", [P, 3, TT])
                GS = ph.sb("GS", [P, TOK], F32R)
                SG = ph.sb("SG", [P, 2, TOK])
                A = ph.sb("A", [P, 2, TOK])
                AHI = ph.sb("AHI", [P, 3, TOK], F32R)
                ALO = ph.sb("ALO", [P, 3, TOK], F32R)
                NL = 16 if layer == 0 else 8

                with nc.Block() as block:
                    @block.sync
                    def _(sp):
                        for i in range(tiles):
                            if i >= RAW:
                                sp.wait_ge(s["w_hi"], i - RAW + 1)
                                sp.wait_ge(s["w_lo"], i - RAW + 1)
                            sp.dma_start(raw[:, i % RAW, :], a[src][i][:, 0:WC]).then_inc(w_in[i % RAW], 16)

                    @block.gpsimd
                    def _(g):
                        for i in range(tiles):
                            g.wait_ge(s["w_hi"], i + 1)
                            if i >= RING:
                                g.wait_ge(s["dn"], i - RING + 1)
                            g.tensor_tensor(WML[:, i % RING, :], raw[:, i % RAW, 0:SEL], WMH[:, i % RING, 0:SEL].bitcast(F32),
                                            ALU.subtract).then_inc(s["w_lo"], 1)
                        if layer != 3:
                            stats_gpsimd(g, s)

                    @block.tensor
                    def _(pe):
                        warm(pe, WARM["rms"] if layer == 0 else WARM["att"])
                        transpose_tensor(pe, HX if layer == 0 else HN, s["scaled"] if layer == 0 else s["ln_norm"], s["tr_done"])
                        warm(pe, WARM["split"])
                        pe.wait_ge(s["tr_lo"], KC)
                        if glu:
                            for t in range(TT):
                                for k in range(KC):
                                    m = mm3(pe, PS[:, 7, t * 16:t * 16 + NL], pair(HH, HL, slice(None), k, slice(t * P, t * P + P)),
                                            weight("rt%d" % layer, KC, k), k == 0, k == KC - 1)
                            m.then_inc(s["lg"], 1)

                        def gates():
                            pe.wait_ge(s["g_ok"], 1)
                            for t in range(TT):
                                m = pe.transpose(PS[0:16, 6, t * P:t * P + P], G[:, t, :], ident)
                            m.then_inc(s["gtr"], 1)
                            pe.wait_ge(s["g_lo"], 1)

                        def hidden(i):
                            b, w = i % 2, i % RING
                            pe.wait_ge(s["w_hi"], i + 1)
                            pe.wait_ge(s["w_lo"], i + 1)
                            if i >= 2:
                                pe.wait_ge(s["ag"], i - 1)
                            for k in range(KC):
                                m = mm3(pe, PS[:, b, :], pair(WMH, WML, slice(None), w, slice(k * P, k * P + P)),
                                        pair(HH, HL, slice(None), k), k == 0, k == KC - 1)
                            if glu:
                                for k in range(KC):
                                    m = mm3(pe, PS[:, 2 + b, :], pair(WMH, WML, slice(None), w, slice(UP + k * P, UP + k * P + P)),
                                            pair(HH, HL, slice(None), k), k == 0, k == KC - 1)
                            m.then_inc(s["gu"], 1)

                        def gate_columns(i):
                            pe.matmul(PS[:, 4 + i % 2, :], WMH[:, i % RING, SEL:SEL + P], GS[:, :], start=True, stop=True).then_inc(s["gs"], 1)

                        def down(i):
                            pe.wait_ge(s["a_lo"], i + 1)
                            for t in range(TT):
                                m = mm3(pe, PS[:, 6 + t // 2, (t % 2) * C:(t % 2 + 1) * C], pair(AHI, ALO, slice(None), i % 3, slice(t * P, t * P + P)),
                                        pair(WMH, WML, slice(None), i % RING, slice(DOWN, DOWN + C)), i == 0 and t % 2 == 0, i == tiles - 1, skip=True)
                                if i == tiles - 1 and t % 2:
                                    m.then_inc(s["dn_t"], 2)
                            if i < tiles - 1:
                                m.then_inc(s["dn"], 1)

                        for i in range(tiles + LAG):
                            if i < tiles:
                                hidden(i)
                            if glu and i == 1:
                                gates()
                                gate_columns(0)
                            if glu and 1 <= i < tiles:
                                gate_columns(i)
                            if i >= LAG:
                                down(i - LAG)

                    @block.scalar
                    def _(act):
                        def weights(i):
                            act.wait_ge(w_in[i % RAW], 16 * (i // RAW + 1))
                            if i >= RING:
                                act.wait_ge(s["dn"], i - RING + 1)
                            act.activation(WMH[:, i % RING, :], raw[:, i % RAW, :], ACT.Copy).then_inc(s["w_hi"], 1)

                        def silu(i):
                            act.wait_ge(s["gu"], i + 1)
                            if i >= 2:
                                act.wait_ge(s["au"], i - 1)
                            act.activation(SG[:, i % 2, :], PS[:, i % 2, :], ACT.Silu).then_inc(s["silu"], 1)

                        if layer == 0:
                            split_scalar(act, s["tr_hi"], s["tr_done"], scale=const("ln2"))
                        else:
                            split_scalar(act, s["tr_hi"], s["tr_done"])
                        for i in range(RAW):
                            weights(i)
                        if layer == 0:
                            act.wait_ge(s["ssub"], 1)
                            act.activation(LG[:, :, 0:8], LG[:, :, 0:8], ACT.Exp).then_inc(s["sexp"], 1)
                            act.activation(LG[:, :, 8:9], LG[:, :, 8:9], ACT.Exp, scale=-1.0).then_inc(s["sexp"], 1)
                        elif layer == 3:
                            act.wait_ge(s["lg"], 1)
                            act.activation(LG[:, :, 0:8], PS[:, 7, 0:64].rearrange("p (t e) -> p t e", t=TT)[:, :, 0:8],
                                           ACT.Exp, scale=-1.0).then_inc(s["sexp"], 1)
                        if glu:
                            act.activation(junk[:, 0:1], ones1[:, 0:1], ACT.Silu).then_inc(s["pre"], 1)
                            silu(0)
                            silu(1)
                            act.wait_ge(s["gtr"], 1)
                            act.wait_ge(s["g_z"], 1 + TT)
                            act.activation(GS[0:16, :], PS[0:16, 6, :], ACT.Copy).then_inc(s["g_hi"], 1)
                        for i in range(tiles):
                            b = i % 2
                            if glu:
                                if i >= 2:
                                    silu(i)
                            else:
                                act.wait_ge(s["gu"], i + 1)
                                if i >= 2:
                                    act.wait_ge(s["a_lo"], i - 1)
                                act.activation(A[:, b, :], PS[:, b, :], ACT.Gelu, bias=const("b1f")[:, i:i + 1]).then_inc(s["ag"], 1)
                            if 1 <= i < tiles - 2:
                                weights(i + 2)
                            act.wait_ge(s["ag"], i + 1)
                            if i >= 3:
                                act.wait_ge(s["dn"], i - 2)
                            act.activation(AHI[:, i % 3, :], A[:, b, :], ACT.Copy).then_inc(s["a_hi"], 1)

                    @block.vector
                    def _(v):
                        if layer == 0:
                            for t in range(TT):
                                v.tensor_scalar(HX[:, t, :], XN[:, t, :], rstd[:, t:t + 1], None, ALU.mult).then_inc(s["scaled"], 1)
                            split_vector(v, s["tr_hi"], s["tr_lo"], scale=const("ln2"))
                        else:
                            ln_vector(v, s)
                            split_vector(v, s["tr_hi"], s["tr_lo"])
                        v.memset(GS[:, :].bitcast(F32), 0.0).then_inc(s["g_z"], 1)
                        for t in range(TT):
                            v.memset(G[:, t, :], 0.0).then_inc(s["g_z"], 1)

                        def factor(t):
                            return {0: gate[:, 1:2], 2: COEF2[:, t:t + 1], 3: gate[:, 7:8]}[layer]

                        if layer != 3:
                            for t in range(TT):
                                v.scalar_tensor_tensor(X[:, t, :], XN[:, t, :] if layer == 0 else const("b2f"), factor(t), X[:, t, :],
                                                       ALU.mult, ALU.add).then_inc(s["y_t"], 1)
                        lgp = PS[:, 7, 0:64].rearrange("p (t e) -> p t e", t=TT)

                        def wide(x):
                            return x.unsqueeze(2).broadcast_to([P, TT, NE])

                        if layer == 0:
                            v.wait_ge(s["lg"], 1)
                            v.tensor_reduce(sm[:, 0, :], lgp[:, :, 0:8], AX.X, ALU.max).then_inc(s["smx"], 1)
                            v.tensor_copy(LG[:, :, 8:9], lgp[:, :, 8:9]).then_inc(s["smx"], 1)
                            v.wait_ge(s["smx"], 2)
                            v.tensor_tensor(LG[:, :, 0:8], lgp[:, :, 0:8], wide(sm[:, 0, :]), ALU.subtract).then_inc(s["ssub"], 1)
                            v.wait_ge(s["sexp"], 2)
                            v.tensor_reduce(sm[:, 1, :], LG[:, :, 0:8], AX.X, ALU.add).then_inc(s["ssum"], 1)
                            v.tensor_scalar(LG[:, :, 8:9], LG[:, :, 8:9], 1.0, None, ALU.add).then_inc(s["ssum"], 1)
                            v.wait_ge(s["ssum"], 2)
                            v.reciprocal(sm[:, 2, :], sm[:, 1, :]).then_inc(s["ssum"], 1)
                            v.wait_ge(s["ssum"], 3)
                            v.wait_ge(s["g_z"], 1 + TT)
                            v.reciprocal(G[:, :, 8:9], LG[:, :, 8:9]).then_inc(s["g_set"], 1)
                            v.tensor_tensor(LG[:, :, 0:8], LG[:, :, 0:8], wide(sm[:, 2, :]), ALU.mult).then_inc(s["ssum"], 1)
                            v.wait_ge(s["ssum"], 4)
                            rank, n = rank_vector(v, s, RK, LG[:, :, 0:8], 0)
                            v.scalar_tensor_tensor(G[:, :, 0:8], rank, 2.0, LG[:, :, 0:8], ALU.is_lt, ALU.mult).then_inc(s["g_set"], 1)
                            v.wait_ge(s["g_set"], 2)
                            v.tensor_copy(G[:, :, 15:16], G[:, :, 14:15]).then_inc(s["g_ok"], 1)
                        elif layer == 3:
                            v.wait_ge(s["sexp"], 1)
                            v.tensor_scalar(LG[:, :, 0:8], LG[:, :, 0:8], 1.0, None, ALU.add).then_inc(s["ssum"], 1)
                            v.wait_ge(s["ssum"], 1)
                            v.reciprocal(LG[:, :, 0:8], LG[:, :, 0:8]).then_inc(s["ssum"], 1)
                            v.wait_ge(s["ssum"], 2)
                            v.tensor_tensor(LG[:, :, 8:16], LG[:, :, 0:8], const("gbias3").unsqueeze(1).broadcast_to([P, TT, NE]), ALU.add).then_inc(s["ssum"], 1)
                            v.wait_ge(s["ssum"], 3)
                            rank, n = rank_vector(v, s, RK, LG[:, :, 8:16], 0)
                            v.scalar_tensor_tensor(LG[:, :, 0:8], rank, 2.0, LG[:, :, 0:8], ALU.is_lt, ALU.mult).then_inc(s["ssum"], 1)
                            v.wait_ge(s["ssum"], 4)
                            v.tensor_reduce(sm[:, 0, :], LG[:, :, 0:8], AX.X, ALU.add).then_inc(s["ssum"], 1)
                            v.wait_ge(s["ssum"], 5)
                            v.reciprocal(sm[:, 1, :], sm[:, 0, :]).then_inc(s["ssum"], 1)
                            v.wait_ge(s["ssum"], 6)
                            v.wait_ge(s["g_z"], 1 + TT)
                            v.tensor_tensor(G[:, :, 0:8], LG[:, :, 0:8], wide(sm[:, 1, :]), ALU.mult).then_inc(s["g_set"], 1)
                            v.tensor_copy(G[:, :, 8:9], ones1[:, 0:TT].unsqueeze(2)).then_inc(s["g_set"], 1)
                            v.wait_ge(s["g_set"], 2)
                            v.tensor_copy(G[:, :, 15:16], G[:, :, 14:15]).then_inc(s["g_ok"], 1)
                        if glu:
                            v.wait_ge(s["g_hi"], 1)
                            v.tensor_tensor(GS[32:48, :], PS[0:16, 6, :], GS[0:16, :].bitcast(F32), ALU.subtract).then_inc(s["g_lo"], 1)
                        for i in range(tiles):
                            b = i % 2
                            if glu:
                                v.wait_ge(s["silu"], i + 1)
                                v.tensor_tensor(SG[:, b, :], SG[:, b, :], PS[:, 2 + b, :], ALU.mult).then_inc(s["au"], 1)
                                if i >= 2:
                                    v.wait_ge(s["a_lo"], i - 1)
                                v.wait_ge(s["au"], i + 1)
                                v.wait_ge(s["gs"], i + 1)
                                v.tensor_tensor(A[:, b, :], SG[:, b, :], PS[:, 4 + b, :], ALU.mult).then_inc(s["ag"], 1)
                            v.wait_ge(s["a_hi"], i + 1)
                            if i >= 3:
                                v.wait_ge(s["dn"], i - 2)
                            v.tensor_tensor(ALO[:, i % 3, :], A[:, b, :], AHI[:, i % 3, :].bitcast(F32), ALU.subtract).then_inc(s["a_lo"], 1)
                        for t in range(TT):
                            v.wait_ge(s["dn_t"], t + 1)
                            if layer != 3:
                                v.wait_ge(s["y_t"], t + 1)
                            y = PS[:, 6 + t // 2, (t % 2) * C:(t % 2 + 1) * C]
                            v.scalar_tensor_tensor(X[:, t, :], y, factor(t), X[:, t, :], ALU.mult, ALU.add).then_inc(s["y_x"], 1)
                        if layer != 3:
                            for t in range(TT):
                                stats_vector(v, s, t, "y_x", t + 1)
                            stats_done(v, s)

        def latent_attention(pi):
            with Phase() as ph:
                s = ph.sem(LN + "kv_ab kv_r kv2 kvt kb_hi kb_lo qp q_hi q_lo sc mxd sub ex pt pts pv rec o_c ct c_hi c_lo proj res")
                KV = CTN[:, bass.ts(pi, TT), :]
                KA = ph.sb("KA", [P, TT, DC])
                KB = ph.sb("KB", [P, TT, DC])
                KV2 = ph.sb("KV2", [P, TT, 2 * DC + 2])
                KBH = ph.sb("KBH", [P, 2, TOK], F32R)
                KBL = ph.sb("KBL", [P, 2, TOK], F32R)
                QH = ph.sb("QH", [P, 8, TOK], F32R)
                QL = ph.sb("QL", [P, 8, TOK], F32R)
                E = [XN[:, :, :].rearrange("p t c -> p (t c)"), HN[:, :, :].rearrange("p t c -> p (t c)")]
                PTS = ph.sb("PTS", [P, 2, 1024])
                mx = ph.sb("mx", [P, 2, 4])
                rin = ph.sb("rin", [P, 2, 4])
                CTX = ph.sb("CTX", [P, TT, MH, DC])
                MT = MH // 2
                NG = 2 * MT

                with nc.Block() as block:
                    @block.gpsimd
                    def _(g):
                        stats_gpsimd(g, s)

                    @block.tensor
                    def _(pe):
                        transpose_tensor(pe, KV2, s["kv2"], s["kvt"], bank=2, tiles=1)
                        warm(pe, WARM["latent"])
                        transpose_tensor(pe, HN, s["ln_norm"], s["tr_done"])
                        warm(pe, WARM["split"])
                        pe.wait_ge(s["tr_lo"], KC)
                        pe.wait_ge(s["kb_lo"], 2)
                        for m in range(MT):
                            for k in range(KC):
                                i = mm3(pe, PS[:, m, :], pair(AH, AL, slice(None), k, slice(m * P, m * P + P)),
                                        pair(HH, HL, slice(None), k), k == 0, k == KC - 1)
                            i.then_inc(s["qp"], 1)

                        def scores(n):
                            j, m = divmod(n, MT)
                            b = n % 2
                            pe.wait_ge(s["q_lo"], m + 1 if j == 0 and n >= 2 else 4 if j == 0 else MT)
                            if n >= 2:
                                pe.wait_ge(s["sub"], n - 1)
                            for qt in range(2):
                                for hh in range(2):
                                    q0 = j * S + qt * P
                                    i = mm3(pe, PS[:, 2 * b + qt, hh * S:hh * S + S], pair(QH, QL, slice(None), m, slice(q0, q0 + P)),
                                            pair(KBH, KBL, slice(None), hh, slice(j * S, j * S + S)))
                            i.then_inc(s["sc"], 1)

                        def values(n):
                            j, m = divmod(n, MT)
                            pe.wait_ge(s["pts"], n + 1)
                            if n >= 2:
                                pe.wait_ge(s["o_c"], n - 1)
                            for qt in range(2):
                                for hh in range(2):
                                    at = (2 * qt + hh) * (DC + 1)
                                    for kt in range(2):
                                        c = qt * 512 + hh * S + kt * P
                                        i = pe.matmul(PS[:, 6 + n % 2, at:at + DC + 1], PTS[:, n % 2, c:c + P],
                                                      KV2[:, 2 * j + kt, DC:2 * DC + 1], start=(kt == 0), stop=(kt == 1))
                            i.then_inc(s["pv"], 1)

                        scores(0)
                        scores(1)
                        pe.wait_ge(s["q_lo"], MT)
                        for n in range(NG):
                            pe.wait_ge(s["ex"], n + 1)
                            if n >= 1:
                                pe.wait_ge(s["pts"], n)
                            for qt in range(2):
                                for c in range(4):
                                    i = pe.transpose(PS[:, 4 + qt, c * P:c * P + P], E[n % 2][:, qt * 512 + c * P:qt * 512 + c * P + P], ident)
                            i.then_inc(s["pt"], 1)
                            if n + 2 < NG:
                                scores(n + 2)
                            if n:
                                values(n - 1)
                        values(NG - 1)
                        pe.wait_ge(s["sub"], NG)
                        pe.wait_ge(s["o_c"], NG)
                        for m in range(MT):
                            if m >= 4:
                                pe.wait_ge(s["c_lo"], m - 3)
                            for t in range(TT):
                                i = pe.transpose(PS[:, m % 4, t * P:t * P + P], CTX[:, t].rearrange("p h d -> p (h d)")[:, m * P:m * P + P], ident)
                            i.then_inc(s["ct"], 1)
                        pe.wait_ge(s["c_lo"], MT)
                        for t in range(TT):
                            for m in range(MT):
                                i = mm3(pe, PS[:, 4 + t, 0:C], pair(QH, QL, slice(None), m, slice(t * P, t * P + P)),
                                        pair(BH, BL, slice(None), m), m == 0, m == MT - 1)
                            i.then_inc(s["proj"], 1)

                    @block.scalar
                    def _(act):
                        act.wait_ge(s["kvt"], 1)
                        for r in range(2):
                            act.activation(KBH[:, r, :], PS[:, 2, :], ACT.Copy, scale=const("halfmask")[:, r:r + 1]).then_inc(s["kb_hi"], 1)
                        split_scalar(act, s["tr_hi"], s["tr_done"])
                        for m in range(MT):
                            act.wait_ge(s["qp"], m + 1)
                            act.activation(QH[:, m, :], PS[:, m, :], ACT.Copy).then_inc(s["q_hi"], 1)

                        def exps(n):
                            act.wait_ge(s["sub"], n + 1)
                            act.activation(E[n % 2], E[n % 2], ACT.Exp).then_inc(s["ex"], 1)

                        exps(0)
                        for n in range(NG):
                            if n + 1 < NG:
                                exps(n + 1)
                            act.wait_ge(s["pt"], n + 1)
                            if n >= 2:
                                act.wait_ge(s["pv"], n - 1)
                            act.activation(PTS[:, n % 2, :], PS[:, 4:6, :].rearrange("p a b -> p (a b)"), ACT.Copy).then_inc(s["pts"], 1)
                        for m in range(MT):
                            act.wait_ge(s["ct"], m + 1)
                            act.activation(QH[:, m, :], PS[:, m % 4, :], ACT.Copy).then_inc(s["c_hi"], 1)

                    @block.vector
                    def _(v):
                        ln_vector(v, s)
                        H = DC // 2
                        for j in range(2):
                            kv = KV[:, 2 * j:2 * j + 2, :]
                            cos = const("kvc").rearrange("p (q d) -> p q d", q=2)
                            sin = const("kvs").rearrange("p (q d) -> p q d", q=2)
                            v.tensor_tensor(KA[:, 2 * j:2 * j + 2, :], kv, cos, ALU.mult).then_inc(s["kv_ab"], 1)
                            v.tensor_tensor(KB[:, 2 * j:2 * j + 2, 0:H], kv[:, :, H:DC], sin[:, :, 0:H], ALU.mult).then_inc(s["kv_ab"], 1)
                            v.tensor_tensor(KB[:, 2 * j:2 * j + 2, H:DC], kv[:, :, 0:H], sin[:, :, H:DC], ALU.mult).then_inc(s["kv_ab"], 1)
                        v.tensor_copy(KV2[:, :, 2 * DC:2 * DC + 1], ones1[:, 0:TT].unsqueeze(2)).then_inc(s["kv_r"], 1)
                        v.wait_ge(s["kv_ab"], 6)
                        v.tensor_tensor(KV2[:, :, 0:DC], KA[:, :, :], KB[:, :, :], ALU.add).then_inc(s["kv_r"], 1)
                        v.tensor_tensor(KV2[:, :, DC:2 * DC], KA[:, :, :], KB[:, :, :], ALU.add).then_inc(s["kv_r"], 1)
                        v.wait_ge(s["kv_r"], 3)
                        v.nop().then_inc(s["kv2"], TT)
                        for r in range(2):
                            v.wait_ge(s["kb_hi"], r + 1)
                            if r == 0:
                                v.wait_ge(s["kb_hi"], 2)
                            v.scalar_tensor_tensor(KBL[:, r, :], PS[:, 2, :], const("halfmask")[:, r:r + 1], KBH[:, r, :].bitcast(F32),
                                                   ALU.mult, ALU.subtract).then_inc(s["kb_lo"], 1)
                        split_vector(v, s["tr_hi"], s["tr_lo"])
                        for m in range(MT):
                            v.wait_ge(s["q_hi"], m + 1)
                            v.tensor_tensor(QL[:, m, :], PS[:, m, :], QH[:, m, :].bitcast(F32), ALU.subtract).then_inc(s["q_lo"], 1)

                        def shift(n):
                            b = n % 2
                            v.wait_ge(s["sc"], n + 1)
                            sc = PS[:, 2 * b:2 * b + 2, :].rearrange("p a (h k) -> p (a h) k", h=2)
                            v.tensor_reduce(mx[:, b, :], sc, AX.X, ALU.max).then_inc(s["mxd"], 1)
                            if n >= 2:
                                v.wait_ge(s["pt"], n - 1)
                            v.wait_ge(s["mxd"], n + 1)
                            v.tensor_tensor(E[b].rearrange("p (a k) -> p a k", a=4), sc,
                                            mx[:, b, :].unsqueeze(2).broadcast_to([P, 4, S]), ALU.subtract).then_inc(s["sub"], 1)

                        def outputs(n):
                            j, m = divmod(n, MT)
                            b = n % 2
                            v.wait_ge(s["pv"], n + 1)
                            o = PS[:, 6 + b, 0:4 * (DC + 1)].rearrange("p (a d) -> p a d", a=4)
                            v.reciprocal(rin[:, b, :], o[:, :, DC]).then_inc(s["rec"], 1)
                            v.wait_ge(s["rec"], n + 1)
                            v.tensor_tensor(CTX[:, 2 * j:2 * j + 2, 2 * m:2 * m + 2, :],
                                            o[:, :, 0:DC].rearrange("p (q h) d -> p q h d", q=2),
                                            rin[:, b, :].rearrange("p (q h) -> p q h", q=2).unsqueeze(3).broadcast_to([P, 2, 2, DC]),
                                            ALU.mult).then_inc(s["o_c"], 1)

                        shift(0)
                        for n in range(NG):
                            if n + 1 < NG:
                                shift(n + 1)
                            if n >= 2:
                                outputs(n - 2)
                        outputs(NG - 2)
                        outputs(NG - 1)
                        for m in range(MT):
                            v.wait_ge(s["c_hi"], m + 1)
                            v.tensor_tensor(QL[:, m, :], PS[:, m % 4, :], QH[:, m, :].bitcast(F32), ALU.subtract).then_inc(s["c_lo"], 1)
                        for t in range(TT):
                            v.wait_ge(s["proj"], t + 1)
                            v.scalar_tensor_tensor(X[:, t, :], PS[:, 4 + t, 0:C], gate[:, 2:3], X[:, t, :], ALU.mult, ALU.add).then_inc(s["res"], 1)
                            stats_vector(v, s, t, "res", t + 1)
                        stats_done(v, s)

        def low_rank():
            with Phase() as ph:
                s = ph.sem(LN + "pr ex la lr lb top mr ne sp su rs ga mz mt m_hi m_lo lo_ res")
                L = ph.sb("L", [P, TT, 32])
                LB = ph.sb("LB", [P, TT, LR])
                LM = ph.sb("LM", [P, TT, LR])
                top = ph.sb("top", [P, TT, 8])
                sm = ph.sb("sm", [P, 2, TT])
                M = ph.sb("M", [P, TT, P])
                MHI = ph.sb("MHI", [P, 1, TOK], F32R)
                MLO = ph.sb("MLO", [P, 1, TOK], F32R)
                with nc.Block() as block:
                    @block.gpsimd
                    def _(g):
                        g.memset(M[:, :, LR:P], 0.0).then_inc(s["mz"], 1)
                        stats_gpsimd(g, s)

                    @block.tensor
                    def _(pe):
                        transpose_tensor(pe, HN, s["ln_norm"], s["tr_done"])
                        pe.wait_ge(s["tr_lo"], KC)
                        for t in range(TT):
                            for k in range(KC):
                                m = mm3(pe, PS[:, 4 + t, 0:352], pair(HH, HL, slice(None), k, slice(t * P, t * P + P)),
                                        weight("l1f", KC, k), k == 0, k == KC - 1)
                            m.then_inc(s["pr"], 1)
                        pe.wait_ge(s["mz"], 1)
                        transpose_tensor(pe, M, s["ga"], s["mt"], bank=2, tiles=1)
                        pe.wait_ge(s["m_lo"], 1)
                        for t in range(TT):
                            mm3(pe, PS[:, t % 2, (t // 2) * C:(t // 2 + 1) * C], (MHI[:, 0, t * P:t * P + P], MLO[:, 0, t * P:t * P + P]),
                                weight("l1b")).then_inc(s["lo_"], 1)

                    @block.scalar
                    def _(act):
                        split_scalar(act, s["tr_hi"], s["tr_done"])
                        for t in range(TT):
                            act.wait_ge(s["pr"], t + 1)
                            act.activation(L[:, t, :], PS[:, 4 + t, 320:352], ACT.Exp, scale=-1.0).then_inc(s["ex"], 1)
                        split_scalar(act, s["m_hi"], s["mt"], bank=2, hh=MHI, tiles=1)

                    @block.vector
                    def _(v):
                        ln_vector(v, s)
                        split_vector(v, s["tr_hi"], s["tr_lo"])
                        v.wait_ge(s["ex"], TT)
                        v.tensor_scalar(L[:, :, :], L[:, :, :], 1.0, None, ALU.add).then_inc(s["la"], 1)
                        v.wait_ge(s["la"], 1)
                        v.reciprocal(L[:, :, :], L[:, :, :]).then_inc(s["lr"], 1)
                        v.wait_ge(s["lr"], 1)
                        for t in range(TT):
                            v.tensor_tensor(LB[:, t, :].rearrange("p (a b) -> p a b", b=2), L[:, t, :].unsqueeze(2).broadcast_to([P, 32, 2]),
                                            const("lora_b").rearrange("p (a b) -> p a b", b=2), ALU.add).then_inc(s["lb"], 1)
                        for t in range(TT):
                            v.wait_ge(s["lb"], t + 1)
                            v.max(top[:, t, :], LB[:, t, :]).then_inc(s["top"], 1)
                        for t in range(TT):
                            v.wait_ge(s["top"], t + 1)
                            v.match_replace(LM[:, t, :], top[:, t, :], LB[:, t, :], -3.0e38).then_inc(s["mr"], 1)
                        v.wait_ge(s["mr"], TT)
                        v.tensor_tensor(LM[:, :, :], LM[:, :, :], LB[:, :, :], ALU.not_equal).then_inc(s["ne"], 1)
                        v.wait_ge(s["ne"], 1)
                        v.tensor_tensor(LM[:, :, :], LM[:, :, :], LB[:, :, :], ALU.mult).then_inc(s["sp"], 1)
                        v.wait_ge(s["sp"], 1)
                        v.tensor_reduce(sm[:, 0, :], LM[:, :, :], AX.X, ALU.add).then_inc(s["su"], 1)
                        v.wait_ge(s["su"], 1)
                        v.reciprocal(sm[:, 1, :], sm[:, 0, :]).then_inc(s["su"], 1)
                        v.wait_ge(s["su"], 2)
                        v.tensor_scalar(sm[:, 1, :], sm[:, 1, :], 8.0 * 2.0, None, ALU.mult).then_inc(s["rs"], 1)
                        v.wait_ge(s["rs"], 1)
                        for t in range(TT):
                            v.scalar_tensor_tensor(M[:, t, 0:LR], LM[:, t, :], sm[:, 1, t:t + 1], PS[:, 4 + t, 256:320],
                                                   ALU.mult, ALU.mult).then_inc(s["ga"], 1)
                        split_vector(v, s["m_hi"], s["m_lo"], bank=2, hh=MHI, hl=MLO, tiles=1)
                        for t in range(TT):
                            v.scalar_tensor_tensor(X[:, t, :], PS[:, 4 + t, 0:C], gate[:, 3:4], X[:, t, :], ALU.mult, ALU.add).then_inc(s["res"], 1)
                        v.wait_ge(s["lo_"], TT)
                        v.wait_ge(s["res"], TT)
                        for t in range(TT):
                            v.scalar_tensor_tensor(X[:, t, :], PS[:, t % 2, (t // 2) * C:(t // 2 + 1) * C], gate[:, 3:4], X[:, t, :],
                                                   ALU.mult, ALU.add).then_inc(s["res"], 1)
                        for t in range(TT):
                            stats_vector(v, s, t, "res", TT + t + 1)
                        stats_done(v, s)

        def score_attention(pi):
            with Phase() as ph:
                s = ph.sem(LN + "mk_in mk qp qk_b q_hi q_lo sc e1 e2 e3 neg ex rc rg res")
                MU = ph.sb("MU", [P, 2, S], U8)
                MB = ph.sb("MB", [P, 2, S], U8)
                MF = ph.sb("MF", [P, 2, S])
                MG = ph.sb("MG", [P, 2, S])
                Q = ph.sb("Q", [P, 2, TOK])
                QH = ph.sb("QH", [P, 2, TOK], F32R)
                QL = ph.sb("QL", [P, 2, TOK], F32R)
                E = ph.sb("E", [P, TT, S])
                mx = ph.sb("mx", [P, TT])
                live = ph.sb("live", [P, TT])
                sm = ph.sb("sm", [P, 3, TT])
                with nc.Block() as block:
                    @block.sync
                    def _(sp):
                        sp.dma_start(MU[:, :, :], a["maskS"].rearrange("(q p) k -> p q k", p=P)).then_inc(s["mk_in"], 16)
                        sp.dma_start(MB[:, :, :].rearrange("p a b -> p (a b)"), a["maskB"][:, bass.ts(pi, TOK)].broadcast_to([P, TOK])).then_inc(s["mk_in"], 16)

                    @block.gpsimd
                    def _(g):
                        stats_gpsimd(g, s)

                    @block.tensor
                    def _(pe):
                        for r in range(2):
                            m = mm3(pe, PS[:, r, :], weight("qk2", 2, r), (CTH[:, :], CTL[:, :]))
                            m.then_inc(s["qp"], 1)
                        pe.wait_ge(s["q_lo"], 2)
                        for t in range(TT):
                            j = t // 2
                            mm3(pe, PS[:, 2 + t, 0:S], pair(QH, QL, slice(None), 0, slice(t * P, t * P + P)),
                                pair(QH, QL, slice(None), 1, slice(j * S, j * S + S))).then_inc(s["sc"], 1)

                    @block.scalar
                    def _(act):
                        for r in range(2):
                            act.wait_ge(s["qp"], r + 1)
                            act.activation(Q[:, r, :], PS[:, r, :], ACT.Identity, bias=const("qkb2")[:, r:r + 1]).then_inc(s["qk_b"], 1)
                            act.wait_ge(s["qk_b"], r + 1)
                            act.activation(QH[:, r, :], Q[:, r, :], ACT.Copy).then_inc(s["q_hi"], 1)
                        for t in range(TT):
                            act.wait_ge(s["neg"], t + 1)
                            act.activation(E[:, t, :], E[:, t, :], ACT.Exp, bias=mx[:, t:t + 1], accum_out=sm[:, 0, t:t + 1]).then_inc(s["ex"], 1)

                    @block.vector
                    def _(v):
                        ln_vector(v, s)
                        for r in range(2):
                            v.wait_ge(s["q_hi"], r + 1)
                            v.tensor_tensor(QL[:, r, :], Q[:, r, :], QH[:, r, :].bitcast(F32), ALU.subtract).then_inc(s["q_lo"], 1)
                        v.wait_ge(s["mk_in"], 32)
                        v.tensor_scalar(MF[:, :, :], MU[:, :, :], -1.0e38, None, ALU.mult).then_inc(s["mk"], 1)
                        v.tensor_scalar(MG[:, :, :], MB[:, :, :], -1.0e38, None, ALU.mult).then_inc(s["mk"], 1)
                        v.wait_ge(s["ln_norm"], TT)
                        v.wait_ge(s["mk"], 2)
                        for t in range(TT):
                            v.wait_ge(s["sc"], t + 1)
                            v.scalar_tensor_tensor(E[:, t, :], PS[:, 2 + t, 0:S], DC ** -0.5, HN[:, t, :], ALU.mult, ALU.mult).then_inc(s["e1"], 1)
                        for t in range(TT):
                            v.wait_ge(s["e1"], t + 1)
                            v.tensor_tensor(E[:, t, :], E[:, t, :], MF[:, t % 2, :], ALU.add).then_inc(s["e2"], 1)
                        for t in range(TT):
                            v.wait_ge(s["e2"], t + 1)
                            v.tensor_tensor(E[:, t, :], E[:, t, :], MG[:, t // 2, :], ALU.add).then_inc(s["e3"], 1)
                        for t in range(TT):
                            v.wait_ge(s["e3"], t + 1)
                            v.tensor_reduce(mx[:, t:t + 1], E[:, t, :], AX.X, ALU.max, negate=True).then_inc(s["neg"], 1)
                        v.wait_ge(s["neg"], TT)
                        v.tensor_scalar(live[:, :], mx[:, :], 1.0e37, None, ALU.is_lt).then_inc(s["rc"], 1)
                        v.wait_ge(s["ex"], TT)
                        v.wait_ge(s["rc"], 1)
                        v.tensor_tensor(sm[:, 0, :], sm[:, 0, :], live[:, :], ALU.mult).then_inc(s["rc"], 1)
                        v.wait_ge(s["rc"], 2)
                        v.reciprocal(sm[:, 1, :], sm[:, 0, :]).then_inc(s["rc"], 1)
                        v.wait_ge(s["rc"], 3)
                        v.scalar_tensor_tensor(sm[:, 2, :], sm[:, 1, :], gate[:, 4:5], live[:, :], ALU.mult, ALU.mult).then_inc(s["rg"], 1)
                        v.wait_ge(s["rg"], 1)
                        for t in range(TT):
                            v.scalar_tensor_tensor(X[:, t, :], E[:, t, :], sm[:, 2, t:t + 1], X[:, t, :], ALU.mult, ALU.add).then_inc(s["res"], 1)
                        for t in range(TT):
                            stats_vector(v, s, t, "res", t + 1)
                        stats_done(v, s)

        def router(pi):
            with Phase() as ph:
                s = ph.sem(LN + "lg smx ssub sexp ssum rank oh pw st")
                LG = ph.sb("LG", [P, TT, 8])
                RK = ph.sb("RK", [P, 3, TT, NE, NE])
                sm = ph.sb("sm", [P, 3, TT])
                HOT = ph.sb("HOT", [P, TT, 2 * NE])
                PWP = ph.sb("PWP", [P, TT, 2 * NE])
                with nc.Block() as block:
                    @block.tensor
                    def _(pe):
                        transpose_tensor(pe, HN, s["ln_norm"], s["tr_done"])
                        pe.wait_ge(s["tr_lo"], KC)
                        for t in range(TT):
                            for k in range(KC):
                                m = mm3(pe, PS[:, 2, t * 8:t * 8 + 8], pair(HH, HL, slice(None), k, slice(t * P, t * P + P)),
                                        weight("rt2", KC, k), k == 0, k == KC - 1)
                        m.then_inc(s["lg"], 1)

                    @block.scalar
                    def _(act):
                        split_scalar(act, s["tr_hi"], s["tr_done"])
                        act.wait_ge(s["ssub"], 1)
                        act.activation(LG[:, :, :], LG[:, :, :], ACT.Exp).then_inc(s["sexp"], 1)

                    @block.vector
                    def _(v):
                        ln_vector(v, s)
                        split_vector(v, s["tr_hi"], s["tr_lo"])
                        lgp = PS[:, 2, 0:32].rearrange("p (t e) -> p t e", t=TT)

                        def wide(x):
                            return x.unsqueeze(2).broadcast_to([P, TT, NE])
                        v.wait_ge(s["lg"], 1)
                        v.tensor_reduce(sm[:, 0, :], lgp, AX.X, ALU.max).then_inc(s["smx"], 1)
                        v.wait_ge(s["smx"], 1)
                        v.tensor_tensor(LG[:, :, :], lgp, wide(sm[:, 0, :]), ALU.subtract).then_inc(s["ssub"], 1)
                        v.wait_ge(s["sexp"], 1)
                        v.tensor_reduce(sm[:, 1, :], LG[:, :, :], AX.X, ALU.add).then_inc(s["ssum"], 1)
                        v.wait_ge(s["ssum"], 1)
                        v.reciprocal(sm[:, 2, :], sm[:, 1, :]).then_inc(s["ssum"], 1)
                        v.wait_ge(s["ssum"], 2)
                        v.tensor_tensor(LG[:, :, :], LG[:, :, :], wide(sm[:, 2, :]), ALU.mult).then_inc(s["ssum"], 1)
                        v.wait_ge(s["ssum"], 3)
                        rank, n = rank_vector(v, s, RK, LG[:, :, :], 0)
                        for r in range(2):
                            v.tensor_scalar(HOT[:, :, NE * r:NE * r + NE], rank, float(r), None, ALU.is_equal).then_inc(s["oh"], 1)
                            v.wait_ge(s["oh"], r + 1)
                            v.tensor_tensor(PWP[:, :, NE * r:NE * r + NE], HOT[:, :, NE * r:NE * r + NE], LG[:, :, :], ALU.mult).then_inc(s["pw"], 1)
                        v.wait_ge(s["pw"], 2)
                        v.tensor_copy(OH[:, bass.ts(pi, TT), :], HOT[:, :, :]).then_inc(s["st"], 1)
                        v.tensor_copy(PW[:, bass.ts(pi, TT), :], PWP[:, :, :]).then_inc(s["st"], 1)

        def capacity():
            NT = PAIRS * TT
            with Phase() as ph:
                s = ph.sem("cm tot run cnt kp kw kr")
                RUN = ph.sb("RUN", [P, NT + 1, 2 * NE])
                CNT = ph.sb("CNT", [P, NT, 2 * NE])
                with nc.Block() as block:
                    @block.tensor
                    def _(pe):
                        ohs = OH[:, :, :].rearrange("p t e -> p (t e)")
                        pe.matmul(PS[:, 0, 0:NT * 16], trib[:, :], ohs, start=True, stop=True).then_inc(s["cm"], 1)
                        pe.matmul(PS[:, 1, 0:NT * 16], onesb[:, :], ohs, start=True, stop=True).then_inc(s["tot"], 1)

                    @block.vector
                    def _(v):
                        within = PS[:, 0, 0:NT * 16].rearrange("p (t e) -> p t e", t=NT)
                        total = PS[:, 1, 0:NT * 16].rearrange("p (t e) -> p t e", t=NT)
                        v.memset(RUN[:, 0, :], 0.0).then_inc(s["run"], 1)
                        v.wait_ge(s["tot"], 1)
                        for t in range(NT):
                            v.wait_ge(s["run"], t + 1)
                            v.tensor_tensor(RUN[:, t + 1, :], RUN[:, t, :], total[:, t, :], ALU.add).then_inc(s["run"], 1)
                        v.wait_ge(s["run"], NT + 1)
                        v.wait_ge(s["cm"], 1)
                        v.tensor_tensor(CNT[:, :, :], within, RUN[:, 0:NT, :], ALU.add).then_inc(s["cnt"], 1)
                        v.wait_ge(s["cnt"], 1)
                        v.tensor_tensor(CNT[:, :, NE:2 * NE], CNT[:, :, NE:2 * NE],
                                        RUN[:, NT, 0:NE].unsqueeze(1).broadcast_to([P, NT, NE]), ALU.add).then_inc(s["cnt"], 1)
                        v.wait_ge(s["cnt"], 2)
                        v.tensor_scalar(CNT[:, :, :], CNT[:, :, :], float(CAP), None, ALU.is_le).then_inc(s["kp"], 1)
                        v.wait_ge(s["kp"], 1)
                        v.tensor_tensor(CNT[:, :, :], CNT[:, :, :], PW[:, :, :], ALU.mult).then_inc(s["kw"], 1)
                        v.wait_ge(s["kw"], 1)
                        v.tensor_reduce(COEF[:, :], CNT[:, :, :], AX.X, ALU.add).then_inc(s["kr"], 1)
                        v.wait_ge(s["kr"], 1)
                        v.tensor_scalar(COEF[:, :], COEF[:, :], gate[:, 5:6], None, ALU.mult).then_inc(s["kr"], 1)

        setup()
        with nc.Fori(0, PAIRS) as i:
            load_pair(i)
            graph_attention()
            small_attention(0)
            experts(0)
            latent_attention(i)
            low_rank()
            score_attention(i)
            router(i)
            store_pair(i)
        capacity()
        with nc.Fori(0, PAIRS) as i:
            load_pair(i, routed=True)
            experts(2)
            small_attention(3)
            experts(3)
            store_pair(i)
        with Phase() as ph:
            s = ph.sem("stored")
            with nc.Block() as block:
                @block.sync
                def _(sp):
                    sp.dma_start(out.rearrange("(t p) c -> p t c", p=P), XALL[:, :, :]).then_inc(s["stored"], 16)
                    sp.wait_ge(s["stored"], 16)


def _rows(w, n=P):
    w = np.asarray(w)
    return np.concatenate([w, np.zeros((n - w.shape[0],) + w.shape[1:], w.dtype)]) if w.shape[0] < n else w


def _ktiles(w):
    return np.concatenate([w[:P], w[P:]], axis=1)


def _swap8(w):
    n = w.shape[-1]
    return np.ascontiguousarray(w.reshape(w.shape[:-1] + (n // 16, 2, 8))[..., ::-1, :]).reshape(w.shape)


def _pad_cols(w, n):
    return np.concatenate([w, np.zeros(w.shape[:-1] + (n - w.shape[-1],), w.dtype)], axis=-1)


def _hidden_tiles(gate, up, down, tiles, sizes=()):
    n = tiles * P
    gate, up = _pad_cols(gate, n), _pad_cols(up, n)
    down = _rows(down, n)
    g = gate.reshape(KC, P, tiles, P).transpose(2, 1, 0, 3).reshape(tiles, P, KC * P)
    u = up.reshape(KC, P, tiles, P).transpose(2, 1, 0, 3).reshape(tiles, P, KC * P)
    sel = _selector(sizes, tiles).reshape(P, tiles, P).transpose(1, 0, 2)
    return np.ascontiguousarray(np.concatenate([g, u, down.reshape(tiles, P, C), sel], axis=2))


def _selector(sizes, tiles):
    owner = np.concatenate([np.full(n, e) for e, n in enumerate(sizes)] + [np.full(tiles * P - sum(sizes), -1)])
    sel = np.zeros((P, tiles * P), np.float32)
    for e in range(len(sizes)):
        sel[e] = owner == e
        sel[32 + e] = owner == e
    return sel


def _layout(i):
    g = {k: np.asarray(v) for k, v in i.items()}
    f = np.float32
    arrays = {}
    arrays["x"] = g["x"].reshape(B * S, C)
    ctx = g["ctx_512"]
    arrays["ctx"] = ctx.reshape(B * S, DC)
    arrays["ctxT"] = _rows(np.ascontiguousarray(ctx.reshape(B * S, DC).T))
    arrays["maskS"] = g["mask_SxS2_bk1"]
    arrays["maskB"] = g["mask_BxS2_bf0"].reshape(1, B * S)

    wq, wk = g["L0_ffn_wq"], g["L0_ffn_wk"]
    rt0 = _pad_cols(np.concatenate([g["L0_ffn_w_router"], g["L0_ffn_w_sh_eg"]], axis=1), 16)
    l1 = np.concatenate([g["L1_ffn_base_W"].T, g["L1_ffn_A"].T, g["L1_ffn_router_W"].T], axis=1)
    W = {
        "gat0": _rows(g["L0_xattn_W0"].transpose(1, 0, 2).reshape(DC, 256)),
        "gat1": _ktiles(g["L0_xattn_W1"].transpose(1, 0, 2).reshape(256, 256)),
        "qk0": _ktiles(np.concatenate([wq, _swap8(wq), wk, _swap8(wk)], axis=1)),
        "v0": _ktiles(g["L0_ffn_wv"]), "o0": _ktiles(g["L0_ffn_wo"]), "rt0": _ktiles(rt0),
        "l1f": _ktiles(l1), "l1b": _rows(g["L1_ffn_B"].T),
        "qk2": _rows(np.concatenate([_pad_cols(g["L2_xattn_Wq"].T, P), _pad_cols(g["L2_xattn_Wk"].T, P)], axis=1)),
        "rt2": _ktiles(g["L2_ffn_router_w"].T),
        "q3": _ktiles(g["L3_xattn_Wq"].T), "k3": _rows(g["L3_xattn_Wkv_expand"][:C].T),
        "v3": _rows(g["L3_xattn_Wkv_expand"][C:].T), "o3": _ktiles(g["L3_xattn_Wout"].T),
        "rt3": _ktiles(g["L3_ffn_gate_w"].T),
    }
    for name, n in WCOLS:
        assert W[name].shape == (P, n), (name, W[name].shape, n)
    arrays["wpack"] = _pad_cols(np.concatenate([W[n] for n, _ in WCOLS], axis=1), CHUNKS * CHUNK)

    def spread(v):
        return np.broadcast_to(np.asarray(v).reshape(1, -1), (P, np.asarray(v).size))

    def columns(v, n):
        return np.ascontiguousarray(v.reshape(n, P).T)

    feat, pos = np.arange(P), np.arange(S)
    inv = (1.0 / f(1000000.0) ** (np.arange(0, 16, 2, dtype=f) / f(16))).astype(f)
    ang = (pos[None, :].astype(f) * inv[feat % 8][:, None]).astype(f).astype(np.float64)
    sign = np.where(feat % 16 < 8, -1.0, 1.0)[:, None]
    inv2 = (1.0 / f(10000.0) ** (np.arange(0, DC, 2, dtype=f) / f(DC))).astype(f)
    ang2 = np.repeat((pos[:, None].astype(f) * inv2[None, :]).astype(f), 2, axis=1).astype(np.float64)
    sign2 = np.where(np.arange(DC) < DC // 2, -1.0, 1.0)[None, :]
    e0, e1 = np.meshgrid(np.arange(NE), np.arange(NE), indexing="ij")
    bq, bk = g["L0_ffn_bq"], g["L0_ffn_bk"]
    CC = {
        "ident": np.eye(P), "causal": np.where(feat[None, :] > feat[:, None], MASKED, 0.0),
        "headmask": (feat[:, None] // 16 == np.arange(8)[None, :]),
        "halfmask": (feat[:, None] // 64 == np.arange(2)[None, :]),
        "tri": feat[:, None] <= feat[None, :],
        "ropec": np.cos(ang), "ropes": np.sin(ang) * sign,
        "kvc": np.cos(ang2).reshape(2, P, DC).transpose(1, 0, 2).reshape(P, 2 * DC),
        "kvs": (np.sin(ang2) * sign2).reshape(2, P, DC).transpose(1, 0, 2).reshape(P, 2 * DC),
        "lower": spread((e1 < e0).astype(f)), "upper": spread((e1 > e0).astype(f)),
        "ln1": columns(g["L0_ffn_w_ln1"], KC), "ln2": columns(g["L0_ffn_w_ln2"], KC),
        "qkb": np.concatenate([columns(b, KC) for b in (bq, _swap8(bq), bk, _swap8(bk))], axis=1),
        "b1f": columns(g["L2_ffn_b1"], T2),
        "qkb2": _rows(np.stack([g["L2_xattn_bq"], g["L2_xattn_bk"]], axis=1)),
        "aself0": spread(g["L0_xattn_a_self0"]), "aneigh0": spread(g["L0_xattn_a_neigh0"]),
        "aself1": spread(g["L0_xattn_a_self1"]), "aneigh1": spread(g["L0_xattn_a_neigh1"]),
        "gb0": spread(g["L0_xattn_b0"]), "gb1": spread(g["L0_xattn_b1"]), "bv0": spread(g["L0_ffn_bv"]),
        "lora_b": spread(g["L1_ffn_biases"]), "b2f": spread(g["L2_ffn_b2"]), "gbias3": spread(g["L3_ffn_gate_bias"]),
        "gates": spread(np.stack([g["g_xattn"], g["g_ffn"]], axis=1)),
    }
    arrays["consts"] = np.ascontiguousarray(np.concatenate([CC[n].astype(f) for n, _ in CCOLS], axis=1))

    kcq = g["L1_xattn_w_kc_q"].transpose(0, 2, 1)
    wqr = g["L1_xattn_W_qr"]
    def two(w):
        lo = np.concatenate([w[:, P:], np.zeros((MH, 2 * P - w.shape[1], w.shape[2]), w.dtype)], axis=1)
        return np.concatenate([w[:, :P], lo], axis=2)
    wkr = g["L1_xattn_W_kr"].transpose(0, 2, 1)
    wkr = np.concatenate([wkr, np.zeros_like(wkr)], axis=1)
    wq1 = g["L1_xattn_Wq"].reshape(MH, P, C)
    wo1 = g["L1_xattn_Wo"].T.reshape(MH, P, C)
    arrays["fold"] = np.ascontiguousarray(np.concatenate([two(kcq), two(wqr), wkr, wq1, g["L1_xattn_w_kc_kv"], wo1], axis=2))

    def cat(w):
        return w.transpose(1, 0, 2).reshape(w.shape[1], -1)
    arrays["moe0"] = _hidden_tiles(
        np.concatenate([cat(g["L0_ffn_w_gate_e"]), g["L0_ffn_w_sh_gate"]], axis=1),
        np.concatenate([cat(g["L0_ffn_w_up_e"]), g["L0_ffn_w_sh_up"]], axis=1),
        np.concatenate([g["L0_ffn_w_down_e"].reshape(-1, C), g["L0_ffn_w_sh_down"]], axis=0), T0, [MOE_I] * NE + [SH_I])
    up, sg = g["L3_ffn_up_w"].transpose(0, 2, 1), g["L3_ffn_shared_gw"].T
    arrays["moe3"] = _hidden_tiles(
        np.concatenate([cat(up[:, :, :H3]), sg[:, HS3:]], axis=1),
        np.concatenate([cat(up[:, :, H3:]), sg[:, :HS3]], axis=1),
        np.concatenate([g["L3_ffn_down_w"].transpose(0, 2, 1).reshape(-1, C), g["L3_ffn_shared_dw"].T], axis=0), T3, [H3] * NE + [HS3])
    w1 = g["L2_ffn_w1"].T
    arrays["ffn2"] = np.ascontiguousarray(_hidden_tiles(w1, w1, g["L2_ffn_w2"].T, T2)[:, :, [*range(256), *range(512, 896)]])
    return {k: np.ascontiguousarray(v) for k, v in arrays.items()}


def kernel(**inputs):
    import concourse.bacc as bacc
    from concourse.bass_utils import run_bass_kernel_spmd

    nc = bacc.Bacc("TRN2", target_bir_lowering=False, num_devices=1)
    arrays = _layout(inputs)
    feeds, aps = {}, {}
    for name, array in arrays.items():
        feeds[f"in_{name}"] = array
        aps[name] = nc.dram_tensor(f"in_{name}", array.shape, mybir.dt.from_np(array.dtype), kind="ExternalInput").ap()
    out = nc.dram_tensor("out_0", (B * S, C), F32, kind="ExternalOutput").ap()
    build(nc, aps, out)
    result = run_bass_kernel_spmd(nc, [feeds], core_ids=[0])
    return result.results[0]["out_0"].reshape(B, S, C)
```
